# Optimizing a Trainium2 kernel written in Bass

```python
import numpy as np
import jax
import jax.numpy as jnp

def _softmax(x, axis=-1):
    return jax.nn.softmax(x, axis=axis)

def _gelu(x):
    return jax.nn.gelu(x, approximate=True)

def _silu(x):
    return jax.nn.silu(x)

def _sigmoid(x):
    return jax.nn.sigmoid(x)

def _layernorm(x, axis=-1, eps=1e-05):
    m = jnp.mean(x, axis=axis, keepdims=True)
    v = jnp.var(x, axis=axis, keepdims=True)
    return (x - m) / jnp.sqrt(v + eps)

def _scatter_add(tgt, idx, src, axis=0):
    return tgt.at[idx].add(src)

def _segment_sum(src, seg, n):
    return jax.ops.segment_sum(src, seg, n)
kernel_name = 'mk_xattn_ffn_d2_seqx_r4_b171fe'

def setup_inputs(seed: int=0):
    np.random.seed(seed)
    _w = jnp.asarray

    def _rec_inputs():
        import jax
        import jax.numpy as jnp
        _rk = jax.random.key(seed)
        x = 2.818e-05 + 1 * jax.random.normal(jax.random.fold_in(_rk, 1), (4, 512, 512), jnp.float32)
        _lenS = 512 - jax.random.randint(jax.random.fold_in(_rk, 7), (4,), 0, max(1, 512 // 4) + 1, jnp.int32)
        _lenS2 = 512 - jax.random.randint(jax.random.fold_in(_rk, 8), (4,), 0, max(1, 512 // 4) + 1, jnp.int32)
        _ctx_1024P = jax.random.normal(jax.random.fold_in(_rk, 11), (4, 16, 256), jnp.float32)
        _ctx_1024c = jax.random.dirichlet(jax.random.fold_in(_rk, 511), 0.3 * jnp.ones((16,), jnp.float32), (4, 512))
        _ctx_1024t = jnp.einsum('bsk,bkd->bsd', _ctx_1024c, _ctx_1024P)
        _ctx_1024t = _ctx_1024t * jax.lax.rsqrt(jnp.mean(jnp.square(_ctx_1024t)) + 1e-12) * 0.953939
        ctx_1024 = 7.22013e-05 + 1.00017 * (_ctx_1024t + 0.3 * jax.random.normal(jax.random.fold_in(_rk, 611), (4, 512, 256), jnp.float32))
        return (x, ctx_1024)
    x, ctx_1024 = _rec_inputs()

    def _L0_xattn_setup():
        import jax, jax.numpy as jnp
        import numpy as np
        B_, L_, D_MODEL = (4, 512, 256)
        D_STATE, D_CONV, EXPAND = (16, 4, 2)
        D_INNER = EXPAND * D_MODEL
        DT_RANK = (D_MODEL + 15) // 16

        def silu(x):
            return x * jax.nn.sigmoid(x)
        key = jax.random.key(seed)
        ks = jax.random.split(key, 10)
        f32 = jnp.float32
        hidden_states = jax.random.normal(ks[0], (B_, L_, D_MODEL), dtype=f32)
        z = jax.random.normal(ks[1], (B_, D_INNER, L_), dtype=f32)
        in_proj_w = jax.random.normal(ks[2], (D_INNER, D_MODEL), dtype=f32) * 0.02
        conv_w = jax.random.normal(ks[3], (D_INNER, 1, D_CONV), dtype=f32) * 0.1
        conv_b = jax.random.normal(ks[4], (D_INNER,), dtype=f32) * 0.02
        x_proj_w = jax.random.normal(ks[5], (DT_RANK + 2 * D_STATE, D_INNER), dtype=f32) * 0.02
        dt_proj_w = jax.random.uniform(ks[6], (D_INNER, DT_RANK), dtype=f32, minval=-DT_RANK ** (-0.5), maxval=DT_RANK ** (-0.5))
        dt = jnp.exp(jax.random.uniform(ks[7], (D_INNER,), dtype=f32, minval=np.log(0.001), maxval=np.log(0.1)))
        dt_proj_b = jnp.log(jnp.expm1(dt))
        A_log = jnp.log(jnp.broadcast_to(jnp.arange(1, D_STATE + 1, dtype=f32), (D_INNER, D_STATE)))
        D = jnp.ones((D_INNER,), f32)
        return {'hidden_states': hidden_states, 'z': z, 'in_proj_w': in_proj_w, 'conv_w': conv_w, 'conv_b': conv_b, 'x_proj_w': x_proj_w, 'dt_proj_w': dt_proj_w, 'dt_proj_b': dt_proj_b, 'A_log': A_log, 'D': D}
    _L0_xattn_all = _L0_xattn_setup()
    _L0_xattn_in = {k: v for k, v in _L0_xattn_all.items() if k in ('in_proj_w', 'conv_w', 'conv_b', 'x_proj_w', 'dt_proj_w', 'dt_proj_b', 'A_log', 'D')}
    del _L0_xattn_all

    def _L0_ffn_setup():
        import jax, jax.numpy as jnp
        import numpy as np
        TOP_K = 4

        def _silu_and_mul(gu):
            g, u = jnp.split(gu, 2, axis=-1)
            return jax.nn.silu(g) * u
        key = jax.random.key(seed)
        ks = jax.random.split(key, 7)
        H, E, I, Is = (512, 16, 352, 1408)
        s = 0.02
        return {'hidden_states': jax.random.normal(ks[0], (4, 256, H), dtype=jnp.float32), 'gate_w': jax.random.normal(ks[1], (E, H), dtype=jnp.float32) * s, 'sgate_w': jax.random.normal(ks[2], (1, H), dtype=jnp.float32) * s, 'w13': jax.random.normal(ks[3], (E, 2 * I, H), dtype=jnp.float32) * s, 'w2': jax.random.normal(ks[4], (E, H, I), dtype=jnp.float32) * s, 'shared_gate_up_w': jax.random.normal(ks[5], (2 * Is, H), dtype=jnp.float32) * s, 'shared_down_w': jax.random.normal(ks[6], (H, Is), dtype=jnp.float32) * s}
    _L0_ffn_all = _L0_ffn_setup()
    _L0_ffn_in = {k: v for k, v in _L0_ffn_all.items() if k in ('gate_w', 'sgate_w', 'w13', 'w2', 'shared_gate_up_w', 'shared_down_w')}
    del _L0_ffn_all

    def _L1_xattn_setup():
        import jax, jax.numpy as jnp
        import numpy as np
        import math
        B, L, DM = (2, 512, 256)
        DS, DC, EXP = (16, 4, 2)
        DI = EXP * DM
        DR = math.ceil(DM / 16)
        DT_MIN, DT_MAX, DT_FLOOR = (0.001, 0.1, 0.0001)

        def _ssm_forward(hidden_states, z, in_proj_w, conv_w, conv_b, x_proj_w, dt_proj_w, dt_proj_b, A_log, D):
            b = hidden_states.shape[0]
            x = jnp.einsum('ed,bld->bel', in_proj_w, hidden_states)
            xp = jnp.pad(x, ((0, 0), (0, 0), (DC - 1, 0)))
            xc = jax.lax.conv_general_dilated(xp, conv_w[:, None, :], window_strides=(1,), padding='VALID', dimension_numbers=('NCH', 'OIH', 'NCH'), feature_group_count=DI)
            u = jax.nn.silu(xc + conv_b[None, :, None])
            x_dbl = jnp.einsum('ke,bel->bkl', x_proj_w, u)
            dt_lo = x_dbl[:, :DR]
            Bm = x_dbl[:, DR:DR + DS]
            Cm = x_dbl[:, DR + DS:]
            delta = jax.nn.softplus(jnp.einsum('er,brl->bel', dt_proj_w, dt_lo) + dt_proj_b[None, :, None])
            A = -jnp.exp(A_log)

            def step(state, xs):
                d_t, B_t, C_t, u_t = xs
                dA = jnp.exp(d_t[..., None] * A)
                state = state * dA + (d_t * u_t)[..., None] * B_t[:, None, :]
                y_t = jnp.einsum('ben,bn->be', state, C_t)
                return (state, y_t)
            xs = (jnp.moveaxis(delta, -1, 0), jnp.moveaxis(Bm, -1, 0), jnp.moveaxis(Cm, -1, 0), jnp.moveaxis(u, -1, 0))
            state0 = jnp.zeros((b, DI, DS), delta.dtype)
            _, ys = jax.lax.scan(step, state0, xs)
            y = jnp.moveaxis(ys, 0, -1)
            y = y + D[None, :, None] * u
            y = y * jax.nn.silu(z)
            return jnp.swapaxes(y, 1, 2)
        key = jax.random.key(seed)
        ks = jax.random.split(key, 8)
        hidden_states = jax.random.normal(ks[0], (B, L, DM), jnp.float32)
        z = jax.random.normal(ks[1], (B, DI, L), jnp.float32)
        in_proj_w = jax.random.normal(ks[2], (DI, DM), jnp.float32) * DM ** (-0.5)
        conv_w = jax.random.normal(ks[3], (DI, DC), jnp.float32) * DC ** (-0.5)
        conv_b = jnp.zeros((DI,), jnp.float32)
        x_proj_w = jax.random.normal(ks[4], (DR + 2 * DS, DI), jnp.float32) * DI ** (-0.5)
        dt_std = DR ** (-0.5)
        dt_proj_w = jax.random.uniform(ks[5], (DI, DR), jnp.float32, -dt_std, dt_std)
        dt = jnp.exp(jax.random.uniform(ks[6], (DI,), jnp.float32) * (math.log(DT_MAX) - math.log(DT_MIN)) + math.log(DT_MIN))
        dt = jnp.clip(dt, DT_FLOOR)
        dt_proj_b = dt + jnp.log(-jnp.expm1(-dt))
        A_log = jnp.log(jnp.broadcast_to(jnp.arange(1, DS + 1, dtype=jnp.float32), (DI, DS)))
        D = jnp.ones((DI,), jnp.float32)
        return dict(hidden_states=hidden_states, z=z, in_proj_w=in_proj_w, conv_w=conv_w, conv_b=conv_b, x_proj_w=x_proj_w, dt_proj_w=dt_proj_w, dt_proj_b=dt_proj_b, A_log=A_log, D=D)
    _L1_xattn_all = _L1_xattn_setup()
    _L1_xattn_in = {k: v for k, v in _L1_xattn_all.items() if k in ('in_proj_w', 'conv_w', 'conv_b', 'x_proj_w', 'dt_proj_w', 'dt_proj_b', 'A_log', 'D')}
    del _L1_xattn_all

    def _L1_ffn_setup():
        import jax, jax.numpy as jnp
        import numpy as np
        EPS = 1e-05

        def _quant_weight(w):
            scale = jnp.mean(jnp.abs(w)) + EPS
            wq = jnp.clip(jnp.round(w / scale), -1.0, 1.0)
            return (wq, scale)

        def _quant_act(x):
            s = jnp.max(jnp.abs(x), axis=-1, keepdims=True) / 127.0 + EPS
            xq = jnp.clip(jnp.round(x / s), -128.0, 127.0)
            return (xq, s)

        def _qlinear(x, w):
            wq, ws = _quant_weight(w)
            xq, xs = _quant_act(x)
            y = jnp.einsum('bsi,oi->bso', xq, wq)
            return y * xs * ws
        key = jax.random.key(seed)
        k1, k2, k3, k4 = jax.random.split(key, 4)
        H, I = (512, 2048)
        x = jax.random.normal(k1, (4, 1024, H), dtype=jnp.float32)
        w_gate = jax.random.normal(k2, (I, H), dtype=jnp.float32) * (1.0 / np.sqrt(H))
        w_up = jax.random.normal(k3, (I, H), dtype=jnp.float32) * (1.0 / np.sqrt(H))
        w_down = jax.random.normal(k4, (H, I), dtype=jnp.float32) * (1.0 / np.sqrt(I))
        return {'x': x, 'w_gate': w_gate, 'w_up': w_up, 'w_down': w_down}
    _L1_ffn_all = _L1_ffn_setup()
    _L1_ffn_in = {k: v for k, v in _L1_ffn_all.items() if k in ('w_gate', 'w_up', 'w_down')}
    del _L1_ffn_all
    return {'x': x, 'ctx_1024': ctx_1024, 'L0_xattn_in_proj_w': _L0_xattn_in['in_proj_w'], 'L0_xattn_conv_w': _L0_xattn_in['conv_w'], 'L0_xattn_conv_b': _L0_xattn_in['conv_b'], 'L0_xattn_x_proj_w': _L0_xattn_in['x_proj_w'], 'L0_xattn_dt_proj_w': _L0_xattn_in['dt_proj_w'], 'L0_xattn_dt_proj_b': _L0_xattn_in['dt_proj_b'], 'L0_xattn_A_log': _L0_xattn_in['A_log'], 'L0_xattn_D': _L0_xattn_in['D'], 'L0_ffn_gate_w': _L0_ffn_in['gate_w'], 'L0_ffn_sgate_w': _L0_ffn_in['sgate_w'], 'L0_ffn_w13': _L0_ffn_in['w13'], 'L0_ffn_w2': _L0_ffn_in['w2'], 'L0_ffn_shared_gate_up_w': _L0_ffn_in['shared_gate_up_w'], 'L0_ffn_shared_down_w': _L0_ffn_in['shared_down_w'], 'L1_xattn_in_proj_w': _L1_xattn_in['in_proj_w'], 'L1_xattn_conv_w': _L1_xattn_in['conv_w'], 'L1_xattn_conv_b': _L1_xattn_in['conv_b'], 'L1_xattn_x_proj_w': _L1_xattn_in['x_proj_w'], 'L1_xattn_dt_proj_w': _L1_xattn_in['dt_proj_w'], 'L1_xattn_dt_proj_b': _L1_xattn_in['dt_proj_b'], 'L1_xattn_A_log': _L1_xattn_in['A_log'], 'L1_xattn_D': _L1_xattn_in['D'], 'L1_ffn_w_gate': _L1_ffn_in['w_gate'], 'L1_ffn_w_up': _L1_ffn_in['w_up'], 'L1_ffn_w_down': _L1_ffn_in['w_down']}

def reference(x, ctx_1024, L0_xattn_in_proj_w, L0_xattn_conv_w, L0_xattn_conv_b, L0_xattn_x_proj_w, L0_xattn_dt_proj_w, L0_xattn_dt_proj_b, L0_xattn_A_log, L0_xattn_D, L0_ffn_gate_w, L0_ffn_sgate_w, L0_ffn_w13, L0_ffn_w2, L0_ffn_shared_gate_up_w, L0_ffn_shared_down_w, L1_xattn_in_proj_w, L1_xattn_conv_w, L1_xattn_conv_b, L1_xattn_x_proj_w, L1_xattn_dt_proj_w, L1_xattn_dt_proj_b, L1_xattn_A_log, L1_xattn_D, L1_ffn_w_gate, L1_ffn_w_up, L1_ffn_w_down):
    import jax
    import jax.numpy as jnp

    def _L0_xattn_ref(hidden_states, z, in_proj_w, conv_w, conv_b, x_proj_w, dt_proj_w, dt_proj_b, A_log, D):
        import jax, jax.numpy as jnp
        import numpy as np
        B_, L_, D_MODEL = (4, 512, 256)
        D_STATE, D_CONV, EXPAND = (16, 4, 2)
        D_INNER = EXPAND * D_MODEL
        DT_RANK = (D_MODEL + 15) // 16

        def silu(x):
            return x * jax.nn.sigmoid(x)
        Bsz, L, _ = hidden_states.shape
        d_inner, _, d_conv = conv_w.shape
        dt_rank = dt_proj_w.shape[1]
        d_state = A_log.shape[1]
        x = jnp.einsum('bld,ed->bel', hidden_states, in_proj_w)
        xc = jax.lax.conv_general_dilated(x, conv_w, window_strides=(1,), padding=[(d_conv - 1, 0)], feature_group_count=d_inner, dimension_numbers=('NCH', 'OIH', 'NCH'))
        x = silu(xc + conv_b[None, :, None])
        x_dbl = jnp.einsum('bdl,ed->bel', x, x_proj_w)
        dt_low, Bm, Cm = jnp.split(x_dbl, [dt_rank, dt_rank + d_state], axis=1)
        dt = jnp.einsum('brl,dr->bdl', dt_low, dt_proj_w)
        dt = jax.nn.softplus(dt + dt_proj_b[None, :, None])
        A = -jnp.exp(A_log)
        dt_t = jnp.moveaxis(dt, -1, 0)
        B_t = jnp.moveaxis(Bm, -1, 0)
        C_t = jnp.moveaxis(Cm, -1, 0)
        u_t = jnp.moveaxis(x, -1, 0)

        def step(state, inp):
            d, b, c, u = inp
            dA = jnp.exp(d[..., None] * A)
            state = state * dA + (d * u)[..., None] * b[:, None, :]
            y = jnp.einsum('bdn,bn->bd', state, c)
            return (state, y)
        state0 = jnp.zeros((Bsz, d_inner, d_state), x.dtype)
        _, ys = jax.lax.scan(step, state0, (dt_t, B_t, C_t, u_t))
        y = jnp.moveaxis(ys, 0, 2)
        y = y + D[None, :, None] * x
        y = y * silu(z)
        return jnp.swapaxes(y, 1, 2)

    def _L0_ffn_ref(hidden_states, gate_w, sgate_w, w13, w2, shared_gate_up_w, shared_down_w):
        import jax, jax.numpy as jnp
        import numpy as np
        TOP_K = 4

        def _silu_and_mul(gu):
            g, u = jnp.split(gu, 2, axis=-1)
            return jax.nn.silu(g) * u
        B, S, H = hidden_states.shape
        x = hidden_states.reshape(-1, H)
        E = gate_w.shape[0]
        shared = _silu_and_mul(x @ shared_gate_up_w.T) @ shared_down_w.T
        shared = shared * jax.nn.sigmoid(x @ sgate_w.T)
        router_logits = x @ gate_w.T
        routing_weights = jax.nn.softmax(router_logits.astype(jnp.float32), axis=-1)
        topk_w, topk_ids = jax.lax.top_k(routing_weights, TOP_K)

        def body(acc, ew):
            w13_e, w2_e, e = ew
            coef = jnp.sum(jnp.where(topk_ids == e, topk_w, 0.0), axis=-1)
            h = _silu_and_mul(x @ w13_e.T)
            acc = acc + (h @ w2_e.T).astype(jnp.float32) * coef[:, None]
            return (acc, None)
        init = jnp.zeros((x.shape[0], H), dtype=jnp.float32)
        sparse_out, _ = jax.lax.scan(body, init, (w13, w2, jnp.arange(E)))
        out = shared + sparse_out.astype(x.dtype)
        return out.reshape(B, S, H)

    def _L1_xattn_ref(hidden_states, z, in_proj_w, conv_w, conv_b, x_proj_w, dt_proj_w, dt_proj_b, A_log, D):
        import jax, jax.numpy as jnp
        import numpy as np
        import math
        B, L, DM = (2, 512, 256)
        DS, DC, EXP = (16, 4, 2)
        DI = EXP * DM
        DR = math.ceil(DM / 16)
        DT_MIN, DT_MAX, DT_FLOOR = (0.001, 0.1, 0.0001)

        def _ssm_forward(hidden_states, z, in_proj_w, conv_w, conv_b, x_proj_w, dt_proj_w, dt_proj_b, A_log, D):
            b = hidden_states.shape[0]
            x = jnp.einsum('ed,bld->bel', in_proj_w, hidden_states)
            xp = jnp.pad(x, ((0, 0), (0, 0), (DC - 1, 0)))
            xc = jax.lax.conv_general_dilated(xp, conv_w[:, None, :], window_strides=(1,), padding='VALID', dimension_numbers=('NCH', 'OIH', 'NCH'), feature_group_count=DI)
            u = jax.nn.silu(xc + conv_b[None, :, None])
            x_dbl = jnp.einsum('ke,bel->bkl', x_proj_w, u)
            dt_lo = x_dbl[:, :DR]
            Bm = x_dbl[:, DR:DR + DS]
            Cm = x_dbl[:, DR + DS:]
            delta = jax.nn.softplus(jnp.einsum('er,brl->bel', dt_proj_w, dt_lo) + dt_proj_b[None, :, None])
            A = -jnp.exp(A_log)

            def step(state, xs):
                d_t, B_t, C_t, u_t = xs
                dA = jnp.exp(d_t[..., None] * A)
                state = state * dA + (d_t * u_t)[..., None] * B_t[:, None, :]
                y_t = jnp.einsum('ben,bn->be', state, C_t)
                return (state, y_t)
            xs = (jnp.moveaxis(delta, -1, 0), jnp.moveaxis(Bm, -1, 0), jnp.moveaxis(Cm, -1, 0), jnp.moveaxis(u, -1, 0))
            state0 = jnp.zeros((b, DI, DS), delta.dtype)
            _, ys = jax.lax.scan(step, state0, xs)
            y = jnp.moveaxis(ys, 0, -1)
            y = y + D[None, :, None] * u
            y = y * jax.nn.silu(z)
            return jnp.swapaxes(y, 1, 2)
        return _ssm_forward(hidden_states, z, in_proj_w, conv_w, conv_b, x_proj_w, dt_proj_w, dt_proj_b, A_log, D)

    def _L1_ffn_ref(x, w_gate, w_up, w_down):
        import jax, jax.numpy as jnp
        import numpy as np
        EPS = 1e-05

        def _quant_weight(w):
            scale = jnp.mean(jnp.abs(w)) + EPS
            wq = jnp.clip(jnp.round(w / scale), -1.0, 1.0)
            return (wq, scale)

        def _quant_act(x):
            s = jnp.max(jnp.abs(x), axis=-1, keepdims=True) / 127.0 + EPS
            xq = jnp.clip(jnp.round(x / s), -128.0, 127.0)
            return (xq, s)

        def _qlinear(x, w):
            wq, ws = _quant_weight(w)
            xq, xs = _quant_act(x)
            y = jnp.einsum('bsi,oi->bso', xq, wq)
            return y * xs * ws
        gate = jax.nn.silu(_qlinear(x, w_gate))
        up = _qlinear(x, w_up)
        return _qlinear(gate * up, w_down)
    x = x + _L0_xattn_ref(ctx_1024, _layernorm(x, axis=-1), L0_xattn_in_proj_w, L0_xattn_conv_w, L0_xattn_conv_b, L0_xattn_x_proj_w, L0_xattn_dt_proj_w, L0_xattn_dt_proj_b, L0_xattn_A_log, L0_xattn_D)
    x = x + _L0_ffn_ref(_layernorm(x, axis=-1), L0_ffn_gate_w, L0_ffn_sgate_w, L0_ffn_w13, L0_ffn_w2, L0_ffn_shared_gate_up_w, L0_ffn_shared_down_w)
    x = x + _L1_xattn_ref(ctx_1024, _layernorm(x, axis=-1), L1_xattn_in_proj_w, L1_xattn_conv_w, L1_xattn_conv_b, L1_xattn_x_proj_w, L1_xattn_dt_proj_w, L1_xattn_dt_proj_b, L1_xattn_A_log, L1_xattn_D)
    x = x + _L1_ffn_ref(_layernorm(x, axis=-1), L1_ffn_w_gate, L1_ffn_w_up, L1_ffn_w_down)
    return x

_drawn_inputs = setup_inputs


def setup_inputs(seed=0):
    import zlib

    import numpy as np

    out = dict(_drawn_inputs(seed))
    spreads = {'L0_xattn_D': (1.0, 0.6), 'L1_xattn_conv_b': (0.0, 0.1), 'L1_xattn_D': (1.0, 0.2)}
    factors = {'L0_xattn_in_proj_w': 2.668,
     'L0_xattn_conv_w': 2.726,
     'L0_xattn_conv_b': 6.722,
     'L0_xattn_x_proj_w': 8.0,
     'L0_xattn_dt_proj_w': 8.0,
     'L0_xattn_dt_proj_b': 8.0,
     'L0_xattn_A_log': 8.0,
     'L0_ffn_gate_w': 5.606,
     'L0_ffn_sgate_w': 5.22,
     'L0_ffn_w13': 5.008,
     'L0_ffn_w2': 4.986,
     'L1_xattn_dt_proj_w': 4.438}
    for name, (base, spread) in spreads.items():
        noise = np.random.default_rng([zlib.crc32(name.encode()), seed]).standard_normal(out[name].shape)
        drawn = base * np.exp(spread * noise) if base else spread * noise
        out[name] = jnp.asarray(drawn.astype(out[name].dtype))
    for name, factor in factors.items():
        out[name] = (out[name] * factor).astype(out[name].dtype)
    return out
```

```python
import concourse.bass as bass
from concourse import mybir
from contextlib import ExitStack

F32 = mybir.dt.float32
BF16 = mybir.dt.bfloat16
I32 = mybir.dt.int32
U32 = mybir.dt.uint32
ALU = mybir.AluOpType
ACT = mybir.ActivationFunctionType
AX = mybir.AxisListType
ds = bass.ds

P = 128
B, L, H = 4, 512, 512
T = B * L
TT = T // P
DM = 256
DI, NS, DC, DR = 512, 16, 4, 16
KC = DI // P
HC = KC // 2
HK = H // P
E, TOPK, IE = 16, 4, 352
ISH = 1408
NSH = ISH // IE
NSTEP = T * TOPK // P + E
NSLOT = NSTEP * P
R = 4
SKEW = 3
WR = 4
IF = 2048
FC = IF // 512
FK = IF // P
EPS = 1e-5
ROUND = 12582912.0
ICH = [(0, 128), (128, 128), (256, 96)]


class Mem:

    def __init__(self, nc, ctx, tag):
        self.nc, self.ctx, self.tag, self.sems = nc, ctx, tag, []

    def sb(self, name, shape, dt=F32):
        return self.ctx.enter_context(self.nc.sbuf_tensor(f"{self.tag}_{name}", shape, dt))

    def ps(self, name, shape, dt=F32):
        return self.ctx.enter_context(self.nc.psum_tensor(f"{self.tag}_{name}", shape, dt))

    def sem(self, name):
        self.sems.append(self.ctx.enter_context(self.nc.semaphore(f"{self.tag}_{name}")))
        return self.sems[-1]

    def clear(self):
        with self.nc.Block() as block:
            @block.sync
            def _(sp):
                for s in self.sems:
                    sp.sem_clear(s)


def ssm_layer(nc, l, d, X, Y):
    with ExitStack() as ctx:
        m = Mem(nc, ctx, f"ssm{l}")
        ident = m.sb("ident", [P, P])
        sel = m.sb("sel", [96, 2 * NS, P], BF16)
        ctxT = m.sb("ctxT", [P, 2, T])
        w_in = m.sb("w_in", [P, 2, DI])
        w_dt = m.sb("w_dt", [P, KC, DR])
        w_bc = m.sb("w_bc", [P, KC, 96])
        w_up = m.sb("w_up", [DR, DI])
        cw = m.sb("cw", [P, KC, DC])
        cb = m.sb("cb", [P, KC])
        db = m.sb("db", [P, KC])
        alog = m.sb("alog", [P, KC, NS])
        A = m.sb("A", [P, KC, NS])
        Dv = m.sb("Dv", [P, KC])
        diagD = m.sb("diagD", [P, KC, P])
        acc = m.sb("acc", [P, KC, L])
        tmp = m.sb("tmp", [P, KC, L])
        dlt = m.sb("dlt", [P, 2, KC, L])
        du = m.sb("du", [P, 2, KC, L])
        dts = m.sb("dts", [DR, L])
        bc3 = m.sb("bc3", [96, 2, L], BF16)
        bres = m.sb("bres", [96, L])
        Bs = m.sb("Bs", [P, R, L])
        Cs = m.sb("Cs", [P, R, L])
        dA = m.sb("dA", [P, R, HC, L])
        hs = m.sb("hs", [P, R, HC, L])

        pB = m.ps("pB", [P, L])
        pC = m.ps("pC", [P, L])
        pY = [[m.ps(f"pY{i}{k}", [P, L]) for k in range(HC)] for i in range(2)]
        pw = [m.ps(f"pw{i}", [P, L]) for i in range(2)]

        loaded = m.sem("loaded")
        x_in = m.sem("x_in")
        a_exp = m.sem("a_exp")
        a_neg = m.sem("a_neg")
        diag_rdy = m.sem("diag_rdy")
        in_rdy = m.sem("in_rdy")
        conv_a = m.sem("conv_a")
        conv_v = m.sem("conv_v")
        u_rdy = m.sem("u_rdy")
        xp_rdy = m.sem("xp_rdy")
        dts_rdy = m.sem("dts_rdy")
        bc_split = m.sem("bc_split")
        dtz_rdy = m.sem("dtz_rdy")
        ar_rdy = m.sem("ar_rdy")
        e_rdy = m.sem("e_rdy")
        t_rdy = m.sem("t_rdy")
        q_rdy = m.sem("q_rdy")
        ln_rdy = m.sem("ln_rdy")
        d_step = m.sem("d_step")
        bc_rdy = m.sem("bc_rdy")
        bc_evac = m.sem("bc_evac")
        exp_rdy = m.sem("exp_rdy")
        bu_done = m.sem("bu_done")
        scan_done = m.sem("scan_done")
        prod_done = m.sem("prod_done")
        sum_done = m.sem("sum_done")
        y_init = m.sem("y_init")
        y_out = m.sem("y_out")

        STEPS = 2 * NS

        with nc.Block() as block:

            @block.sync
            def _(sp):
                n = 0
                for dst, src in [(ident[:], d["ident"]), (sel[:], d["sel"]),
                                 (w_in[:], d[f"w_in{l}"].rearrange("(k p) n -> p k n", p=P)),
                                 (w_dt[:], d[f"w_dt{l}"].rearrange("(k p) n -> p k n", p=P)),
                                 (w_bc[:], d[f"w_bc{l}"].rearrange("(k p) n -> p k n", p=P)),
                                 (w_up[:], d[f"w_up{l}"]),
                                 (cw[:], d[f"cw{l}"].rearrange("(k p) n -> p k n", p=P)),
                                 (cb[:], d[f"cb{l}"]), (db[:], d[f"db{l}"]), (Dv[:], d[f"D{l}"]),
                                 (alog[:], d[f"alog{l}"].rearrange("(k p) n -> p k n", p=P)),
                                 (ctxT[:], d["ctxT"].rearrange("(k p) n -> p k n", p=P))]:
                    sp.dma_start(dst, src).then_inc(loaded, 16)
                    n += 16
                if l == 0:
                    sp.dma_start(X[:], d["x"].rearrange("(i p) n -> p i n", p=P)).then_inc(x_in, 16)
                    sp.wait_ge(x_in, 16)
                sp.wait_ge(loaded, n)

            NLOAD = 12 * 16

            @block.tensor
            def _(pe):
                pe.sem_inc(sum_done, R)
                pe.wait_ge(loaded, NLOAD)

                def prologue(b):
                    for c in range(KC):
                        g = b * KC + c
                        if c >= 2:
                            pe.wait_ge(conv_v, 3 * (g - 1))
                        elif b:
                            pe.wait_ge(ar_rdy, (b - 1) * KC + c + 3)
                        for k in range(2):
                            mm = nc.tensor.matmul(pw[c % 2][:], w_in[:, k, c * P:(c + 1) * P],
                                                  ctxT[:, k, b * L:(b + 1) * L], start=(k == 0), stop=(k == 1))
                        mm.then_inc(in_rdy, 1)
                    pe.wait_ge(u_rdy, b + 1)
                    for c in range(KC):
                        mm = nc.tensor.matmul(pw[0][0:DR, :], w_dt[:, c, :], Y[:, b * KC + c, :],
                                              start=(c == 0), stop=(c == KC - 1))
                    mm.then_inc(xp_rdy, 1)
                    for c in range(KC):
                        mm = nc.tensor.matmul(pw[1][0:96, :], w_bc[:, c, :], Y[:, b * KC + c, :],
                                              start=(c == 0), stop=(c == KC - 1))
                    mm.then_inc(xp_rdy, 1)
                    pe.wait_ge(dts_rdy, b + 1)
                    for c in range(KC):
                        if c == 1:
                            pe.wait_ge(bc_split, 5 * (b + 1))
                        if c >= 2:
                            pe.wait_ge(ar_rdy, b * KC + c - 1)
                        nc.tensor.matmul(pw[c % 2][:], w_up[:, c * P:(c + 1) * P], dts[:],
                                         start=True, stop=True).then_inc(dtz_rdy, 1)

                def spread(b, s, n):
                    pe.wait_ge(bc_evac, s + 1)
                    nc.tensor.matmul(pB[:], sel[:, ds(n, 1), :], bc3[:, b % 2, :], start=True, stop=True)
                    nc.tensor.matmul(pC[:], sel[:, ds(n + NS, 1), :], bc3[:, b % 2, :],
                                     start=True, stop=True).then_inc(bc_rdy, 1)

                def add(half, s, j, last=False):
                    pe.wait_ge(prod_done, s + 1 + R)
                    for k in range(HC):
                        mm = nc.tensor.matmul(pY[half][k][:], ident[:], hs[:, j, k, :],
                                              start=False, stop=last, skip_group_check=True)
                    mm.then_inc(sum_done, 1)

                def scan(b, half):
                    s0 = b * STEPS + half * NS
                    pe.wait_ge(d_step, 3 * (b + 1))
                    pe.wait_ge(bc_split, 5 * (b + 1))
                    if b:
                        pe.wait_ge(y_out, (2 * b + half) - 1)
                    for k in range(HC):
                        c = half * HC + k
                        mm = nc.tensor.matmul(pY[half][k][:], diagD[:, c, :], Y[:, b * KC + c, :],
                                              start=True, stop=False, skip_group_check=True)
                    mm.then_inc(y_init, 1)
                    for n in range(R):
                        spread(b, s0 + n, n)
                        if n >= SKEW:
                            add(half, s0 + n - SKEW, n - SKEW)
                    with pe.Fori(1, NS // R) as i:
                        for j in range(R):
                            spread(b, s0 + R * i + j, R * i + j)
                            add(half, s0 + R * i + j - SKEW, (j - SKEW) % R)
                    for n in range(NS - SKEW, NS):
                        add(half, s0 + n, n % R, last=(n == NS - 1))

                prologue(0)
                pe.wait_ge(diag_rdy, KC + 1)
                for b in range(B):
                    scan(b, 0)
                    if b + 1 < B:
                        prologue(b + 1)
                    scan(b, 1)

            @block.scalar
            def _(act):
                act.wait_ge(loaded, NLOAD)
                nc.scalar.activation(alog[:], alog[:], ACT.Exp).then_inc(a_exp, 1)
                act.wait_ge(a_exp, 1)
                nc.scalar.activation(A[:], alog[:], ACT.Copy, scale=-1.0).then_inc(a_neg, 1)
                act.sem_inc(bc_evac, 1)

                def prologue(b):
                    for c in range(KC):
                        g = b * KC + c
                        act.wait_ge(in_rdy, g + 1)
                        if b:
                            act.wait_ge(d_step, 3 * b)
                        nc.scalar.activation(acc[:, c, :], pw[c % 2][:], ACT.Identity,
                                             bias=cb[:, c:c + 1], scale=cw[:, c, DC - 1:DC]).then_inc(conv_a, 1)
                    act.wait_ge(conv_v, 3 * KC * (b + 1))
                    nc.scalar.activation(Y[:, b * KC:(b + 1) * KC, :], acc[:], ACT.Silu).then_inc(u_rdy, 1)
                    act.wait_ge(xp_rdy, 2 * b + 1)
                    nc.scalar.copy(dts[:], pw[0][0:DR, :]).then_inc(dts_rdy, 1)
                    act.wait_ge(u_rdy, b + 1)
                    for c in range(KC):
                        act.wait_ge(dtz_rdy, b * KC + c + 1)
                        nc.scalar.activation(acc[:, c, :], pw[c % 2][:], ACT.Abs, bias=db[:, c:c + 1])
                        nc.scalar.activation(dlt[:, b % 2, c, :], pw[c % 2][:], ACT.Relu,
                                             bias=db[:, c:c + 1]).then_inc(ar_rdy, 1)
                    act.wait_ge(ar_rdy, (b + 1) * KC)
                    nc.scalar.activation(acc[:], acc[:], ACT.Exp, scale=-1.0).then_inc(e_rdy, 1)
                    act.wait_ge(q_rdy, b + 1)
                    nc.scalar.activation(tmp[:], tmp[:], ACT.Ln, bias=1.0).then_inc(ln_rdy, 1)

                def step(b, half, s, n, j):
                    act.wait_ge(bc_rdy, s + 1)
                    act.wait_ge(bu_done, s + 1)
                    nc.scalar.copy(Bs[:, j, :], pB[:])
                    act.wait_ge(prod_done, s + 1)
                    nc.scalar.copy(Cs[:, j, :], pC[:]).then_inc(bc_evac, 1)
                    act.wait_ge(scan_done, s + 1)
                    for k in range(HC):
                        c = half * HC + k
                        ex = nc.scalar.activation(dA[:, j, k, 1:L], dlt[:, b % 2, c, 1:L], ACT.Exp,
                                                  scale=A[:, c, ds(n, 1)])
                    ex.then_inc(exp_rdy, 1)

                def y_to_sbuf(q):
                    b, half = q // 2, q % 2
                    act.wait_ge(sum_done, (q + 1) * NS + R)
                    for k in range(HC):
                        cp = nc.scalar.copy(Y[:, b * KC + half * HC + k, :], pY[half][k][:])
                    cp.then_inc(y_out, 1)

                def scan(b, half):
                    s0 = b * STEPS + half * NS
                    act.wait_ge(d_step, 3 * (b + 1))
                    for n in range(R):
                        step(b, half, s0 + n, n, n)
                    if b or half:
                        y_to_sbuf(2 * b + half - 1)
                    with act.Fori(1, NS // R) as i:
                        for j in range(R):
                            step(b, half, s0 + R * i + j, R * i + j, j)

                prologue(0)
                act.wait_ge(a_neg, 1)
                act.wait_ge(diag_rdy, KC + 1)
                for b in range(B):
                    scan(b, 0)
                    if b + 1 < B:
                        prologue(b + 1)
                    scan(b, 1)
                y_to_sbuf(2 * B - 1)

            @block.vector
            def _(dve):
                dve.wait_ge(loaded, NLOAD)
                for c in range(KC):
                    nc.vector.tensor_scalar(diagD[:, c, :], ident[:], Dv[:, c:c + 1], None,
                                            ALU.mult).then_inc(diag_rdy, 1)
                nc.vector.memset(dA[:, :, :, 0:1], 0.0).then_inc(diag_rdy, 1)
                dve.sem_inc(bu_done, R)
                dve.sem_inc(scan_done, R)

                def prologue(b):
                    for c in range(KC):
                        g = b * KC + c
                        dve.wait_ge(conv_a, g + 1)
                        for t in range(1, DC):
                            if t > 1:
                                dve.wait_ge(conv_v, 3 * g + t - 1)
                            nc.vector.scalar_tensor_tensor(
                                out=acc[:, c, t:L], in0=pw[c % 2][:, 0:L - t], scalar=cw[:, c, DC - 1 - t:DC - t],
                                in1=acc[:, c, t:L], op0=ALU.mult, op1=ALU.add).then_inc(conv_v, 1)
                    dve.wait_ge(xp_rdy, 2 * b + 2)
                    q = 5 * b
                    part = bc3[:, b % 2, :]
                    nc.vector.tensor_copy(part, pw[1][0:96, :]).then_inc(bc_split, 1)
                    dve.wait_ge(bc_split, q + 1)
                    nc.vector.tensor_tensor(bres[64:96, :], pw[1][64:96, :], part[64:96, :],
                                            ALU.subtract).then_inc(bc_split, 1)
                    nc.vector.tensor_tensor(part[32:64, :], pw[1][32:64, :], part[32:64, :],
                                            ALU.subtract).then_inc(bc_split, 1)
                    dve.wait_ge(bc_split, q + 3)
                    nc.vector.tensor_copy(part[64:96, :], bres[64:96, :]).then_inc(bc_split, 1)
                    dve.wait_ge(bc_split, q + 4)
                    nc.vector.tensor_tensor(part[64:96, :], bres[64:96, :], part[64:96, :],
                                            ALU.subtract).then_inc(bc_split, 1)
                    dve.wait_ge(e_rdy, b + 1)
                    nc.vector.tensor_scalar(tmp[:], acc[:], 1.0, -1.0, ALU.add, ALU.add).then_inc(t_rdy, 1)
                    dve.wait_ge(t_rdy, b + 1)
                    nc.vector.tensor_tensor(acc[:], acc[:], tmp[:], ALU.subtract).then_inc(q_rdy, 1)
                    dve.wait_ge(q_rdy, b + 1)
                    D_ = dlt[:, b % 2, :, :]
                    nc.vector.tensor_tensor(D_, D_, acc[:], ALU.add).then_inc(d_step, 1)
                    dve.wait_ge(d_step, 3 * b + 1)
                    dve.wait_ge(ln_rdy, b + 1)
                    nc.vector.tensor_tensor(D_, D_, tmp[:], ALU.add).then_inc(d_step, 1)
                    dve.wait_ge(d_step, 3 * b + 2)
                    nc.vector.tensor_tensor(du[:, b % 2, :, :], D_, Y[:, b * KC:(b + 1) * KC, :],
                                            ALU.mult).then_inc(d_step, 1)

                def step(b, half, s, j):
                    dve.wait_ge(bc_evac, s + 2)
                    dve.wait_ge(sum_done, s + 1)
                    nc.vector.tensor_tensor(hs[:, j, :, :], du[:, b % 2, half * HC:(half + 1) * HC, :],
                                            Bs[:, j:j + 1, :].to_broadcast([P, HC, L]), ALU.mult).then_inc(bu_done, 1)
                    dve.wait_ge(exp_rdy, s + 1)
                    dve.wait_ge(bu_done, s + 1 + R)
                    flat = hs[:, j, :, :].rearrange("p k t -> p (k t)")
                    nc.vector.tensor_tensor_scan(flat, dA[:, j, :, :].rearrange("p k t -> p (k t)"), flat,
                                                 0.0, ALU.mult, ALU.add).then_inc(scan_done, 1)

                def scan(b, half):
                    s0 = b * STEPS + half * NS
                    dve.wait_ge(d_step, 3 * (b + 1))
                    for n in range(R):
                        step(b, half, s0 + n, n)
                    with dve.Fori(1, NS // R) as i:
                        for j in range(R):
                            step(b, half, s0 + R * i + j, j)

                prologue(0)
                for b in range(B):
                    scan(b, 0)
                    if b + 1 < B:
                        prologue(b + 1)
                    scan(b, 1)

            @block.gpsimd
            def _(pool):
                pool.sem_inc(prod_done, R)

                def step(s, j):
                    pool.wait_ge(scan_done, s + 1 + R)
                    pool.wait_ge(bc_evac, s + 2)
                    nc.gpsimd.tensor_tensor(hs[:, j, :, :], hs[:, j, :, :],
                                            Cs[:, j:j + 1, :].to_broadcast([P, HC, L]), ALU.mult).then_inc(prod_done, 1)

                for n in range(R):
                    step(n, n)
                with pool.Fori(1, B * STEPS // R) as i:
                    for j in range(R):
                        step(R * i + j, j)
        if l == 0:
            m.clear()


def gate(nc, l, d, X, Y, r):
    with ExitStack() as ctx:
        m = Mem(nc, ctx, f"gate{l}")
        ident = m.sb("ident", [P, P])
        st = m.sb("st", [P, 2, TT, 6])
        mv = m.sb("mv", [P, 2, TT, 2])
        sd = m.sb("sd", [P, 2, TT])
        rstd = m.sb("rstd", [P, 2, TT])
        nmr = m.sb("nmr", [P, 2, TT])
        eps = m.sb("eps", [P, 1])
        G = m.sb("G", [P, 4, L])
        xn = m.sb("xn", [P, 4, H])
        wr = m.sb("wr", [P, HK, E + 1])
        pt = [m.ps(f"pt{i}", [P, KC, P]) for i in range(4)]
        pn = [m.ps(f"pn{i}", [P, HK, P]) for i in range(2)]
        plog = m.ps("plog", [P, TT, 32])

        loaded = m.sem("loaded")
        eps_rdy = m.sem("eps_rdy")
        st_rdy = m.sem("st_rdy")
        mv_rdy = m.sem("mv_rdy")
        sd_rdy = m.sem("sd_rdy")
        rs_rdy = m.sem("rs_rdy")
        ln_rdy = m.sem("ln_rdy")
        g_rdy = m.sem("g_rdy")
        yg_rdy = m.sem("yg_rdy")
        tr_rdy = m.sem("tr_rdy")
        x_rdy = m.sem("x_rdy")
        xn_rdy = m.sem("xn_rdy")
        xn_out = [m.sem(f"xn_out{i}") for i in range(4)]
        tn_rdy = m.sem("tn_rdy")
        xT_rdy = m.sem("xT_rdy")
        lg_rdy = m.sem("lg_rdy")
        lg_out = m.sem("lg_out")

        with nc.Block() as block:

            @block.sync
            def _(sp):
                sp.dma_start(ident[:], d["ident"]).then_inc(loaded, 16)
                if l == 0:
                    sp.dma_start(wr[:], d["w_router"].rearrange("(k p) n -> p k n", p=P)).then_inc(loaded, 16)
                    for i in range(TT):
                        sp.wait_ge(xn_rdy, i + 1)
                        sp.dma_start(r["xn_d"][i * P:(i + 1) * P, :], xn[:, i % 4, :]).then_inc(xn_out[i % 4], 16)
                    for q in range(4):
                        sp.wait_ge(xn_out[q], 16 * TT // 4)

            NLOAD = 32 if l == 0 else 16

            @block.vector
            def _(dve):
                nc.vector.memset(eps[:], EPS).then_inc(eps_rdy, 1)
                for i in range(TT):
                    nc.vector.bn_stats(st[:, 0, i, :], X[:, i, :]).then_inc(st_rdy, 1)
                for i in range(TT):
                    dve.wait_ge(st_rdy, i + 1)
                    nc.vector.bn_aggr(mv[:, 0, i, :], st[:, 0, i, :]).then_inc(mv_rdy, 1)
                dve.wait_ge(sd_rdy, 1)
                nc.vector.reciprocal(rstd[:, 0, :], sd[:, 0, :]).then_inc(rs_rdy, 1)
                dve.wait_ge(rs_rdy, 1)
                nc.vector.scalar_tensor_tensor(out=nmr[:, 0, :], in0=mv[:, 0, :, 0], scalar=-1.0, in1=rstd[:, 0, :],
                                               op0=ALU.mult, op1=ALU.mult).then_inc(ln_rdy, 1)
                for b in range(B):
                    for c in range(KC):
                        i = b * KC + c
                        dve.wait_ge(tr_rdy, i + 1)
                        nc.vector.tensor_tensor(X[:, i, :], X[:, i, :], pt[i % 4][:].rearrange("p k t -> p (k t)"),
                                                ALU.add).then_inc(x_rdy, 1)
                    if l:
                        continue
                    own = slice(b * KC, (b + 1) * KC)
                    for c in range(KC):
                        i = b * KC + c
                        dve.wait_ge(x_rdy, i + 1)
                        nc.vector.bn_stats(st[:, 1, i, :], X[:, i, :]).then_inc(st_rdy, 1)
                    for c in range(KC):
                        i = b * KC + c
                        dve.wait_ge(st_rdy, TT + i + 1)
                        nc.vector.bn_aggr(mv[:, 1, i, :], st[:, 1, i, :]).then_inc(mv_rdy, 1)
                    dve.wait_ge(sd_rdy, b + 2)
                    nc.vector.reciprocal(rstd[:, 1, own], sd[:, 1, own]).then_inc(rs_rdy, 1)
                    dve.wait_ge(rs_rdy, b + 2)
                    nc.vector.scalar_tensor_tensor(out=nmr[:, 1, own], in0=mv[:, 1, own, 0], scalar=-1.0,
                                                   in1=rstd[:, 1, own], op0=ALU.mult, op1=ALU.mult).then_inc(ln_rdy, 1)
                    dve.wait_ge(ln_rdy, b + 2)
                    for c in range(KC):
                        i = b * KC + c
                        if i >= 4:
                            dve.wait_ge(xn_out[i % 4], 16 * (i // 4))
                            dve.wait_ge(tn_rdy, i - 3)
                        nc.vector.tensor_scalar(xn[:, i % 4, :], X[:, i, :], rstd[:, 1, i:i + 1], nmr[:, 1, i:i + 1],
                                                ALU.mult, ALU.add).then_inc(xn_rdy, 1)

            @block.scalar
            def _(act):
                act.wait_ge(eps_rdy, 1)
                act.wait_ge(mv_rdy, TT)
                nc.scalar.activation(sd[:, 0, :], mv[:, 0, :, 1], ACT.Sqrt, bias=eps[:]).then_inc(sd_rdy, 1)
                act.wait_ge(ln_rdy, 1)

                def silus(b):
                    for c in range(KC):
                        i = b * KC + c
                        if i >= 4:
                            act.wait_ge(yg_rdy, i - 3)
                        nc.scalar.activation(G[:, i % 4, :], X[:, i, :], ACT.Silu, bias=nmr[:, 0, i:i + 1],
                                             scale=rstd[:, 0, i:i + 1]).then_inc(g_rdy, 1)

                def second(b):
                    own = slice(b * KC, (b + 1) * KC)
                    act.wait_ge(mv_rdy, TT + (b + 1) * KC)
                    nc.scalar.activation(sd[:, 1, own], mv[:, 1, own, 1], ACT.Sqrt, bias=eps[:]).then_inc(sd_rdy, 1)

                def evac(b):
                    for c in range(KC):
                        i = b * KC + c
                        act.wait_ge(tn_rdy, i + 1)
                        nc.scalar.copy(r["xT"][:, :, i * P:(i + 1) * P], pn[i % 2][:]).then_inc(xT_rdy, 1)

                silus(0)
                for b in range(B):
                    if b + 1 < B:
                        silus(b + 1)
                    if l == 0:
                        second(b)
                        evac(b)
                if l == 0:
                    act.wait_ge(lg_rdy, TT)
                    nc.scalar.copy(r["logit"][:], plog[:, :, 0:E + 1]).then_inc(lg_out, 1)

            @block.gpsimd
            def _(pool):
                for i in range(TT):
                    pool.wait_ge(g_rdy, i + 1)
                    nc.gpsimd.tensor_tensor(Y[:, i, :], Y[:, i, :], G[:, i % 4, :], ALU.mult).then_inc(yg_rdy, 1)

            @block.tensor
            def _(pe):
                pe.wait_ge(loaded, NLOAD)
                for b in range(B):
                    pe.wait_ge(yg_rdy, (b + 1) * KC)
                    for t in range(KC):
                        i = b * KC + t
                        if i >= 4:
                            pe.wait_ge(x_rdy, i - 3)
                        for c in range(KC):
                            tr = nc.tensor.transpose(pt[i % 4][:, c, :], Y[:, b * KC + c, t * P:(t + 1) * P], ident[:])
                        tr.then_inc(tr_rdy, 1)
                    if l:
                        continue
                    for t in range(KC):
                        i = b * KC + t
                        pe.wait_ge(xn_rdy, i + 1)
                        if i >= 2:
                            pe.wait_ge(xT_rdy, i - 1)
                        for k in range(HK):
                            tr = nc.tensor.transpose(pn[i % 2][:, k, :], xn[:, i % 4, k * P:(k + 1) * P], ident[:])
                        tr.then_inc(tn_rdy, 1)
                    for t in range(KC):
                        i = b * KC + t
                        pe.wait_ge(xT_rdy, i + 1)
                        for k in range(HK):
                            mm = nc.tensor.matmul(plog[:, i, 0:E + 1], r["xT"][:, k, i * P:(i + 1) * P], wr[:, k, :],
                                                  start=(k == 0), stop=(k == HK - 1))
                        mm.then_inc(lg_rdy, 1)
        if l == 0:
            m.clear()


def routing(nc, d, r):
    with ExitStack() as ctx:
        m = Mem(nc, ctx, "rt")
        tri = m.sb("tri", [P, P])
        ones = m.sb("ones", [P, P])
        e_of = m.sb("e_of", [P, E])
        thr = m.sb("thr", [P, TT])
        col = m.sb("col", [P, P])
        tok = m.sb("tok", [P, TT])
        ex = m.sb("ex", [P, TT, E])
        mx = m.sb("mx", [P, TT])
        sm = m.sb("sm", [P, TT])
        ri = m.sb("ri", [P, TT])
        i8 = m.sb("i8", [P, TT, 8], U32)
        idf = m.sb("idf", [P, TT, 8])
        oh = m.sb("oh", [P, TOPK, TT, E])
        M = m.sb("M", [P, TT, E])
        base = m.sb("base", [P, TT, E])
        cnt = m.sb("cnt", [P, TT, E])
        off = m.sb("off", [P, TT + 1, E])
        cmp = m.sb("cmp", [P, E, TT])
        nt = m.sb("nt", [P, E])
        incl = m.sb("incl", [P, E])
        start = m.sb("start", [P, E])
        one_e = m.sb("one_e", [P, E])
        pos = m.sb("pos", [P, TT, TOPK])
        posi = m.sb("posi", [P, TT, TOPK], I32)
        sti = m.sb("sti", [P, TT, TOPK], I32)
        stf = m.sb("stf", [P, TT, TOPK])
        pp = m.sb("pp", [P, TT, TOPK])
        ohp = m.sb("ohp", [P, 4, P])
        ohs = m.sb("ohs", [P, 4, NSTEP])
        scm = m.sb("scm", [1, NSTEP, E])
        se = m.sb("se", [1, NSTEP + 1])
        pr_ = m.ps("pr", [P, TT * E])
        pc = m.ps("pc", [P, TT * E])
        pi = m.ps("pi", [P, NSTEP])

        loaded = m.sem("loaded")
        mx_rdy = m.sem("mx_rdy")
        e_rdy = m.sem("e_rdy")
        m_rdy = m.sem("m_rdy")
        rk_rdy = m.sem("rk_rdy")
        oh_rdy = m.sem("oh_rdy")
        oh_used = m.sem("oh_used")
        step = m.sem("step")
        fin = m.sem("fin")

        with nc.Block() as block:
            @block.sync
            def _(sp):
                for dst, n in [(tri, "tri"), (ones, "ones"), (e_of, "e_of"), (thr, "thr"), (col, "col"), (tok, "tok")]:
                    sp.dma_start(dst[:], d[n]).then_inc(loaded, 16)

            @block.scalar
            def _(act):
                act.wait_ge(mx_rdy, 1)
                nc.scalar.activation(ex[:], ex[:], ACT.Exp).then_inc(e_rdy, 1)
                nc.scalar.activation(r["sig"][:], r["logit"][:, :, E], ACT.Sigmoid).then_inc(fin, 1)

            @block.vector
            def _(dve):
                n = [0]

                def own(ins):
                    ins.then_inc(step, 1)
                    n[0] += 1
                    dve.wait_ge(step, n[0])

                V = nc.vector
                logit = r["logit"][:, :, 0:E]
                dve.wait_ge(loaded, 96)
                own(V.reduce_max(mx[:], logit, AX.X))
                V.tensor_tensor(ex[:], logit, mx[:].unsqueeze(2).to_broadcast([P, TT, E]), ALU.subtract).then_inc(mx_rdy, 1)
                dve.wait_ge(e_rdy, 1)
                own(V.reduce_sum(sm[:], ex[:], AX.X))
                own(V.reciprocal(ri[:], sm[:]))
                own(V.tensor_tensor(ex[:], ex[:], ri[:].unsqueeze(2).to_broadcast([P, TT, E]), ALU.mult))
                for i in range(TT):
                    mxi = V.max(r["w8"][:, i, :], ex[:, i, :])
                own(mxi)
                for i in range(TT):
                    mxi = V.max_index(i8[:, i, :], r["w8"][:, i, :], ex[:, i, :])
                own(mxi)
                own(V.tensor_copy(idf[:], i8[:]))
                for k in range(TOPK):
                    q = V.tensor_tensor(oh[:, k, :, :], e_of[:].unsqueeze(1).to_broadcast([P, TT, E]),
                                        idf[:, :, k:k + 1].to_broadcast([P, TT, E]), ALU.is_equal)
                own(q)
                own(V.tensor_tensor(M[:], oh[:, 0, :, :], oh[:, 1, :, :], ALU.add))
                own(V.tensor_tensor(M[:], M[:], oh[:, 2, :, :], ALU.add))
                own(V.tensor_tensor(M[:], M[:], oh[:, 3, :, :], ALU.add))
                V.memset(one_e[:], 1.0).then_inc(m_rdy, 1)
                own(V.memset(off[:, 0, :], 0.0))
                dve.wait_ge(rk_rdy, 2)
                own(V.tensor_copy(cnt[:].rearrange("p t e -> p (t e)"), pc[:]))
                for i in range(TT):
                    own(V.tensor_tensor(off[:, i + 1, :], off[:, i, :], cnt[:, i, :], ALU.add))
                own(V.tensor_tensor(cmp[:], off[:, TT, :].unsqueeze(2).to_broadcast([P, E, TT]),
                                    thr[:].unsqueeze(1).to_broadcast([P, E, TT]), ALU.is_gt))
                own(V.reduce_sum(nt[:], cmp[:], AX.X))
                own(V.tensor_scalar(nt[:], nt[:], 1.0, None, ALU.max))
                own(V.tensor_tensor_scan(incl[:], one_e[:], nt[:], 0.0, ALU.mult, ALU.add))
                own(V.tensor_tensor(start[:], incl[:], nt[:], ALU.subtract))
                own(V.scalar_tensor_tensor(out=base[:], in0=start[:].unsqueeze(1).to_broadcast([P, TT, E]), scalar=float(P),
                                           in1=off[:, 0:TT, :], op0=ALU.mult, op1=ALU.add))
                own(V.tensor_tensor(base[:], base[:], pr_[:].rearrange("p (t e) -> p t e", e=E), ALU.add))
                for k in range(TOPK):
                    q = V.tensor_tensor(oh[:, k, :, :], oh[:, k, :, :], base[:], ALU.mult)
                own(q)
                for k in range(TOPK):
                    q = V.reduce_sum(pos[:, :, k], oh[:, k, :, :], AX.X)
                own(q)
                V.tensor_copy(r["pos"][:], pos[:])
                own(V.tensor_copy(posi[:], pos[:]))
                own(V.tensor_scalar(sti[:], posi[:], 7, None, ALU.arith_shift_right))
                own(V.tensor_scalar(posi[:], posi[:], P - 1, None, ALU.bitwise_and))
                V.tensor_copy(stf[:], sti[:])
                own(V.tensor_copy(pp[:], posi[:]))
                for g in range(TT * TOPK):
                    i, k = g // TOPK, g % TOPK
                    if g >= 4:
                        dve.wait_ge(oh_used, g - 3)
                    V.tensor_scalar(ohp[:, g % 4, :], col[:], pp[:, i, k:k + 1], None, ALU.is_equal)
                    V.tensor_scalar(ohs[:, g % 4, :], col[:, 0:NSTEP], stf[:, i, k:k + 1], tok[:, i:i + 1],
                                    ALU.is_equal, ALU.mult).then_inc(oh_rdy, 1)
                own(V.tensor_tensor(scm[:], start[0:1, :].unsqueeze(1).to_broadcast([1, NSTEP, E]),
                                    col[0:1, 0:NSTEP].unsqueeze(2).to_broadcast([1, NSTEP, E]), ALU.is_le))
                own(V.memset(se[:], -1.0))
                own(V.reduce_sum(se[0:1, 1:NSTEP + 1], scm[:], AX.X))
                own(V.tensor_scalar(se[0:1, 1:NSTEP + 1], se[0:1, 1:NSTEP + 1], -1.0, None, ALU.add))
                V.tensor_tensor(r["tab"][0:1, 1, :], se[0:1, 1:NSTEP + 1], se[0:1, 0:NSTEP], ALU.subtract)
                own(V.tensor_copy(r["tab"][0:1, 0, :], se[0:1, 1:NSTEP + 1]))
                own(V.tensor_scalar(r["tab"][0:1, 2, :], r["tab"][0:1, 0, :], WR - 1, None, ALU.bitwise_and))
                dve.wait_ge(oh_used, TT * TOPK)
                own(V.tensor_copy(r["idx"][:], pi[:]))

            @block.tensor
            def _(pe):
                pe.wait_ge(loaded, 96)
                pe.wait_ge(m_rdy, 1)
                Mf = M[:].rearrange("p t e -> p (t e)")
                nc.tensor.matmul(pr_[:], tri[:], Mf, start=True, stop=True).then_inc(rk_rdy, 1)
                nc.tensor.matmul(pc[:], ones[:], Mf, start=True, stop=True).then_inc(rk_rdy, 1)
                G = TT * TOPK
                for g in range(G):
                    pe.wait_ge(oh_rdy, g + 1)
                    nc.tensor.matmul(pi[:], ohp[:, g % 4, :], ohs[:, g % 4, :], start=(g == 0),
                                     stop=(g == G - 1)).then_inc(oh_used, 1)


def experts(nc, d, r, X):
    with ExitStack() as ctx:
        m = Mem(nc, ctx, "moe")
        ident = m.sb("ident", [P, P])
        W1 = m.sb("W1", [P, WR, HK, 2 * IE])
        W2 = m.sb("W2", [P, WR, 3, H])
        xg = m.sb("xg", [P, 2, H])
        ist = m.sb("ist", [P, 2], U32)
        xt = m.sb("xt", [P, HK, P])
        sg = m.sb("sg", [P, IE])
        hh = m.sb("hh", [P, IE])
        ht = m.sb("ht", [P, 3, P])
        yo = m.sb("yo", [P, 2, H])
        pt = m.ps("pt", [P, HK, P])
        pg = m.ps("pg", [P, IE])
        pu = m.ps("pu", [P, IE])
        py = m.ps("py", [P, H])

        loaded = m.sem("loaded")
        wa = [m.sem(f"wa{i}") for i in range(WR)]
        wb = [m.sem(f"wb{i}") for i in range(2)]
        xg_in = [m.sem(f"xg_in{i}") for i in range(2)]
        ix_rdy = m.sem("ix_rdy")
        ix_seen = m.sem("ix_seen")
        w_free = m.sem("w_free")
        tx_rdy = m.sem("tx_rdy")
        xt_rdy = m.sem("xt_rdy")
        gu_rdy = m.sem("gu_rdy")
        sg_rdy = m.sem("sg_rdy")
        hh_rdy = m.sem("hh_rdy")
        th_rdy = m.sem("th_rdy")
        ht_rdy = m.sem("ht_rdy")
        y_rdy = m.sem("y_rdy")
        y_out = m.sem("y_out")
        y_st = [m.sem(f"y_st{i}") for i in range(2)]

        NA = NSH * TT
        NALL = NA + NSTEP

        def w_load(eng, slot, w13, w2, e, sem):
            w1 = W1[:, ds(slot, 1), :, :].rearrange("p o k n -> p (o k) n")
            w2_ = W2[:, ds(slot, 1), :, :].rearrange("p o k n -> p (o k) n")
            eng.dma_start(w1, w13[ds(e, 1), :, :].rearrange("e (k p) n -> p (e k) n", p=P)).then_inc(sem, 16)
            eng.dma_start(w2_[:, 0:2, :], w2[ds(e, 1), 0:256, :].rearrange("e (k p) n -> p (e k) n", p=P)).then_inc(sem, 16)
            eng.dma_start(w2_[0:96, 2, :], w2[ds(e, 1), 256:IE, :].rearrange("e p n -> p (e n)")).then_inc(sem, 16)

        with nc.Block() as block:

            @block.sync
            def _(sp):
                sp.dma_start(ident[:], d["ident"]).then_inc(loaded, 16)
                for j in range(NSH):
                    w_load(sp, j, d["w13s"], d["w2s"], j, wa[j])

                def step(s, j):
                    e = sp.value_load(r["tab"][0:1, 0, ds(s, 1)], min_val=0, max_val=E - 1)
                    f = sp.value_load(r["tab"][0:1, 1, ds(s, 1)], min_val=0, max_val=1)
                    w = sp.value_load(r["tab"][0:1, 2, ds(s, 1)], min_val=0, max_val=WR - 1)
                    with sp.If(f == 1):
                        w_load(sp, w, d["w13e"], d["w2e"], e, wb[j])
                    with sp.Else():
                        sp.sem_inc(wb[j], 48)

                for s in range(2):
                    sp.wait_ge(y_rdy, (s + 1) * TT)
                    step(s, s)
                with sp.Fori(1, NSTEP // 2) as i:
                    for j in range(2):
                        sp.wait_ge(y_rdy, 2 * i + (j + NA - WR + 1))
                        sp.sem_inc(w_free, 1)
                        sp.wait_ge(wb[j], 48 * i)
                        sp.sem_inc(w_free, 1)
                        step(2 * i + j, j)
                for j in range(2):
                    sp.wait_ge(wb[j], 48 * NSTEP // 2)

            @block.gpsimd
            def _(pool):
                def fetch(s, j):
                    nc.gpsimd.tensor_copy(ist[:, j:j + 1], r["idx"][:, ds(s, 1)]).then_inc(ix_rdy, 1)
                    pool.wait_ge(ix_rdy, s + 1)
                    pool.sem_inc(ix_seen, 1)
                    nc.gpsimd.indirect_dma_start(
                        out=xg[:, j, :], out_offset=None, in_=r["xn_d"],
                        in_offset=bass.IndirectOffsetOnAxis(ap=ist[:, j:j + 1], axis=0)).then_inc(xg_in[j], 16)

                for s in range(2):
                    fetch(s, s)
                with pool.Fori(1, NSTEP // 2) as i:
                    for j in range(2):
                        pool.wait_ge(tx_rdy, 2 * i + (j - 1))
                        fetch(2 * i + j, j)

            @block.tensor
            def _(pe):
                def x_transpose(s, n16, j):
                    pe.wait_ge(xg_in[j], n16)
                    pe.wait_ge(ht_rdy, s + (NA - 1))
                    for k in range(HK):
                        tr = nc.tensor.transpose(pt[:, k, :], xg[:, j, k * P:(k + 1) * P], ident[:])
                    tr.then_inc(tx_rdy, 1)

                def down(g, w):
                    pe.wait_ge(ht_rdy, g + 1)
                    if not (isinstance(g, int) and g < 1):
                        pe.wait_ge(y_out, g)
                    for q, (o, n) in enumerate(ICH):
                        mm = nc.tensor.matmul(py[:], ht[0:n, q, :], w2_of(w, n, q), start=(q == 0), stop=(q == 2))
                    mm.then_inc(y_rdy, 1)

                def w2_of(w, n, q):
                    return W2[0:n, w, q, :] if isinstance(w, int) else \
                        W2[0:n, ds(w, 1), q, :].rearrange("p o n -> p (o n)")

                def w1_of(w, k, o):
                    return W1[:, w, k, o:o + IE] if isinstance(w, int) else \
                        W1[:, ds(w, 1), k, o:o + IE].rearrange("p o n -> p (o n)")

                def h_transpose(g):
                    pe.wait_ge(hh_rdy, g + 1)
                    pe.wait_ge(xt_rdy, g + 2)
                    for q, (o, n) in enumerate(ICH):
                        tr = nc.tensor.transpose(pt[0:n, q, :], hh[:, o:o + n], ident[:])
                    tr.then_inc(th_rdy, 1)

                def up(g, w):
                    pe.wait_ge(xt_rdy, g + 1)
                    for ps, o in ((pg, 0), (pu, IE)):
                        for k in range(HK):
                            mm = nc.tensor.matmul(ps[:], xt[:, k, :], w1_of(w, k, o), start=(k == 0), stop=(k == HK - 1))
                    mm.then_inc(gu_rdy, 1)

                def slot_of(s):
                    return pe.value_load(r["tab"][0:1, 2, ds(s, 1)], min_val=0, max_val=WR - 1)

                pe.wait_ge(loaded, 16)
                for q in range(NSH):
                    pe.wait_ge(wa[q], 48)
                    for t in range(2):
                        g = q * TT + t
                        if g >= 2:
                            down(g - 2, q - 1)
                        if g >= 1:
                            h_transpose(g - 1)
                        up(g, q)
                    with pe.Fori(1, TT // 2) as i:
                        for j in range(2):
                            g = 2 * i + (q * TT + j)
                            down(g - 2, q)
                            h_transpose(g - 1)
                            up(g, q)
                for s in range(2):
                    x_transpose(s, 16, s)
                    down(NA + s - 2, NSH - 1)
                    h_transpose(NA + s - 1)
                    w = slot_of(s)
                    pe.wait_ge(wb[s], 48)
                    up(NA + s, w)
                with pe.Fori(1, NSTEP // 2) as i:
                    for j in range(2):
                        s = 2 * i + j
                        x_transpose(s, 16 * i + 16, j)
                        down(s + (NA - 2), slot_of(s - 2))
                        h_transpose(s + (NA - 1))
                        pe.wait_ge(wb[j], 48 * i + 48)
                        up(s + NA, slot_of(s))
                down(NALL - 2, slot_of(NSTEP - 2))
                pe.wait_ge(hh_rdy, NALL)
                for q, (o, n) in enumerate(ICH):
                    tr = nc.tensor.transpose(pt[0:n, q, :], hh[:, o:o + n], ident[:])
                tr.then_inc(th_rdy, 1)
                down(NALL - 1, slot_of(NSTEP - 1))

            @block.scalar
            def _(act):
                def h_evac(g):
                    act.wait_ge(th_rdy, g + 1)
                    nc.scalar.copy(ht[:, 0:2, :], pt[:, 0:2, :])
                    nc.scalar.copy(ht[0:96, 2, :], pt[0:96, 2, :]).then_inc(ht_rdy, 1)

                def silu(g):
                    act.wait_ge(gu_rdy, g + 1)
                    nc.scalar.activation(sg[:], pg[:], ACT.Silu).then_inc(sg_rdy, 1)

                def y_store(s, j):
                    act.wait_ge(y_out, s + (NA + 1))
                    act.dma_start(r["y_d"][ds(s * P, P), :], yo[:, j, :]).then_inc(y_st[j], 16)

                def shared(g, t):
                    if not (isinstance(g, int) and g == 0):
                        act.wait_ge(gu_rdy, g)
                    nc.scalar.copy(xt[:], r["xT"][:, :, ds(t * P, P)]).then_inc(xt_rdy, 1)

                def slots(s):
                    act.wait_ge(tx_rdy, s + 1)
                    nc.scalar.copy(xt[:], pt[:]).then_inc(xt_rdy, 1)

                for q in range(NSH):
                    for t in range(2):
                        g = q * TT + t
                        shared(g, t)
                        if g >= 1:
                            h_evac(g - 1)
                        silu(g)
                    with act.Fori(1, TT // 2) as i:
                        for j in range(2):
                            g = 2 * i + (q * TT + j)
                            shared(g, 2 * i + j)
                            h_evac(g - 1)
                            silu(g)
                for s in range(2):
                    slots(s)
                    h_evac(NA + s - 1)
                    silu(NA + s)
                with act.Fori(1, NSTEP // 2) as i:
                    for j in range(2):
                        s = 2 * i + j
                        slots(s)
                        h_evac(s + (NA - 1))
                        silu(s + NA)
                        y_store(s - 2, j)
                h_evac(NALL - 1)
                for j in range(2):
                    y_store(NSTEP - 2 + j, j)
                for j in range(2):
                    act.wait_ge(y_st[j], 16 * NSTEP // 2)

            @block.vector
            def _(dve):
                def h(g):
                    dve.wait_ge(sg_rdy, g + 1)
                    nc.vector.tensor_tensor(hh[:], sg[:], pu[:], ALU.mult).then_inc(hh_rdy, 1)

                def y_shared(g, t):
                    dve.wait_ge(y_rdy, g + 1)
                    if not (isinstance(g, int) and g < TT):
                        dve.wait_ge(y_out, g - (TT - 1))
                    xs = X[:, ds(t, 1), :].rearrange("p o n -> p (o n)")
                    nc.vector.scalar_tensor_tensor(out=xs, in0=py[:], scalar=r["sig"][:, ds(t, 1)], in1=xs,
                                                   op0=ALU.mult, op1=ALU.add).then_inc(y_out, 1)

                def y_slots(s, j, n16):
                    dve.wait_ge(y_rdy, s + (NA + 1))
                    if n16 is not None:
                        dve.wait_ge(y_st[j], n16)
                    nc.vector.tensor_copy(yo[:, j, :], py[:]).then_inc(y_out, 1)

                for q in range(NSH):
                    for t in range(2):
                        g = q * TT + t
                        if g >= 2:
                            y_shared(g - 2, TT - 2 + t)
                        h(g)
                    with dve.Fori(1, TT // 2) as i:
                        for j in range(2):
                            g = 2 * i + (q * TT + j)
                            if q == 0:
                                dve.wait_ge(y_rdy, g - 1)
                                t = 2 * i + (j - 2)
                                xs = X[:, ds(t, 1), :].rearrange("p o n -> p (o n)")
                                nc.vector.scalar_tensor_tensor(out=xs, in0=py[:], scalar=r["sig"][:, ds(t, 1)], in1=xs,
                                                               op0=ALU.mult, op1=ALU.add).then_inc(y_out, 1)
                            else:
                                y_shared(g - 2, 2 * i + (j - 2))
                            h(g)
                for s in range(2):
                    y_shared(NA - 2 + s, TT - 2 + s)
                    h(NA + s)
                for j in range(2):
                    y_slots(j, j, None)
                    h(NA + 2 + j)
                with dve.Fori(2, NSTEP // 2) as i:
                    for j in range(2):
                        y_slots(2 * i + (j - 2), j, 16 * i - 16)
                        h(2 * i + (NA + j))
                for j in range(2):
                    y_slots(NSTEP - 2 + j, j, 16 * (NSTEP // 2) - 16)


def combine(nc, r, X):
    with ExitStack() as ctx:
        m = Mem(nc, ctx, "comb")
        NR = 8
        yr = m.sb("yr", [P, NR, H])
        got = [m.sem(f"got{i}") for i in range(NR)]
        used = m.sem("used")
        with nc.Block() as block:
            @block.gpsimd
            def _(pool):
                for g in range(TT * TOPK):
                    i, k = g // TOPK, g % TOPK
                    if g >= NR:
                        pool.wait_ge(used, g - NR + 1)
                    nc.gpsimd.indirect_dma_start(
                        out=yr[:, g % NR, :], out_offset=None, in_=r["y_d"],
                        in_offset=bass.IndirectOffsetOnAxis(ap=r["pos"][:, i, k:k + 1], axis=0)).then_inc(got[g % NR], 16)

            @block.vector
            def _(dve):
                for g in range(TT * TOPK):
                    i, k = g // TOPK, g % TOPK
                    dve.wait_ge(got[g % NR], 16 * (g // NR + 1))
                    if k:
                        dve.wait_ge(used, g)
                    nc.vector.scalar_tensor_tensor(out=X[:, i, :], in0=yr[:, g % NR, :], scalar=r["w8"][:, i, k:k + 1],
                                                   in1=X[:, i, :], op0=ALU.mult, op1=ALU.add).then_inc(used, 1)


def quant_ffn(nc, d, X, out):
    with ExitStack() as ctx:
        m = Mem(nc, ctx, "ffn")
        ident = m.sb("ident", [P, P], BF16)
        ones = m.sb("ones", [P, P])
        stg = m.sb("stg", [P, 2, 2048])
        Wq = [m.sb(f"Wq{i}", [P, 4, 2048], BF16) for i in range(3)]
        wsum = m.sb("wsum", [P, 3, 4])
        wtot = m.sb("wtot", [P, 3])
        wsc = m.sb("wsc", [P, 3])
        whi = m.sb("whi", [P, 3])
        wlo = m.sb("wlo", [P, 3])
        neg = m.sb("neg", [P, 2048])
        eps = m.sb("eps", [P, 1])
        st = m.sb("st", [P, TT, 6])
        mv = m.sb("mv", [P, TT, 2])
        sd = m.sb("sd", [P, TT])
        rstd = m.sb("rstd", [P, TT])
        nmr = m.sb("nmr", [P, TT])
        xn = m.sb("xn", [P, 2, H])
        xq = m.sb("xq", [P, 2, H], BF16)
        xqT = m.sb("xqT", [P, 2, HK, P], BF16)
        sx = m.sb("sx", [P, TT, 5])
        sh = m.sb("sh", [P, TT, 4])
        gg = m.sb("gg", [P, 2, IF])
        hq = m.sb("hq", [P, 2, IF], BF16)
        hqT = m.sb("hqT", [P, 2, FK, P], BF16)
        pa = m.ps("pa", [P, 4])
        pg = [m.ps(f"pg{i}", [P, 512]) for i in range(2)]
        pu = [m.ps(f"pu{i}", [P, 512]) for i in range(2)]
        pt = m.ps("pt", [P, 8, P], BF16)
        pd = m.ps("pd", [P, H])

        loaded = m.sem("loaded")
        stg_in = [m.sem(f"stg_in{i}") for i in range(2)]
        abs_rdy = m.sem("abs_rdy")
        stg_used = m.sem("stg_used")
        tot_rdy = m.sem("tot_rdy")
        w_step = m.sem("w_step")
        wq_rdy = m.sem("wq_rdy")
        eps_rdy = m.sem("eps_rdy")
        mv_rdy = m.sem("mv_rdy")
        sd_rdy = m.sem("sd_rdy")
        ln_rdy = m.sem("ln_rdy")
        step = m.sem("step")
        xq_rdy = m.sem("xq_rdy")
        tx_rdy = m.sem("tx_rdy")
        xqT_rdy = m.sem("xqT_rdy")
        gu_rdy = m.sem("gu_rdy")
        sg_rdy = m.sem("sg_rdy")
        gh_rdy = m.sem("gh_rdy")
        hq_rdy = m.sem("hq_rdy")
        th_rdy = m.sem("th_rdy")
        hqT_rdy = m.sem("hqT_rdy")
        dn_rdy = m.sem("dn_rdy")
        x_rdy = m.sem("x_rdy")
        o_out = m.sem("o_out")

        src = [d["w_gate"].rearrange("(k p) n -> k p n", p=P), d["w_up"].rearrange("(k p) n -> k p n", p=P),
               d["w_down"].rearrange("(g k p) n -> g p k n", k=4, p=P)]

        def piece(w, k):
            return src[w][k] if w < 2 else src[w][k]

        with nc.Block() as block:

            @block.sync
            def _(sp):
                sp.dma_start(ident[:], d["ident_bf"]).then_inc(loaded, 16)
                sp.dma_start(ones[:], d["ones"]).then_inc(loaded, 16)
                n = 0
                for turn in range(2):
                    for w in range(3):
                        for k in range(4):
                            if n >= 2:
                                sp.wait_ge(stg_used, n - 1)
                            dst = stg[:, n % 2, :] if w < 2 else stg[:, n % 2, :].rearrange("p (k n) -> p k n", k=4)
                            sp.dma_start(dst, piece(w, k)).then_inc(stg_in[n % 2], 16)
                            n += 1
                for i in range(TT):
                    sp.wait_ge(x_rdy, i + 1)
                    sp.dma_start(out[i * P:(i + 1) * P, :], X[:, i, :]).then_inc(o_out, 16)
                sp.wait_ge(o_out, 16 * TT)

            @block.vector
            def _(dve):
                V = nc.vector
                n = [0]

                def own(ins):
                    ins.then_inc(step, 1)
                    n[0] += 1
                    dve.wait_ge(step, n[0])

                V.memset(eps[:], EPS).then_inc(eps_rdy, 1)
                for i in range(TT):
                    q = V.bn_stats(st[:, i, :], X[:, i, :])
                own(q)
                for i in range(TT):
                    q = V.bn_aggr(mv[:, i, :], st[:, i, :])
                q.then_inc(mv_rdy, 1)
                dve.wait_ge(sd_rdy, 1)
                own(V.reciprocal(rstd[:], sd[:]))
                own(V.scalar_tensor_tensor(out=nmr[:], in0=mv[:, :, 0], scalar=-1.0, in1=rstd[:], op0=ALU.mult, op1=ALU.mult))
                N = 0
                for w in range(3):
                    for k in range(4):
                        dve.wait_ge(stg_in[N % 2], 16 * (N // 2 + 1))
                        V.tensor_reduce(wsum[:, w, k:k + 1], stg[:, N % 2, :], AX.X, ALU.add,
                                        apply_absolute_value=True).then_inc(stg_used, 1)
                        N += 1
                dve.wait_ge(stg_used, N)
                V.reduce_sum(wtot[:], wsum[:], AX.X).then_inc(abs_rdy, 1)
                dve.wait_ge(tot_rdy, 1)
                own(V.tensor_scalar(wsc[:], pa[:, 0:3], 1.0 / (H * IF), EPS, ALU.mult, ALU.add))
                V.tensor_scalar(whi[:], wsc[:], 0.5, None, ALU.mult)
                own(V.tensor_scalar(wlo[:], wsc[:], -0.5, None, ALU.mult))
                for w in range(3):
                    for k in range(4):
                        dve.wait_ge(stg_in[N % 2], 16 * (N // 2 + 1))
                        own(V.tensor_scalar(neg[:], stg[:, N % 2, :], wlo[:, w:w + 1], None, ALU.is_lt))
                        V.scalar_tensor_tensor(out=Wq[w][:, k, :], in0=stg[:, N % 2, :], scalar=whi[:, w:w + 1], in1=neg[:],
                                               op0=ALU.is_gt, op1=ALU.subtract).then_inc(stg_used, 1)
                        N += 1
                        dve.wait_ge(stg_used, N)
                V.memset(neg[:, 0:1], 0.0).then_inc(wq_rdy, 1)

                def quant(dst, src_, s, flat_n):
                    own(V.tensor_reduce(s[:, 0:1], src_, AX.X, ALU.max, apply_absolute_value=True))
                    own(V.tensor_scalar(s[:, 1:2], s[:, 0:1], 1.0 / 127.0, EPS, ALU.mult, ALU.add))
                    own(V.reciprocal(s[:, 2:3], s[:, 1:2]))
                    own(V.tensor_scalar(src_, src_, s[:, 2:3], ROUND, ALU.mult, ALU.add))
                    return V.tensor_scalar(dst, src_, -ROUND, 127.0, ALU.add, ALU.min)

                def x_quant(i):
                    xi = xn[:, i % 2, :]
                    own(V.tensor_scalar(xi, X[:, i, :], rstd[:, i:i + 1], nmr[:, i:i + 1], ALU.mult, ALU.add))
                    if i >= 2:
                        dve.wait_ge(tx_rdy, i - 1)
                    own(quant(xq[:, i % 2, :], xi, sx[:, i, :], H))
                    V.tensor_scalar(sx[:, i, 3:4], sx[:, i, 1:2], wsc[:, 0:1], None, ALU.mult)
                    V.tensor_scalar(sx[:, i, 4:5], sx[:, i, 1:2], wsc[:, 1:2], None, ALU.mult).then_inc(xq_rdy, 1)

                x_quant(0)
                for i in range(TT):
                    if i + 1 < TT:
                        x_quant(i + 1)
                    for f in range(FC):
                        g = i * FC + f
                        dve.wait_ge(sg_rdy, g + 1)
                        if f == 0:
                            dve.wait_ge(xq_rdy, i + 1)
                        s = gg[:, i % 2, f * 512:(f + 1) * 512]
                        V.scalar_tensor_tensor(out=s, in0=pu[g % 2][:], scalar=sx[:, i, 4:5], in1=s,
                                               op0=ALU.mult, op1=ALU.mult).then_inc(gh_rdy, 1)
                    dve.wait_ge(gh_rdy, (i + 1) * FC)
                    if i >= 2:
                        dve.wait_ge(th_rdy, 2 * (i - 1))
                    own(quant(hq[:, i % 2, :], gg[:, i % 2, :], sh[:, i, :], IF))
                    V.tensor_scalar(sh[:, i, 3:4], sh[:, i, 1:2], wsc[:, 2:3], None, ALU.mult).then_inc(hq_rdy, 1)
                    if i:
                        dve.wait_ge(dn_rdy, i)
                        V.scalar_tensor_tensor(out=X[:, i - 1, :], in0=pd[:], scalar=sh[:, i - 1, 3:4], in1=X[:, i - 1, :],
                                               op0=ALU.mult, op1=ALU.add).then_inc(x_rdy, 1)
                dve.wait_ge(dn_rdy, TT)
                dve.wait_ge(hq_rdy, TT)
                V.scalar_tensor_tensor(out=X[:, TT - 1, :], in0=pd[:], scalar=sh[:, TT - 1, 3:4], in1=X[:, TT - 1, :],
                                       op0=ALU.mult, op1=ALU.add).then_inc(x_rdy, 1)

            @block.scalar
            def _(act):
                act.wait_ge(eps_rdy, 1)
                act.wait_ge(mv_rdy, 1)
                nc.scalar.activation(sd[:], mv[:, :, 1], ACT.Sqrt, bias=eps[:]).then_inc(sd_rdy, 1)

                def xT(i):
                    act.wait_ge(tx_rdy, i + 1)
                    nc.scalar.copy(xqT[:, i % 2, :, :], pt[:, 0:HK, :]).then_inc(xqT_rdy, 1)

                xT(0)
                for i in range(TT):
                    act.wait_ge(xq_rdy, i + 1)
                    for f in range(FC):
                        g = i * FC + f
                        act.wait_ge(gu_rdy, g + 1)
                        if i >= 2:
                            act.wait_ge(hq_rdy, i - 1)
                        nc.scalar.activation(gg[:, i % 2, f * 512:(f + 1) * 512], pg[g % 2][:], ACT.Silu,
                                             scale=sx[:, i, 3:4]).then_inc(sg_rdy, 1)
                    if i + 1 < TT:
                        xT(i + 1)
                    for a in range(2):
                        act.wait_ge(th_rdy, 2 * i + a + 1)
                        nc.scalar.copy(hqT[:, i % 2, 8 * a:8 * a + 8, :], pt[:]).then_inc(hqT_rdy, 1)

            @block.tensor
            def _(pe):
                pe.wait_ge(loaded, 32)
                pe.wait_ge(abs_rdy, 1)
                nc.tensor.matmul(pa[:, 0:3], ones[:], wtot[:], start=True, stop=True).then_inc(tot_rdy, 1)
                pe.wait_ge(wq_rdy, 1)

                def xT(i):
                    pe.wait_ge(xq_rdy, i + 1)
                    if i:
                        pe.wait_ge(hqT_rdy, 2 * (i - 1))
                    for k in range(HK):
                        tr = nc.tensor.transpose(pt[:, k, :], xq[:, i % 2, k * P:(k + 1) * P], ident[:])
                    tr.then_inc(tx_rdy, 1)

                def down(i):
                    pe.wait_ge(hq_rdy, i + 1)
                    for a in range(2):
                        if a:
                            pe.wait_ge(hqT_rdy, 2 * i + 1)
                        elif i + 1 < TT:
                            pe.wait_ge(xqT_rdy, i + 2)
                        for k in range(8):
                            o = (8 * a + k) * P
                            tr = nc.tensor.transpose(pt[:, k, :], hq[:, i % 2, o:o + P], ident[:])
                        tr.then_inc(th_rdy, 1)
                    if i:
                        pe.wait_ge(x_rdy, i)
                    for k in range(FK):
                        if k % 8 == 0:
                            pe.wait_ge(hqT_rdy, 2 * i + k // 8 + 1)
                        mm = nc.tensor.matmul(pd[:], hqT[:, i % 2, k, :], Wq[2][:, k // 4, (k % 4) * H:(k % 4 + 1) * H],
                                              start=(k == 0), stop=(k == FK - 1))
                    mm.then_inc(dn_rdy, 1)

                xT(0)
                for i in range(TT):
                    pe.wait_ge(xqT_rdy, i + 1)
                    for f in range(FC):
                        g = i * FC + f
                        if g >= 2:
                            pe.wait_ge(gh_rdy, g - 1)
                        for ps, w in ((pg, 0), (pu, 1)):
                            for k in range(HK):
                                mm = nc.tensor.matmul(ps[g % 2][:], xqT[:, i % 2, k, :], Wq[w][:, k, f * 512:(f + 1) * 512],
                                                      start=(k == 0), stop=(k == HK - 1))
                        mm.then_inc(gu_rdy, 1)
                    if i + 1 < TT:
                        xT(i + 1)
                    down(i)


def bass_program(nc, d, out):
    with ExitStack() as ctx:
        m = Mem(nc, ctx, "all")
        X = m.sb("X", [P, TT, H])
        Y = m.sb("Y", [P, TT, L])
        xn_d = nc.dram_tensor("xn_rows", (T, H), F32).ap()
        y_d = nc.dram_tensor("y_rows", (NSLOT, H), F32).ap()
        ssm_layer(nc, 0, d, X, Y)
        with ExitStack() as c2:
            q = Mem(nc, c2, "moeio")
            r = {"xn_d": xn_d, "y_d": y_d,
                 "xT": q.sb("xT", [P, HK, T]),
                 "logit": q.sb("logit", [P, TT, E + 1]),
                 "w8": q.sb("w8", [P, TT, 8]),
                 "pos": q.sb("pos", [P, TT, TOPK], U32),
                 "idx": q.sb("idx", [P, NSTEP], U32),
                 "tab": q.sb("tab", [1, 3, NSTEP], I32),
                 "sig": q.sb("sig", [P, TT])}
            gate(nc, 0, d, X, Y, r)
            routing(nc, d, r)
            experts(nc, d, r, X)
            combine(nc, r, X)
        ssm_layer(nc, 1, d, X, Y)
        gate(nc, 1, d, X, Y, None)
        quant_ffn(nc, d, X, out)


def layouts(inputs):
    import numpy as np
    a = {k: np.asarray(v) for k, v in inputs.items()}
    c = np.ascontiguousarray
    p = np.arange(P)
    d = {
        "x": c(a["x"].reshape(T, H)),
        "ctxT": c(a["ctx_1024"].reshape(T, DM).T),
        "ident": np.eye(P, dtype=np.float32),
        "sel": c((p[:96, None, None] % (2 * NS) == np.arange(2 * NS)[None, :, None])
                 * np.ones((1, 1, P))).astype(mybir.dt.np(BF16)),
    }
    d.update({
        "ident_bf": np.eye(P, dtype=np.float32).astype(mybir.dt.np(BF16)),
        "tri": np.triu(np.ones((P, P), np.float32), 1),
        "ones": np.ones((P, P), np.float32),
        "e_of": np.tile(np.arange(E, dtype=np.float32), (P, 1)),
        "thr": np.tile(np.arange(TT, dtype=np.float32) * P, (P, 1)),
        "col": np.tile(np.arange(P, dtype=np.float32), (P, 1)),
        "tok": c((np.arange(TT)[None, :] * P + p[:, None]).astype(np.float32)),
        "w_router": c(np.concatenate([a["L0_ffn_gate_w"], a["L0_ffn_sgate_w"]], 0).T),
        "w13e": c(a["L0_ffn_w13"].transpose(0, 2, 1)),
        "w2e": c(a["L0_ffn_w2"].transpose(0, 2, 1)),
        "w13s": c(a["L0_ffn_shared_gate_up_w"].reshape(2, NSH, IE, H).transpose(1, 3, 0, 2).reshape(NSH, H, 2 * IE)),
        "w2s": c(a["L0_ffn_shared_down_w"].reshape(H, NSH, IE).transpose(1, 2, 0)),
        "w_gate": c(a["L1_ffn_w_gate"].T),
        "w_up": c(a["L1_ffn_w_up"].T),
        "w_down": c(a["L1_ffn_w_down"].T),
    })
    for l in range(2):
        w = {k[len(f"L{l}_xattn_"):]: v for k, v in a.items() if k.startswith(f"L{l}_xattn_")}
        xp = w["x_proj_w"]
        d[f"w_in{l}"] = c(w["in_proj_w"].T)
        d[f"w_dt{l}"] = c(xp[:DR].T)
        d[f"w_bc{l}"] = c(np.concatenate([xp[DR:]] * 3, 0).T)
        d[f"w_up{l}"] = c(w["dt_proj_w"].T)
        d[f"cw{l}"] = c(w["conv_w"].reshape(DI, DC))
        d[f"cb{l}"] = c(w["conv_b"].reshape(KC, P).T)
        d[f"db{l}"] = c(w["dt_proj_b"].reshape(KC, P).T)
        d[f"D{l}"] = c(w["D"].reshape(KC, P).T)
        d[f"alog{l}"] = c(w["A_log"])
    return d


def kernel(**inputs):
    import numpy as np
    import concourse.bacc as bacc
    from concourse.bass_utils import run_bass_kernel_spmd

    nc = bacc.Bacc("TRN2", target_bir_lowering=False, num_devices=1)
    arrays = {f"in_{k}": v for k, v in layouts(inputs).items()}
    aps = {k[3:]: nc.dram_tensor(k, v.shape, mybir.dt.from_np(v.dtype), kind="ExternalInput").ap()
           for k, v in arrays.items()}
    out = nc.dram_tensor("out_0_dram", (T, H), F32, kind="ExternalOutput").ap()
    bass_program(nc, aps, out)
    r = run_bass_kernel_spmd(nc, [arrays], core_ids=[0])
    return r.results[0]["out_0_dram"].reshape(B, L, H)
```

```python
import concourse.bass as bass
from concourse import mybir
from contextlib import ExitStack

F32 = mybir.dt.float32
F16 = mybir.dt.float16
BF16 = mybir.dt.bfloat16
I32 = mybir.dt.int32
U32 = mybir.dt.uint32
ALU = mybir.AluOpType
ACT = mybir.ActivationFunctionType
AX = mybir.AxisListType
ds = bass.ds

P = 128
B, L, H = 4, 512, 512
T = B * L
TT = T // P
DM = 256
DI, NS, DC, DR = 512, 16, 4, 16
KC = DI // P
HC = KC // 2
HK = H // P
E, TOPK, IE = 16, 4, 352
ISH = 1408
NSH = ISH // IE
NSTEP = T * TOPK // P + E
NSLOT = NSTEP * P
NEX = E + NSH
WE = 4 * 2 * IE + 3 * H
WS = 256.0
XS = 256.0
HS = 16.0
NA = NSH * TT
NALL = NA + NSTEP
R = 4
WR = 3
IF = 2048
FC = IF // 512
FK = IF // P
STEPS = 2 * NS
EPS = 1e-5
ROUND = 12582912.0
ICH = [(0, 128), (128, 128), (256, 96)]


class Mem:

    def __init__(self, nc, ctx, tag):
        self.nc, self.ctx, self.tag, self.sems = nc, ctx, tag, []

    def sb(self, name, shape, dt=F32):
        return self.ctx.enter_context(self.nc.sbuf_tensor(f"{self.tag}_{name}", shape, dt))

    def ps(self, name, shape, dt=F32):
        return self.ctx.enter_context(self.nc.psum_tensor(f"{self.tag}_{name}", shape, dt))

    def sem(self, name):
        self.sems.append(self.ctx.enter_context(self.nc.semaphore(f"{self.tag}_{name}")))
        return self.sems[-1]

    def clear(self):
        with self.nc.Block() as block:
            @block.sync
            def _(sp):
                for s in self.sems:
                    sp.sem_clear(s)


class Ssm:

    def __init__(self, nc, m, l, d, dbl, nb, ny, ring, alias):
        self.alias, self.ny = alias, ny
        self.nc, self.l, self.d, self.dbl, self.nb, self.ring = nc, l, d, dbl, nb, ring
        self.sel = m.sb("sel", [96, 2 * NS, P], BF16)
        self.cx = m.sb("cx", [P, 2, L])
        self.w_in = m.sb("w_in", [P, 2, DI])
        self.w_x = m.sb("w_x", [P, KC, 96 + DR])
        self.w_up = m.sb("w_up", [P, DI])
        self.cw = m.sb("cw", [P, KC, DC])
        self.cb = m.sb("cb", [P, KC])
        self.db = m.sb("db", [P, KC])
        self.alog = m.sb("alog", [P, KC, NS])
        self.A = m.sb("A", [P, KC, NS])
        self.Dv = m.sb("Dv", [P, KC])
        self.diagD = m.sb("diagD", [P, KC, P])
        self.ident = m.sb("ident", [P, P])
        self.U = m.sb("U", [P, dbl, KC, L])
        self.dlt = m.sb("dlt", [P, dbl, KC, L])
        self.du = m.sb("du", [P, dbl, KC, L])
        self.bc3 = m.sb("bc3", [96, dbl, L], BF16)
        self.low = m.sb("low", [P, L])
        self.Bs = m.sb("Bs", [P, ring, L])
        self.Cs = m.sb("Cs", [P, R, L])
        self.dA = m.sb("dA", [P, ring, HC, L])
        self.hs = m.sb("hs", [P, R, HC, L])
        self.pair = m.sb("pair", [P, 2, HC, L])
        if alias:
            self.acc = self.hs[:, 0:2, :, :].rearrange("p a b t -> p (a b) t")
            self.tmp = self.hs[:, 2:4, :, :].rearrange("p a b t -> p (a b) t")
        else:
            self.acc = m.sb("acc", [P, KC, L])[:]
            self.tmp = m.sb("tmp", [P, KC, L])[:]
        self.pB = [m.ps(f"pB{i}", [P, L]) for i in range(nb)]
        self.pC = [m.ps(f"pC{i}", [P, L]) for i in range(nb)]
        self.pY = [[m.ps(f"pY{i}{k}", [P, L]) for k in range(HC)] for i in range(ny)]
        self.pw = [self.pB[0], self.pC[0]] if alias else [m.ps(f"pw{i}", [P, L]) for i in range(2)]

        self.loaded = m.sem("loaded")
        self.cx_in = m.sem("cx_in")
        self.a_exp = m.sem("a_exp")
        self.a_neg = m.sem("a_neg")
        self.diag_rdy = m.sem("diag_rdy")
        self.in_rdy = m.sem("in_rdy")
        self.conv_a = m.sem("conv_a")
        self.conv_v = m.sem("conv_v")
        self.u_rdy = m.sem("u_rdy")
        self.xp_rdy = m.sem("xp_rdy")
        self.dts_rdy = m.sem("dts_rdy")
        self.bc_split = m.sem("bc_split")
        self.dtz_rdy = m.sem("dtz_rdy")
        self.ar_rdy = m.sem("ar_rdy")
        self.e_rdy = m.sem("e_rdy")
        self.t_rdy = m.sem("t_rdy")
        self.q_rdy = m.sem("q_rdy")
        self.ln_rdy = m.sem("ln_rdy")
        self.d_step = m.sem("d_step")
        self.bc_rdy = m.sem("bc_rdy")
        self.bc_evac = m.sem("bc_evac")
        self.exp_rdy = m.sem("exp_rdy")
        self.bu_done = m.sem("bu_done")
        self.scan_done = m.sem("scan_done")
        self.prod_done = m.sem("prod_done")
        self.pair_done = m.sem("pair_done")
        self.sum_done = m.sem("sum_done")
        self.y_init = m.sem("y_init")
        self.y_out = m.sem("y_out")
        self.y_dram = m.sem("y_dram")

    NLOAD = 11 * 16

    def load(self, sp):
        d, l = self.d, self.l
        for dst, src in [(self.ident[:], d["ident"]), (self.sel[:], d["sel"]),
                         (self.w_in[:], d[f"w_in{l}"].rearrange("(k p) n -> p k n", p=P)),
                         (self.w_x[:], d[f"w_x{l}"].rearrange("(k p) n -> p k n", p=P)),
                         (self.w_up[96:96 + DR, :], d[f"w_up{l}"]),
                         (self.cw[:], d[f"cw{l}"].rearrange("(k p) n -> p k n", p=P)),
                         (self.cb[:], d[f"cb{l}"]), (self.db[:], d[f"db{l}"]), (self.Dv[:], d[f"D{l}"]),
                         (self.alog[:], d[f"alog{l}"].rearrange("(k p) n -> p k n", p=P))]:
            sp.dma_start(dst, src).then_inc(self.loaded, 16)

    def load_ctx(self, sp, b):
        if b:
            sp.wait_ge(self.in_rdy, KC * b)
        sp.dma_start(self.cx[:], self.d["ctxT"].rearrange("(k p) n -> p k n", p=P)[:, :, b * L:(b + 1) * L])\
          .then_inc(self.cx_in, 16)

    def store_y(self, sp, y_ssm, b):
        sp.wait_ge(self.y_out, 2 * b + 2)
        sp.dma_start(y_ssm[b * L:(b + 1) * L, :].rearrange("(k p) n -> p k n", p=P),
                     self.U[:, b % self.dbl, :, :]).then_inc(self.y_dram, 16)

    def pe_start(self, pe):
        pe.sem_inc(self.sum_done, 1)
        pe.wait_ge(self.loaded, 160)

    def pe_in(self, pe, b, c):
        nc, g = self.nc, b * KC + c
        pe.wait_ge(self.cx_in, 16 * (b + 1))
        if c >= 2:
            pe.wait_ge(self.conv_v, 3 * (g - 1))
        elif b:
            pe.wait_ge(self.ar_rdy, b * KC)
            if self.alias:
                pe.wait_ge(self.bc_evac, b * STEPS + self.nb)
        for k in range(2):
            mm = nc.tensor.matmul(self.pw[c % 2][:], self.w_in[:, k, c * P:(c + 1) * P], self.cx[:, k, :],
                                  start=(k == 0), stop=(k == 1))
        mm.then_inc(self.in_rdy, 1)

    def pe_x(self, pe, b):
        pe.wait_ge(self.u_rdy, b + 1)
        for c in range(KC):
            mm = self.nc.tensor.matmul(self.pw[0][0:96 + DR, :], self.w_x[:, c, :], self.U[:, b % self.dbl, c, :],
                                       start=(c == 0), stop=(c == KC - 1))
        mm.then_inc(self.xp_rdy, 1)

    def pe_dt(self, pe, b, c):
        pe.wait_ge(self.dts_rdy, b + 1)
        if c == 1:
            pe.wait_ge(self.bc_split, 5 * (b + 1))
        if c >= 2:
            pe.wait_ge(self.ar_rdy, b * KC + c - 1)
        self.nc.tensor.matmul(self.pw[(c + 1) % 2][:], self.w_up[96:96 + DR, c * P:(c + 1) * P],
                              self.low[96:96 + DR, :], start=True, stop=True).then_inc(self.dtz_rdy, 1)

    def pe_spread(self, pe, b, s, n, j):
        nc = self.nc
        pe.wait_ge(self.bc_evac, s + 1)
        nc.tensor.matmul(self.pB[j % self.nb][:], self.sel[:, ds(n, 1), :], self.bc3[:, b % self.dbl, :],
                         start=True, stop=True)
        nc.tensor.matmul(self.pC[j % self.nb][:], self.sel[:, ds(n + NS, 1), :], self.bc3[:, b % self.dbl, :],
                         start=True, stop=True).then_inc(self.bc_rdy, 1)

    def pe_y_init(self, pe, b, half):
        if 2 * b + half - self.ny >= 0:
            pe.wait_ge(self.y_out, 2 * b + half + 1 - self.ny)
        for k in range(HC):
            mm = self.nc.tensor.matmul(self.pY[half % self.ny][k][:], self.diagD[:, half * HC + k, :],
                                       self.U[:, b % self.dbl, half * HC + k, :],
                                       start=True, stop=False, skip_group_check=True)
        mm.then_inc(self.y_init, 1)

    def pe_sum(self, pe, half, p, par, last=False):
        pe.wait_ge(self.pair_done, p + 3)
        for k in range(HC):
            mm = self.nc.tensor.matmul(self.pY[half % self.ny][k][:], self.ident[:], self.pair[:, par, k, :],
                                       start=False, stop=last, skip_group_check=True)
        mm.then_inc(self.sum_done, 1)

    def act_start(self, act):
        nc = self.nc
        act.wait_ge(self.loaded, 160)
        nc.scalar.activation(self.alog[:], self.alog[:], ACT.Exp).then_inc(self.a_exp, 1)
        act.wait_ge(self.a_exp, 1)
        nc.scalar.activation(self.A[:], self.alog[:], ACT.Copy, scale=-1.0).then_inc(self.a_neg, 1)
        act.sem_inc(self.bc_evac, self.nb)
        act.wait_ge(self.a_neg, 1)
        act.wait_ge(self.diag_rdy, KC + 1)

    def act_conv(self, act, b, c):
        act.wait_ge(self.in_rdy, b * KC + c + 1)
        if b:
            act.wait_ge(self.d_step, 3 * b)
            if self.alias:
                act.wait_ge(self.pair_done, b * STEPS // 2 + 2)
        self.nc.scalar.activation(self.acc[:, c, :], self.pw[c % 2][:], ACT.Identity,
                                  bias=self.cb[:, c:c + 1], scale=self.cw[:, c, DC - 1:DC]).then_inc(self.conv_a, 1)

    def act_u(self, act, b):
        act.wait_ge(self.conv_v, 3 * KC * (b + 1))
        if b >= self.dbl:
            act.wait_ge(self.y_dram, 16 * (b - self.dbl + 1))
        self.nc.scalar.activation(self.U[:, b % self.dbl, :, :], self.acc, ACT.Silu).then_inc(self.u_rdy, 1)

    def act_dt(self, act, b):
        act.wait_ge(self.xp_rdy, b + 1)
        self.nc.scalar.copy(self.low[96:96 + DR, :], self.pw[0][96:96 + DR, :]).then_inc(self.dts_rdy, 1)

    def act_z(self, act, b, c):
        nc = self.nc
        act.wait_ge(self.u_rdy, b + 1)
        act.wait_ge(self.dtz_rdy, b * KC + c + 1)
        nc.scalar.activation(self.acc[:, c, :], self.pw[(c + 1) % 2][:], ACT.Abs, bias=self.db[:, c:c + 1])
        nc.scalar.activation(self.dlt[:, b % self.dbl, c, :], self.pw[(c + 1) % 2][:], ACT.Relu,
                             bias=self.db[:, c:c + 1]).then_inc(self.ar_rdy, 1)

    def act_e(self, act, b):
        act.wait_ge(self.ar_rdy, (b + 1) * KC)
        self.nc.scalar.activation(self.acc, self.acc, ACT.Exp, scale=-1.0).then_inc(self.e_rdy, 1)

    def act_ln(self, act, b):
        act.wait_ge(self.q_rdy, b + 1)
        self.nc.scalar.activation(self.tmp, self.tmp, ACT.Ln, bias=1.0).then_inc(self.ln_rdy, 1)

    def act_step(self, act, b, half, s, n, j):
        nc, q = self.nc, j % self.ring
        act.wait_ge(self.bc_rdy, s + 1)
        act.wait_ge(self.bu_done, s + 1)
        nc.scalar.copy(self.Bs[:, q, :], self.pB[j % self.nb][:])
        act.wait_ge(self.prod_done, s + 1)
        nc.scalar.copy(self.Cs[:, j, :], self.pC[j % self.nb][:]).then_inc(self.bc_evac, 1)
        act.wait_ge(self.scan_done, s + 1)
        for k in range(HC):
            c = half * HC + k
            ex = nc.scalar.activation(self.dA[:, q, k, 1:L], self.dlt[:, b % self.dbl, c, 1:L], ACT.Exp,
                                      scale=self.A[:, c, ds(n, 1)])
        ex.then_inc(self.exp_rdy, 1)

    def act_y(self, act, b, half):
        act.wait_ge(self.sum_done, (2 * b + half + 1) * NS // 2 + 1)
        for k in range(HC):
            cp = self.nc.scalar.copy(self.U[:, b % self.dbl, half * HC + k, :], self.pY[half % self.ny][k][:])
        cp.then_inc(self.y_out, 1)

    def dve_start(self, dve):
        nc = self.nc
        dve.wait_ge(self.loaded, 160)
        for c in range(KC):
            nc.vector.tensor_scalar(self.diagD[:, c, :], self.ident[:], self.Dv[:, c:c + 1], None,
                                    ALU.mult).then_inc(self.diag_rdy, 1)
        nc.vector.memset(self.dA[:, :, :, 0:1], 0.0).then_inc(self.diag_rdy, 1)
        dve.sem_inc(self.bu_done, self.ring)
        dve.sem_inc(self.scan_done, self.ring)
        dve.sem_inc(self.pair_done, 2)

    def dve_conv(self, dve, b, c):
        g, acc, cw = b * KC + c, self.acc, self.cw
        dve.wait_ge(self.conv_a, g + 1)
        for t in range(1, DC):
            if t > 1:
                dve.wait_ge(self.conv_v, 3 * g + t - 1)
            self.nc.vector.scalar_tensor_tensor(
                out=acc[:, c, t:L], in0=self.pw[c % 2][:, 0:L - t], scalar=cw[:, c, DC - 1 - t:DC - t],
                in1=acc[:, c, t:L], op0=ALU.mult, op1=ALU.add).then_inc(self.conv_v, 1)

    def dve_split(self, dve, b):
        V, q, part, rest, ps = self.nc.vector, 5 * b, self.bc3[:, b % self.dbl, :], self.low[64:96, :], self.pw[0]
        dve.wait_ge(self.xp_rdy, b + 1)
        V.tensor_copy(part, ps[0:96, :]).then_inc(self.bc_split, 1)
        dve.wait_ge(self.bc_split, q + 1)
        V.tensor_tensor(rest, ps[64:96, :], part[64:96, :], ALU.subtract).then_inc(self.bc_split, 1)
        V.tensor_tensor(part[32:64, :], ps[32:64, :], part[32:64, :], ALU.subtract).then_inc(self.bc_split, 1)
        dve.wait_ge(self.bc_split, q + 3)
        V.tensor_copy(part[64:96, :], rest).then_inc(self.bc_split, 1)
        dve.wait_ge(self.bc_split, q + 4)
        V.tensor_tensor(part[64:96, :], rest, part[64:96, :], ALU.subtract).then_inc(self.bc_split, 1)

    def dve_t(self, dve, b):
        V = self.nc.vector
        dve.wait_ge(self.e_rdy, b + 1)
        V.tensor_scalar(self.tmp, self.acc, 1.0, -1.0, ALU.add, ALU.add).then_inc(self.t_rdy, 1)
        dve.wait_ge(self.t_rdy, b + 1)
        V.tensor_tensor(self.acc, self.acc, self.tmp, ALU.subtract).then_inc(self.q_rdy, 1)

    def dve_delta(self, dve, b):
        V, D_ = self.nc.vector, self.dlt[:, b % self.dbl, :, :]
        dve.wait_ge(self.q_rdy, b + 1)
        V.tensor_tensor(D_, D_, self.acc, ALU.add).then_inc(self.d_step, 1)
        dve.wait_ge(self.d_step, 3 * b + 1)
        dve.wait_ge(self.ln_rdy, b + 1)
        V.tensor_tensor(D_, D_, self.tmp, ALU.add).then_inc(self.d_step, 1)
        dve.wait_ge(self.d_step, 3 * b + 2)
        V.tensor_tensor(self.du[:, b % self.dbl, :, :], D_, self.U[:, b % self.dbl, :, :], ALU.mult)\
         .then_inc(self.d_step, 1)

    def dve_step(self, dve, b, half, s, p, j):
        nc, q = self.nc, j % self.ring
        dve.wait_ge(self.bc_evac, s + 1 + self.nb)
        dve.wait_ge(self.pair_done, p + 1)
        nc.vector.tensor_tensor(self.hs[:, j, :, :], self.du[:, b % self.dbl, half * HC:(half + 1) * HC, :],
                                self.Bs[:, q:q + 1, :].to_broadcast([P, HC, L]), ALU.mult).then_inc(self.bu_done, 1)
        dve.wait_ge(self.exp_rdy, s + 1)
        dve.wait_ge(self.bu_done, s + 1 + self.ring)
        flat = self.hs[:, j, :, :].rearrange("p k t -> p (k t)")
        nc.vector.tensor_tensor_scan(flat, self.dA[:, q, :, :].rearrange("p k t -> p (k t)"), flat,
                                     0.0, ALU.mult, ALU.add).then_inc(self.scan_done, 1)

    def dve_pair(self, dve, p, j):
        dve.wait_ge(self.prod_done, 2 * p + 2 + R)
        if not isinstance(p, int) or p:
            dve.wait_ge(self.sum_done, p)
        self.nc.vector.tensor_tensor(self.pair[:, j // 2, :, :], self.hs[:, j, :, :], self.hs[:, j + 1, :, :],
                                     ALU.add).then_inc(self.pair_done, 1)

    def pool_start(self, pool):
        pool.sem_inc(self.prod_done, R)

    def pool_step(self, pool, s, j):
        pool.wait_ge(self.scan_done, s + 1 + self.ring)
        pool.wait_ge(self.bc_evac, s + 1 + self.nb)
        self.nc.gpsimd.tensor_tensor(self.hs[:, j, :, :], self.hs[:, j, :, :],
                                     self.Cs[:, j:j + 1, :].to_broadcast([P, HC, L]), ALU.mult)\
            .then_inc(self.prod_done, 1)


def ssm_first(nc, d, y_ssm):
    with ExitStack() as ctx:
        m = Mem(nc, ctx, "ssm0")
        S = Ssm(nc, m, 0, d, dbl=2, nb=1, ny=2, ring=R, alias=False)
        NCH = 2 * B * STEPS // R
        CW = NEX * WE // NCH
        wst = m.sb("wst", [P, 2, CW])
        whi = m.sb("whi", [P, 2, CW], F16)
        wlo = m.sb("wlo", [P, 2, CW], F16)
        w_in = [m.sem(f"w_in{i}") for i in range(2)]
        hi_rdy = m.sem("hi_rdy")
        lo_rdy = m.sem("lo_rdy")
        w_out = [m.sem(f"w_out{i}") for i in range(2)]

        AT = 16

        with nc.Block() as block:

            @block.sync
            def _(sp):
                S.load(sp)
                S.load_ctx(sp, 0)

                def w_load(k, i):
                    sp.dma_start(wst[:, k, :], d["w_all"][:, ds(i * (2 * CW) + k * CW, CW)]).then_inc(w_in[k], 16)

                def w_store(k, i, n):
                    sp.wait_ge(lo_rdy, n)
                    sp.dma_start(d["w_hi"][:, ds(i * (2 * CW) + k * CW, CW)], whi[:, k, :]).then_inc(w_out[k], 16)
                    sp.dma_start(d["w_lo"][:, ds(i * (2 * CW) + k * CW, CW)], wlo[:, k, :]).then_inc(w_out[k], 16)

                PER = NCH // 2 // B
                for k in range(2):
                    w_load(k, 0)
                for b in range(B):
                    if b + 1 < B:
                        S.load_ctx(sp, b + 1)
                    if b:
                        S.store_y(sp, y_ssm, b - 1)
                    with sp.Fori(b * PER, (b + 1) * PER - (b == B - 1)) as i:
                        for k in range(2):
                            w_store(k, i, 2 * i + k + 1)
                            w_load(k, i + 1)
                for k in range(2):
                    w_store(k, NCH // 2 - 1, NCH - 1 + k)
                S.store_y(sp, y_ssm, B - 1)
                for k in range(2):
                    sp.wait_ge(w_out[k], 16 * NCH)
                sp.wait_ge(S.y_dram, 16 * B)

            @block.tensor
            def _(pe):
                S.pe_start(pe)

                def prologue(b, at):
                    if at == 0 or at == 3:
                        for c in range(2):
                            S.pe_in(pe, b, c + (2 if at else 0))
                    if at == 7:
                        S.pe_x(pe, b)
                    if at == 9 or at == 11:
                        for c in range(2):
                            S.pe_dt(pe, b, c + (2 if at == 11 else 0))

                def scan(b, half):
                    s0, p0 = b * STEPS + half * NS, (b * STEPS + half * NS) // 2
                    pe.wait_ge(S.bc_split, 5 * (b + 1))
                    S.pe_y_init(pe, b, half)
                    for n in range(R):
                        S.pe_spread(pe, b, s0 + n, n, n)
                        if (b or half) and n % 2:
                            S.pe_sum(pe, 1 - half, p0 + n // 2 - 2, n // 2, last=(n == 3))
                        if b + 1 < B:
                            prologue(b + 1, n + R * half)
                    if half:
                        for n in range(R, NS):
                            S.pe_spread(pe, b, s0 + n, n, n % R)
                            if n % 2:
                                S.pe_sum(pe, half, p0 + n // 2 - 2, n // 2 % 2)
                            if b + 1 < B:
                                prologue(b + 1, n + R)
                        return
                    with pe.Fori(1, NS // R) as i:
                        for j in range(R):
                            S.pe_spread(pe, b, R * i + (s0 + j), R * i + j, j)
                            if j % 2:
                                S.pe_sum(pe, half, (R // 2) * i + (p0 + j // 2 - 2), j // 2)

                for at in range(AT):
                    prologue(0, at)
                pe.wait_ge(S.diag_rdy, KC + 1)
                for b in range(B):
                    scan(b, 0)
                    scan(b, 1)
                for p in range(2):
                    S.pe_sum(pe, 1, B * STEPS // 2 - 2 + p, p, last=(p == 1))

            @block.scalar
            def _(act):
                S.act_start(act)

                def prologue(b, at):
                    for c in range(2):
                        if at == 1 or at == 4:
                            S.act_conv(act, b, c + (2 if at == 4 else 0))
                        if at == 10 or at == 12:
                            S.act_z(act, b, c + (2 if at == 12 else 0))
                    if at == 6:
                        S.act_u(act, b)
                    if at == 8:
                        S.act_dt(act, b)
                    if at == 12:
                        S.act_e(act, b)
                    if at == 14:
                        S.act_ln(act, b)

                def hi(k, i):
                    act.wait_ge(w_in[k], 16 * i + 16)
                    if not isinstance(i, int) or i:
                        act.wait_ge(w_out[k], 32 * i)
                    nc.scalar.activation(whi[:, k, :], wst[:, k, :], ACT.Copy, scale=WS)
                    nc.scalar.activation(wst[:, k, :], wst[:, k, :], ACT.Copy, scale=WS).then_inc(hi_rdy, 1)

                def scan(b, half):
                    s0 = b * STEPS + half * NS
                    act.wait_ge(S.d_step, 3 * (b + 1))
                    for n in range(R):
                        S.act_step(act, b, half, s0 + n, n, n)
                        if n == R - 1 and (b or half):
                            S.act_y(act, b - 1 + half, 1 - half)
                        if n % 2 == 0:
                            hi(n // 2, s0 // R)
                        if b + 1 < B:
                            prologue(b + 1, n + R * half)
                    if half:
                        for n in range(R, NS):
                            S.act_step(act, b, half, s0 + n, n, n % R)
                            if n % 2 == 0:
                                hi(n % R // 2, (s0 + n) // R)
                            if b + 1 < B:
                                prologue(b + 1, n + R)
                        return
                    with act.Fori(1, NS // R) as i:
                        for j in range(R):
                            S.act_step(act, b, half, R * i + (s0 + j), R * i + j, j)
                            if j % 2 == 0:
                                hi(j // 2, i + s0 // R)

                for at in range(AT):
                    prologue(0, at)
                for b in range(B):
                    scan(b, 0)
                    scan(b, 1)
                S.act_y(act, B - 1, 1)

            @block.vector
            def _(dve):
                S.dve_start(dve)

                def prologue(b, at):
                    if at == 2 or at == 5:
                        for c in range(2):
                            S.dve_conv(dve, b, c + (2 if at == 5 else 0))
                    if at == 8:
                        S.dve_split(dve, b)
                    if at == 13:
                        S.dve_t(dve, b)
                    if at == 15:
                        S.dve_delta(dve, b)

                def scan(b, half):
                    s0, p0 = b * STEPS + half * NS, (b * STEPS + half * NS) // 2
                    dve.wait_ge(S.d_step, 3 * (b + 1))
                    for n in range(R):
                        S.dve_step(dve, b, half, s0 + n, p0 + n // 2, n)
                        if n == 3 or (n == 1 and (b or half)):
                            S.dve_pair(dve, p0 + n // 2 - 1, (n + 1) % R)
                        if b + 1 < B:
                            prologue(b + 1, n + R * half)
                    if half:
                        for n in range(R, NS):
                            S.dve_step(dve, b, half, s0 + n, p0 + n // 2, n % R)
                            if n % 2:
                                S.dve_pair(dve, p0 + n // 2 - 1, (n + 1) % R)
                            if b + 1 < B:
                                prologue(b + 1, n + R)
                        return
                    with dve.Fori(1, NS // R) as i:
                        for j in range(R):
                            S.dve_step(dve, b, half, R * i + (s0 + j), (R // 2) * i + (p0 + j // 2), j)
                            if j % 2:
                                S.dve_pair(dve, (R // 2) * i + (p0 + j // 2 - 1), (j + 1) % R)

                for at in range(AT):
                    prologue(0, at)
                for b in range(B):
                    scan(b, 0)
                    scan(b, 1)
                S.dve_pair(dve, B * STEPS // 2 - 1, 2)

            @block.gpsimd
            def _(pool):
                S.pool_start(pool)

                def lo(k, n, i32):
                    pool.wait_ge(hi_rdy, n)
                    if i32 is not None:
                        pool.wait_ge(w_out[k], i32)
                    nc.gpsimd.tensor_tensor(wlo[:, k, :], wst[:, k, :], whi[:, k, :], ALU.subtract).then_inc(lo_rdy, 1)

                for n in range(R):
                    S.pool_step(pool, n, n)
                    if n % 2 == 0:
                        lo(n // 2, n // 2 + 1, None)
                with pool.Fori(1, B * STEPS // R) as i:
                    for j in range(R):
                        S.pool_step(pool, R * i + j, j)
                        if j % 2 == 0:
                            lo(j // 2, 2 * i + (j // 2 + 1), 32 * i)
        m.clear()


def gate(nc, l, d, X, y_ssm, r):
    with ExitStack() as ctx:
        m = Mem(nc, ctx, f"gate{l}")
        ident = m.sb("ident", [P, P])
        Y = m.sb("Y", [P, TT, L])
        xT = m.sb("xT", [P, 4, HK, P])
        st = m.sb("st", [P, 2, TT, 6])
        mv = m.sb("mv", [P, 2, TT, 2])
        sd = m.sb("sd", [P, 2, TT])
        rstd = m.sb("rstd", [P, 2, TT])
        nmr = m.sb("nmr", [P, 2, TT])
        eps = m.sb("eps", [P, 1])
        G = m.sb("G", [P, 4, L])
        xn = m.sb("xn", [P, 4, H])
        wr = m.sb("wr", [P, HK, E + 1])
        pt = [m.ps(f"pt{i}", [P, KC, P]) for i in range(4)]
        pn = [m.ps(f"pn{i}", [P, HK, P]) for i in range(2)]
        plog = m.ps("plog", [P, TT, 32])

        loaded = m.sem("loaded")
        x_in = [m.sem(f"x_in{i}") for i in range(B)]
        y_in = [m.sem(f"y_in{i}") for i in range(B)]
        eps_rdy = m.sem("eps_rdy")
        st_rdy = m.sem("st_rdy")
        mv_rdy = m.sem("mv_rdy")
        sd_rdy = m.sem("sd_rdy")
        rs_rdy = m.sem("rs_rdy")
        ln_rdy = m.sem("ln_rdy")
        g_rdy = m.sem("g_rdy")
        yg_rdy = m.sem("yg_rdy")
        tr_rdy = m.sem("tr_rdy")
        x_rdy = m.sem("x_rdy")
        xn_rdy = m.sem("xn_rdy")
        xn_out = [m.sem(f"xn_out{i}") for i in range(4)]
        tn_rdy = m.sem("tn_rdy")
        xT_rdy = m.sem("xT_rdy")
        lg_rdy = m.sem("lg_rdy")
        lg_out = m.sem("lg_out")

        with nc.Block() as block:

            @block.sync
            def _(sp):
                if l == 0:
                    for b in range(B):
                        own = slice(b * KC, (b + 1) * KC)
                        sp.dma_start(X[:, own, :], d["x"].rearrange("(i p) n -> p i n", p=P)[:, own, :]).then_inc(x_in[b], 16)
                sp.dma_start(ident[:], d["ident"]).then_inc(loaded, 16)
                if l == 0:
                    sp.dma_start(wr[:], d["w_router"].rearrange("(k p) n -> p k n", p=P)).then_inc(loaded, 16)
                    for i in range(TT):
                        sp.wait_ge(xn_rdy, i + 1)
                        sp.dma_start(r["xn_d"][i * P:(i + 1) * P, :], xn[:, i % 4, :]).then_inc(xn_out[i % 4], 16)
                    for q in range(4):
                        sp.wait_ge(xn_out[q], 16 * TT // 4)

            NLOAD = 32 if l == 0 else 16

            @block.vector
            def _(dve):
                nc.vector.memset(eps[:], EPS).then_inc(eps_rdy, 1)
                for i in range(TT):
                    if l == 0:
                        dve.wait_ge(x_in[i // KC], 16)
                    nc.vector.bn_stats(st[:, 0, i, :], X[:, i, :]).then_inc(st_rdy, 1)
                for i in range(TT):
                    dve.wait_ge(st_rdy, i + 1)
                    nc.vector.bn_aggr(mv[:, 0, i, :], st[:, 0, i, :]).then_inc(mv_rdy, 1)
                dve.wait_ge(sd_rdy, 1)
                nc.vector.reciprocal(rstd[:, 0, :], sd[:, 0, :]).then_inc(rs_rdy, 1)
                dve.wait_ge(rs_rdy, 1)
                nc.vector.scalar_tensor_tensor(out=nmr[:, 0, :], in0=mv[:, 0, :, 0], scalar=-1.0, in1=rstd[:, 0, :],
                                               op0=ALU.mult, op1=ALU.mult).then_inc(ln_rdy, 1)
                for b in range(B):
                    for c in range(KC):
                        i = b * KC + c
                        dve.wait_ge(tr_rdy, i + 1)
                        nc.vector.tensor_tensor(X[:, i, :], X[:, i, :], pt[i % 4][:].rearrange("p k t -> p (k t)"),
                                                ALU.add).then_inc(x_rdy, 1)
                    if l:
                        continue
                    own = slice(b * KC, (b + 1) * KC)
                    for c in range(KC):
                        i = b * KC + c
                        dve.wait_ge(x_rdy, i + 1)
                        nc.vector.bn_stats(st[:, 1, i, :], X[:, i, :]).then_inc(st_rdy, 1)
                    for c in range(KC):
                        i = b * KC + c
                        dve.wait_ge(st_rdy, TT + i + 1)
                        nc.vector.bn_aggr(mv[:, 1, i, :], st[:, 1, i, :]).then_inc(mv_rdy, 1)
                    dve.wait_ge(sd_rdy, b + 2)
                    nc.vector.reciprocal(rstd[:, 1, own], sd[:, 1, own]).then_inc(rs_rdy, 1)
                    dve.wait_ge(rs_rdy, b + 2)
                    nc.vector.scalar_tensor_tensor(out=nmr[:, 1, own], in0=mv[:, 1, own, 0], scalar=-1.0,
                                                   in1=rstd[:, 1, own], op0=ALU.mult, op1=ALU.mult).then_inc(ln_rdy, 1)
                    dve.wait_ge(ln_rdy, b + 2)
                    for c in range(KC):
                        i = b * KC + c
                        if i >= 4:
                            dve.wait_ge(xn_out[i % 4], 16 * (i // 4))
                            dve.wait_ge(tn_rdy, i - 3)
                        nc.vector.tensor_scalar(xn[:, i % 4, :], X[:, i, :], rstd[:, 1, i:i + 1], nmr[:, 1, i:i + 1],
                                                ALU.mult, ALU.add).then_inc(xn_rdy, 1)

            @block.scalar
            def _(act):
                for b in range(B):
                    own = slice(b * KC, (b + 1) * KC)
                    act.dma_start(Y[:, own, :], y_ssm.rearrange("(i p) t -> p i t", p=P)[:, own, :]).then_inc(y_in[b], 16)
                act.wait_ge(eps_rdy, 1)
                act.wait_ge(mv_rdy, TT)
                nc.scalar.activation(sd[:, 0, :], mv[:, 0, :, 1], ACT.Sqrt, bias=eps[:]).then_inc(sd_rdy, 1)
                act.wait_ge(ln_rdy, 1)

                def silus(b):
                    for c in range(KC):
                        i = b * KC + c
                        if i >= 4:
                            act.wait_ge(yg_rdy, i - 3)
                        nc.scalar.activation(G[:, i % 4, :], X[:, i, :], ACT.Silu, bias=nmr[:, 0, i:i + 1],
                                             scale=rstd[:, 0, i:i + 1]).then_inc(g_rdy, 1)

                def second(b):
                    own = slice(b * KC, (b + 1) * KC)
                    act.wait_ge(mv_rdy, TT + (b + 1) * KC)
                    nc.scalar.activation(sd[:, 1, own], mv[:, 1, own, 1], ACT.Sqrt, bias=eps[:]).then_inc(sd_rdy, 1)

                def evac(b):
                    for c in range(KC):
                        i = b * KC + c
                        act.wait_ge(tn_rdy, i + 1)
                        if i >= 4:
                            act.wait_ge(lg_rdy, i - 3)
                        nc.scalar.copy(xT[:, i % 4, :, :], pn[i % 2][:]).then_inc(xT_rdy, 1)

                silus(0)
                for b in range(B):
                    if b + 1 < B:
                        silus(b + 1)
                    if l == 0:
                        second(b)
                        evac(b)
                if l == 0:
                    act.wait_ge(lg_rdy, TT)
                    nc.scalar.copy(r["logit"][:], plog[:, :, 0:E + 1]).then_inc(lg_out, 1)

            @block.gpsimd
            def _(pool):
                for i in range(TT):
                    pool.wait_ge(y_in[i // KC], 16)
                    pool.wait_ge(g_rdy, i + 1)
                    nc.gpsimd.tensor_tensor(Y[:, i, :], Y[:, i, :], G[:, i % 4, :], ALU.mult).then_inc(yg_rdy, 1)

            @block.tensor
            def _(pe):
                pe.wait_ge(loaded, NLOAD)
                for b in range(B):
                    pe.wait_ge(yg_rdy, (b + 1) * KC)
                    for t in range(KC):
                        i = b * KC + t
                        if i >= 4:
                            pe.wait_ge(x_rdy, i - 3)
                        for c in range(KC):
                            tr = nc.tensor.transpose(pt[i % 4][:, c, :], Y[:, b * KC + c, t * P:(t + 1) * P], ident[:])
                        tr.then_inc(tr_rdy, 1)
                    if l:
                        continue
                    for t in range(KC):
                        i = b * KC + t
                        pe.wait_ge(xn_rdy, i + 1)
                        if i >= 2:
                            pe.wait_ge(xT_rdy, i - 1)
                        for k in range(HK):
                            tr = nc.tensor.transpose(pn[i % 2][:, k, :], xn[:, i % 4, k * P:(k + 1) * P], ident[:])
                        tr.then_inc(tn_rdy, 1)
                    for t in range(KC):
                        i = b * KC + t
                        pe.wait_ge(xT_rdy, i + 1)
                        for k in range(HK):
                            mm = nc.tensor.matmul(plog[:, i, 0:E + 1], xT[:, i % 4, k, :], wr[:, k, :],
                                                  start=(k == 0), stop=(k == HK - 1))
                        mm.then_inc(lg_rdy, 1)
        m.clear()


def routing(nc, d, r):
    with ExitStack() as ctx:
        m = Mem(nc, ctx, "rt")
        tri = m.sb("tri", [P, P])
        ones = m.sb("ones", [P, P])
        e_of = m.sb("e_of", [P, E])
        thr = m.sb("thr", [P, TT])
        col = m.sb("col", [P, P])
        tok = m.sb("tok", [P, TT])
        ex = m.sb("ex", [P, TT, E])
        mx = m.sb("mx", [P, TT])
        sm = m.sb("sm", [P, TT])
        ri = m.sb("ri", [P, TT])
        i8 = m.sb("i8", [P, TT, 8], U32)
        idf = m.sb("idf", [P, TT, 8])
        oh = m.sb("oh", [P, TOPK, TT, E])
        M = m.sb("M", [P, TT, E])
        base = m.sb("base", [P, TT, E])
        cnt = m.sb("cnt", [P, TT, E])
        off = m.sb("off", [P, TT + 1, E])
        cmp = m.sb("cmp", [P, E, TT])
        nt = m.sb("nt", [P, E])
        incl = m.sb("incl", [P, E])
        start = m.sb("start", [P, E])
        one_e = m.sb("one_e", [P, E])
        pos = m.sb("pos", [P, TT, TOPK])
        posi = m.sb("posi", [P, TT, TOPK], I32)
        sti = m.sb("sti", [P, TT, TOPK], I32)
        stf = m.sb("stf", [P, TT, TOPK])
        pp = m.sb("pp", [P, TT, TOPK])
        ohp = m.sb("ohp", [P, 4, P])
        ohs = m.sb("ohs", [P, 4, NSTEP])
        turn = m.sb("turn", [1, E])
        scm = m.sb("scm", [1, NSTEP, E])
        se = m.sb("se", [1, NSTEP + 1])
        ws = m.sb("ws", [1, NSTEP])
        pr_ = m.ps("pr", [P, TT * E])
        pc = m.ps("pc", [P, TT * E])
        pi = m.ps("pi", [P, NSTEP])

        loaded = m.sem("loaded")
        mx_rdy = m.sem("mx_rdy")
        e_rdy = m.sem("e_rdy")
        m_rdy = m.sem("m_rdy")
        rk_rdy = m.sem("rk_rdy")
        oh_rdy = m.sem("oh_rdy")
        oh_used = m.sem("oh_used")
        step = m.sem("step")
        fin = m.sem("fin")

        with nc.Block() as block:
            @block.sync
            def _(sp):
                for dst, n in [(tri, "tri"), (ones, "ones"), (e_of, "e_of"), (thr, "thr"), (col, "col"), (tok, "tok")]:
                    sp.dma_start(dst[:], d[n]).then_inc(loaded, 16)
                sp.dma_start(turn[:], d["turn"]).then_inc(loaded, 16)
                sp.dma_start(r["tab"][:], d["tab"]).then_inc(loaded, 16)

            @block.scalar
            def _(act):
                act.wait_ge(mx_rdy, 1)
                nc.scalar.activation(ex[:], ex[:], ACT.Exp).then_inc(e_rdy, 1)
                nc.scalar.activation(r["sig"][:], r["logit"][:, :, E], ACT.Sigmoid).then_inc(fin, 1)

            @block.vector
            def _(dve):
                n = [0]

                def own(ins):
                    ins.then_inc(step, 1)
                    n[0] += 1
                    dve.wait_ge(step, n[0])

                V = nc.vector
                logit = r["logit"][:, :, 0:E]
                dve.wait_ge(loaded, 128)
                own(V.reduce_max(mx[:], logit, AX.X))
                V.tensor_tensor(ex[:], logit, mx[:].unsqueeze(2).to_broadcast([P, TT, E]), ALU.subtract).then_inc(mx_rdy, 1)
                dve.wait_ge(e_rdy, 1)
                own(V.reduce_sum(sm[:], ex[:], AX.X))
                own(V.reciprocal(ri[:], sm[:]))
                own(V.tensor_tensor(ex[:], ex[:], ri[:].unsqueeze(2).to_broadcast([P, TT, E]), ALU.mult))
                for i in range(TT):
                    mxi = V.max(r["w8"][:, i, :], ex[:, i, :])
                own(mxi)
                for i in range(TT):
                    mxi = V.max_index(i8[:, i, :], r["w8"][:, i, :], ex[:, i, :])
                own(mxi)
                own(V.tensor_copy(idf[:], i8[:]))
                for k in range(TOPK):
                    q = V.tensor_tensor(oh[:, k, :, :], e_of[:].unsqueeze(1).to_broadcast([P, TT, E]),
                                        idf[:, :, k:k + 1].to_broadcast([P, TT, E]), ALU.is_equal)
                own(q)
                own(V.tensor_tensor(M[:], oh[:, 0, :, :], oh[:, 1, :, :], ALU.add))
                own(V.tensor_tensor(M[:], M[:], oh[:, 2, :, :], ALU.add))
                own(V.tensor_tensor(M[:], M[:], oh[:, 3, :, :], ALU.add))
                V.memset(one_e[:], 1.0).then_inc(m_rdy, 1)
                own(V.memset(off[:, 0, :], 0.0))
                dve.wait_ge(rk_rdy, 2)
                own(V.tensor_copy(cnt[:].rearrange("p t e -> p (t e)"), pc[:]))
                for i in range(TT):
                    own(V.tensor_tensor(off[:, i + 1, :], off[:, i, :], cnt[:, i, :], ALU.add))
                own(V.tensor_tensor(cmp[:], off[:, TT, :].unsqueeze(2).to_broadcast([P, E, TT]),
                                    thr[:].unsqueeze(1).to_broadcast([P, E, TT]), ALU.is_gt))
                own(V.reduce_sum(nt[:], cmp[:], AX.X))
                own(V.tensor_scalar(nt[:], nt[:], 1.0, None, ALU.max))
                own(V.tensor_tensor_scan(incl[:], one_e[:], nt[:], 0.0, ALU.mult, ALU.add))
                own(V.tensor_tensor(start[:], incl[:], nt[:], ALU.subtract))
                own(V.scalar_tensor_tensor(out=base[:], in0=start[:].unsqueeze(1).to_broadcast([P, TT, E]), scalar=float(P),
                                           in1=off[:, 0:TT, :], op0=ALU.mult, op1=ALU.add))
                own(V.tensor_tensor(base[:], base[:], pr_[:].rearrange("p (t e) -> p t e", e=E), ALU.add))
                for k in range(TOPK):
                    q = V.tensor_tensor(oh[:, k, :, :], oh[:, k, :, :], base[:], ALU.mult)
                own(q)
                for k in range(TOPK):
                    q = V.reduce_sum(pos[:, :, k], oh[:, k, :, :], AX.X)
                own(q)
                V.tensor_copy(r["pos"][:], pos[:])
                own(V.tensor_copy(posi[:], pos[:]))
                own(V.tensor_scalar(sti[:], posi[:], 7, None, ALU.arith_shift_right))
                own(V.tensor_scalar(posi[:], posi[:], P - 1, None, ALU.bitwise_and))
                V.tensor_copy(stf[:], sti[:])
                own(V.tensor_copy(pp[:], posi[:]))
                for g in range(TT * TOPK):
                    i, k = g // TOPK, g % TOPK
                    if g >= 4:
                        dve.wait_ge(oh_used, g - 3)
                    V.tensor_scalar(ohp[:, g % 4, :], col[:], pp[:, i, k:k + 1], None, ALU.is_equal)
                    V.tensor_scalar(ohs[:, g % 4, :], col[:, 0:NSTEP], stf[:, i, k:k + 1], tok[:, i:i + 1],
                                    ALU.is_equal, ALU.mult).then_inc(oh_rdy, 1)
                own(V.tensor_tensor(scm[:], start[0:1, :].unsqueeze(1).to_broadcast([1, NSTEP, E]),
                                    col[0:1, 0:NSTEP].unsqueeze(2).to_broadcast([1, NSTEP, E]), ALU.is_le))
                own(V.memset(se[:], -1.0))
                own(V.reduce_sum(se[0:1, 1:NSTEP + 1], scm[:], AX.X))
                own(V.tensor_scalar(se[0:1, 1:NSTEP + 1], se[0:1, 1:NSTEP + 1], -1.0, None, ALU.add))
                V.tensor_tensor(r["tab"][0:1, 1, NA:NALL], se[0:1, 1:NSTEP + 1], se[0:1, 0:NSTEP], ALU.subtract)
                V.tensor_copy(r["tab"][0:1, 0, NA:NALL], se[0:1, 1:NSTEP + 1])
                own(V.tensor_tensor(scm[:], scm[:], turn[:].unsqueeze(1).to_broadcast([1, NSTEP, E]), ALU.mult))
                own(V.reduce_sum(ws[:], scm[:], AX.X))
                own(V.tensor_copy(r["tab"][0:1, 2, NA:NALL], ws[:]))
                for q in range(NSH):
                    V.tensor_copy(r["idx"][:, q * TT:(q + 1) * TT], tok[:])
                dve.wait_ge(oh_used, TT * TOPK)
                own(V.tensor_copy(r["idx"][:, NA:NALL], pi[:]))

            @block.tensor
            def _(pe):
                pe.wait_ge(loaded, 128)
                pe.wait_ge(m_rdy, 1)
                Mf = M[:].rearrange("p t e -> p (t e)")
                nc.tensor.matmul(pr_[:], tri[:], Mf, start=True, stop=True).then_inc(rk_rdy, 1)
                nc.tensor.matmul(pc[:], ones[:], Mf, start=True, stop=True).then_inc(rk_rdy, 1)
                G = TT * TOPK
                for g in range(G):
                    pe.wait_ge(oh_rdy, g + 1)
                    nc.tensor.matmul(pi[:], ohp[:, g % 4, :], ohs[:, g % 4, :], start=(g == 0),
                                     stop=(g == G - 1)).then_inc(oh_used, 1)


def experts_and_ssm(nc, d, r, X, y_ssm):
    with ExitStack() as ctx:
        m = Mem(nc, ctx, "moe")
        S = Ssm(nc, m, 1, d, dbl=1, nb=1, ny=1, ring=2, alias=True)
        ident = S.ident
        Wh = m.sb("Wh", [P, WR, WE], F16)
        Wl = m.sb("Wl", [P, WR, WE], F16)
        xg = m.sb("xg", [P, 2, H])
        ist = m.sb("ist", [P, 2], U32)
        xth = m.sb("xth", [P, HK, P], F16)
        xtl = m.sb("xtl", [P, HK, P], F16)
        sg = m.sb("sg", [P, IE])
        hh = m.sb("hh", [P, IE])
        hth = m.sb("hth", [P, 3, P], F16)
        htl = m.sb("htl", [P, 3, P], F16)
        yo = m.sb("yo", [P, 2, H])
        sigs = m.sb("sigs", [P, TT])
        pt = m.ps("pt", [P, HK, P])
        pg = m.ps("pg", [P, IE])
        pu = m.ps("pu", [P, IE])
        py = m.ps("py", [P, H])

        wa = [m.sem(f"wa{i}") for i in range(WR)]
        wb = [m.sem(f"wb{i}") for i in range(2)]
        w_free = m.sem("w_free")
        xg_in = [m.sem(f"xg_in{i}") for i in range(2)]
        ix_rdy = m.sem("ix_rdy")
        ix_seen = m.sem("ix_seen")
        tx_rdy = m.sem("tx_rdy")
        xh_rdy = m.sem("xh_rdy")
        xl_rdy = m.sem("xl_rdy")
        gu_rdy = m.sem("gu_rdy")
        sg_rdy = m.sem("sg_rdy")
        gt_rdy = m.sem("gt_rdy")
        hh_rdy = m.sem("hh_rdy")
        th_rdy = m.sem("th_rdy")
        hth_rdy = m.sem("hth_rdy")
        htl_rdy = m.sem("htl_rdy")
        y_rdy = m.sem("y_rdy")
        py_read = m.sem("py_read")
        y_st = [m.sem(f"y_st{i}") for i in range(2)]
        sg_scl = m.sem("sg_scl")

        PRO = 4
        PER = PRO + STEPS
        assert B * PER == NALL

        def halves(eng, one, b, h):
            g0, s0 = b * PER + PRO + h * NS, b * STEPS + h * NS
            change = g0 + R - 2 < NA <= g0 + NS - 3
            for n in range(NS if change else R):
                one(h, g0 + n, (g0 + n) // 2, s0 + n, (s0 + n) // 2, n, n % R, g0 + n - 2 >= NA)
            if change:
                return
            with eng.Fori(1, NS // R) as i:
                for j in range(R):
                    one(h, R * i + (g0 + j), (R // 2) * i + (g0 + j) // 2, R * i + (s0 + j),
                        (R // 2) * i + (s0 + j) // 2, R * i + j, j, g0 + R - 2 >= NA)

        with nc.Block() as block:

            @block.sync
            def _(sp):
                S.load(sp)
                S.load_ctx(sp, 0)

                def w_load(slot, e, sem):
                    for W, src in ((Wh, d["w_hi"]), (Wl, d["w_lo"])):
                        sp.dma_start(W[:, ds(slot, 1), :].rearrange("p o n -> p (o n)"), src[:, ds(e * WE, WE)])\
                          .then_inc(sem, 16)

                def step(s, j):
                    e = sp.value_load(r["tab"][0:1, 0, ds(s + NA, 1)], min_val=0, max_val=E - 1)
                    f = sp.value_load(r["tab"][0:1, 1, ds(s + NA, 1)], min_val=0, max_val=1)
                    w = sp.value_load(r["tab"][0:1, 2, ds(s + NA, 1)], min_val=0, max_val=WR - 1)
                    with sp.If(f == 1):
                        w_load(w, e, wb[j])
                    with sp.Else():
                        sp.sem_inc(wb[j], 32)

                for q in range(WR):
                    w_load(q, E + q, wa[q])
                sp.wait_ge(y_rdy, TT)
                w_load(0, E + WR, wa[0])
                for s in range(2):
                    sp.wait_ge(y_rdy, (s + 2) * TT)
                    step(s, s)
                with sp.Fori(1, NSTEP // 2) as i:
                    for j in range(2):
                        sp.wait_ge(y_rdy, 2 * i + (j + NA - WR + 1))
                        sp.sem_inc(w_free, 1)
                        sp.wait_ge(wb[j], 32 * i)
                        sp.sem_inc(w_free, 1)
                        step(2 * i + j, j)
                for j in range(2):
                    sp.wait_ge(wb[j], 32 * NSTEP // 2)
                sp.wait_ge(S.y_dram, 16 * B)

            @block.gpsimd
            def _(pool):
                S.pool_start(pool)

                def fetch(g, j):
                    nc.gpsimd.tensor_copy(ist[:, j:j + 1], r["idx"][:, ds(g, 1)]).then_inc(ix_rdy, 1)
                    pool.wait_ge(ix_rdy, g + 1)
                    pool.sem_inc(ix_seen, 1)
                    nc.gpsimd.indirect_dma_start(
                        out=xg[:, j, :], out_offset=None, in_=r["xn_d"],
                        in_offset=bass.IndirectOffsetOnAxis(ap=ist[:, j:j + 1], axis=0)).then_inc(xg_in[j], 16)

                def ahead(g, j):
                    pool.wait_ge(tx_rdy, g + 1)
                    fetch(g + 2, j)

                def one(h, g, g2, s, p, n, j, routed):
                    if not isinstance(g, int) or g + 2 < NALL:
                        ahead(g, j % 2)
                    S.pool_step(pool, s, j)

                for g in range(2):
                    fetch(g, g)
                for b in range(B):
                    for g in range(b * PER, b * PER + PRO):
                        ahead(g, g % 2)
                    halves(pool, one, b, 0)
                    if b + 1 < B:
                        halves(pool, one, b, 1)
                g0, s0 = NALL - NS, B * STEPS - NS
                for n in range(NS):
                    one(1, g0 + n, None, s0 + n, None, n, n % R, True)

            @block.tensor
            def _(pe):
                def w_of(W, w, k, o, n):
                    return W[0:k, ds(w, 1), o:o + n].rearrange("p o n -> p (o n)")

                def slot_of(g):
                    return pe.value_load(r["tab"][0:1, 2, ds(g, 1)], min_val=0, max_val=WR - 1)

                def x_transpose(g, g2, j):
                    pe.wait_ge(xg_in[j], 16 * g2 + 16)
                    if not isinstance(g, int) or g >= 2:
                        pe.wait_ge(htl_rdy, g - 1)
                    for k in range(HK):
                        tr = nc.tensor.transpose(pt[:, k, :], xg[:, j, k * P:(k + 1) * P], ident[:])
                    tr.then_inc(tx_rdy, 1)

                def down(g):
                    w, o = slot_of(g), HK * 2 * IE
                    pe.wait_ge(htl_rdy, g + 1)
                    if not isinstance(g, int) or g:
                        pe.wait_ge(py_read, g)
                    for q, (_, n) in enumerate(ICH):
                        for z, (ht, W) in enumerate(((hth, Wh), (hth, Wl), (htl, Wh))):
                            mm = nc.tensor.matmul(py[:], ht[0:n, q, :], w_of(W, w, n, o + q * H, H),
                                                  start=(q == 0 and z == 0), stop=(q == 2 and z == 2))
                    mm.then_inc(y_rdy, 1)

                def h_transpose(g):
                    pe.wait_ge(hh_rdy, g + 1)
                    if not isinstance(g, int) or g + 1 < NALL:
                        pe.wait_ge(xl_rdy, g + 2)
                    for q, (o, n) in enumerate(ICH):
                        tr = nc.tensor.transpose(pt[0:n, q, :], hh[:, o:o + n], ident[:])
                    tr.then_inc(th_rdy, 1)

                def up(g, g2, j, routed):
                    w = slot_of(g)
                    pe.wait_ge(xl_rdy, g + 1)
                    if routed:
                        pe.wait_ge(wb[j], 32 * g2 - (32 * (NA // 2) - 32))
                    for k in range(HK):
                        for xt, W, z in ((xth, Wh, 0), (xth, Wl, 1), (xtl, Wh, 2)):
                            for ps, o in ((pg, 0), (pu, IE)):
                                mm = nc.tensor.matmul(ps[:], xt[:, k, :], w_of(W, w, P, k * 2 * IE + o, IE),
                                                      start=(k == 0 and z == 0), stop=(k == HK - 1 and z == 2))
                    mm.then_inc(gu_rdy, 1)

                def shared_weights(g):
                    for q in range(NSH):
                        if g <= q * TT < g + NS:
                            pe.wait_ge(wa[q % WR], 32 * (q // WR) + 32)

                def first(g, g2, j):
                    x_transpose(g, g2, j)
                    if not isinstance(g, int) or g >= 2:
                        down(g - 2)

                def second(g, g2, j, routed):
                    if not isinstance(g, int) or g >= 1:
                        h_transpose(g - 1)
                    up(g, g2, j, g >= NA if isinstance(g, int) else routed)

                S.pe_start(pe)
                pe.wait_ge(S.diag_rdy, KC + 1)
                for b in range(B):
                    shared_weights(b * PER)
                    for at in range(PRO):
                        g = b * PER + at
                        first(g, g // 2, g % 2)
                        if at == 0:
                            if b:
                                for p in range(2):
                                    S.pe_sum(pe, 1, b * STEPS // 2 - 2 + p, p, last=(p == 1))
                            S.pe_in(pe, b, 0)
                            S.pe_in(pe, b, 1)
                        if at == 2:
                            S.pe_x(pe, b)
                        if at == 3:
                            S.pe_dt(pe, b, 0)
                            S.pe_dt(pe, b, 1)
                        second(g, g // 2, g % 2, None)
                        if at == 0:
                            S.pe_in(pe, b, 2)
                            S.pe_in(pe, b, 3)
                        if at == 3:
                            S.pe_dt(pe, b, 2)
                            S.pe_dt(pe, b, 3)

                    def one(h, g, g2, s, p, n, j, routed):
                        first(g, g2, j % 2)
                        if isinstance(n, int) and s == b * STEPS:
                            pe.wait_ge(S.ar_rdy, (b + 1) * KC)
                            S.pe_y_init(pe, b, 0)
                        S.pe_spread(pe, b, s, n, j)
                        if j % 2:
                            if not isinstance(n, int) or n >= R:
                                S.pe_sum(pe, 0, p - 2, j // 2)
                            elif s >= b * STEPS + NS:
                                S.pe_sum(pe, 0, p - 2, j // 2, last=(n == 3))
                        second(g, g2, j % 2, routed)
                        if isinstance(n, int) and s == b * STEPS + NS + R - 1:
                            S.pe_y_init(pe, b, 1)

                    for h in range(2):
                        shared_weights(b * PER + PRO + h * NS)
                        halves(pe, one, b, h)
                down(NALL - 2)
                h_transpose(NALL - 1)
                for p in range(2):
                    S.pe_sum(pe, 1, B * STEPS // 2 - 2 + p, p, last=(p == 1))
                down(NALL - 1)

            @block.scalar
            def _(act):
                def x_hi(g):
                    act.wait_ge(tx_rdy, g + 1)
                    nc.scalar.activation(xth[:], pt[:], ACT.Copy, scale=XS).then_inc(xh_rdy, 1)

                def h_hi(g):
                    act.wait_ge(th_rdy, g + 1)
                    nc.scalar.copy(hth[:, 0:2, :], pt[:, 0:2, :])
                    nc.scalar.copy(hth[0:96, 2, :], pt[0:96, 2, :]).then_inc(hth_rdy, 1)

                def silu(g):
                    act.wait_ge(gu_rdy, g + 1)
                    nc.scalar.activation(sg[:], pg[:], ACT.Tanh, scale=0.5 / (XS * WS)).then_inc(sg_rdy, 1)

                def y_store(g, j):
                    act.wait_ge(py_read, g + 1)
                    act.dma_start(r["y_d"][ds(g * P - NA * P, P), :], yo[:, j, :]).then_inc(y_st[j], 16)

                def late(g, j, routed):
                    if not isinstance(g, int) or g >= 1:
                        h_hi(g - 1)
                    silu(g)
                    if routed:
                        y_store(g - 2, j)

                S.act_start(act)
                for b in range(B):
                    for at in range(PRO):
                        g = b * PER + at
                        x_hi(g)
                        if at == 0:
                            if b:
                                S.act_y(act, b - 1, 1)
                                S.store_y(act, y_ssm, b - 1)
                            S.act_conv(act, b, 0)
                            S.act_conv(act, b, 1)
                        if at == 1:
                            S.act_conv(act, b, 2)
                            S.act_conv(act, b, 3)
                            if b + 1 < B:
                                S.load_ctx(act, b + 1)
                        if at == 3:
                            S.act_z(act, b, 0)
                            S.act_z(act, b, 1)
                        late(g, g % 2, g - 2 >= NA)
                        if at == 1:
                            S.act_u(act, b)
                        if at == 2:
                            S.act_dt(act, b)
                        if at == 3:
                            S.act_z(act, b, 2)
                            S.act_z(act, b, 3)
                            S.act_e(act, b)
                            S.act_ln(act, b)

                    def one(h, g, g2, s, p, n, j, routed):
                        x_hi(g)
                        if isinstance(n, int) and s == b * STEPS:
                            act.wait_ge(S.d_step, 3 * (b + 1))
                        S.act_step(act, b, h, s, n, j)
                        if isinstance(n, int) and s == b * STEPS + NS + R - 1:
                            S.act_y(act, b, 0)
                        late(g, j % 2, routed)

                    halves(act, one, b, 0)
                    halves(act, one, b, 1)
                h_hi(NALL - 1)
                for j in range(2):
                    y_store(NALL - 2 + j, j)
                S.act_y(act, B - 1, 1)
                S.store_y(act, y_ssm, B - 1)
                for j in range(2):
                    act.wait_ge(y_st[j], 16 * NSTEP // 2)

            @block.vector
            def _(dve):
                def x_lo(g):
                    dve.wait_ge(xh_rdy, g + 1)
                    nc.vector.scalar_tensor_tensor(out=xtl[:], in0=pt[:], scalar=XS, in1=xth[:],
                                                   op0=ALU.mult, op1=ALU.subtract).then_inc(xl_rdy, 1)

                def h_lo(g):
                    dve.wait_ge(hth_rdy, g + 1)
                    nc.vector.tensor_tensor(htl[:, 0:2, :], pt[:, 0:2, :], hth[:, 0:2, :], ALU.subtract)
                    nc.vector.tensor_tensor(htl[0:96, 2, :], pt[0:96, 2, :], hth[0:96, 2, :], ALU.subtract)\
                      .then_inc(htl_rdy, 1)

                def silu_up(g):
                    dve.wait_ge(sg_rdy, g + 1)
                    nc.vector.scalar_tensor_tensor(out=sg[:], in0=sg[:], scalar=1.0, in1=pg[:],
                                                   op0=ALU.add, op1=ALU.mult).then_inc(gt_rdy, 1)
                    dve.wait_ge(gt_rdy, g + 1)
                    nc.vector.scalar_tensor_tensor(out=hh[:], in0=pu[:], scalar=0.5 * HS / (XS * WS) ** 2, in1=sg[:],
                                                   op0=ALU.mult, op1=ALU.mult).then_inc(hh_rdy, 1)

                def y(g, g2, j, routed):
                    if not routed:
                        t = dve.value_load(r["tab"][0:1, 3, ds(g, 1)], min_val=0, max_val=TT - 1)
                    dve.wait_ge(y_rdy, g + 1)
                    if routed:
                        if not isinstance(g, int) or g >= NA + 2:
                            dve.wait_ge(y_st[j], 16 * g2 - 16 * (NA // 2))
                        nc.vector.tensor_scalar(yo[:, j, :], py[:], 1.0 / (HS * WS), None, ALU.mult).then_inc(py_read, 1)
                        return
                    if not isinstance(g, int) or g:
                        dve.wait_ge(py_read, g)
                    xs = X[:, ds(t, 1), :].rearrange("p o n -> p (o n)")
                    nc.vector.scalar_tensor_tensor(out=xs, in0=py[:], scalar=sigs[:, ds(t, 1)], in1=xs,
                                                   op0=ALU.mult, op1=ALU.add).then_inc(py_read, 1)

                def early(g, g2, j, routed):
                    x_lo(g)
                    if not isinstance(g, int) or g >= 2:
                        y(g - 2, g2 - 1, j, routed)

                nc.vector.tensor_scalar(sigs[:], r["sig"][:], 1.0 / (HS * WS), None, ALU.mult).then_inc(sg_scl, 1)
                S.dve_start(dve)
                dve.wait_ge(sg_scl, 1)
                for b in range(B):
                    for at in range(PRO):
                        g = b * PER + at
                        if at == 0 and b:
                            S.dve_pair(dve, b * STEPS // 2 - 1, 2)
                        early(g, g // 2, g % 2, g - 2 >= NA)
                        if at == 0:
                            S.dve_conv(dve, b, 0)
                            S.dve_conv(dve, b, 1)
                        if at == 1:
                            S.dve_conv(dve, b, 2)
                            S.dve_conv(dve, b, 3)
                        if g:
                            h_lo(g - 1)
                        silu_up(g)
                        if at == 2:
                            S.dve_split(dve, b)
                        if at == 3:
                            S.dve_t(dve, b)
                            S.dve_delta(dve, b)

                    def one(half, g, g2, s, p, n, j, routed):
                        early(g, g2, j % 2, routed)
                        S.dve_step(dve, b, half, s, p, j)
                        h_lo(g - 1)
                        if j == 3 or (j == 1 and not (isinstance(n, int) and s == b * STEPS + 1)):
                            S.dve_pair(dve, p - 1, (j + 1) % R)
                        silu_up(g)

                    halves(dve, one, b, 0)
                    halves(dve, one, b, 1)
                for j in range(2):
                    g = NALL - 2 + j
                    if j:
                        h_lo(g)
                        S.dve_pair(dve, B * STEPS // 2 - 1, 2)
                    y(g, g // 2, j, True)
        m.clear()


def combine(nc, d, r, X, Wq, wsc):
    with ExitStack() as ctx:
        m = Mem(nc, ctx, "comb")
        NR = 8
        NP = 3 * 4
        yr = m.sb("yr", [P, NR, H])
        W = m.sb("W", [P, NP, IF])
        neg = m.sb("neg", [P, 2, IF], BF16)
        ones = m.sb("ones", [P, P])
        wsum = m.sb("wsum", [P, 3, 4])
        wtot = m.sb("wtot", [P, 3])
        whi = m.sb("whi", [P, 3])
        wlo = m.sb("wlo", [P, 3])
        pa = m.ps("pa", [P, 4])

        got = [m.sem(f"got{i}") for i in range(NR)]
        used = m.sem("used")
        w_in = [m.sem(f"w_in{i}") for i in range(NP)]
        ones_in = m.sem("ones_in")
        abs_rdy = m.sem("abs_rdy")
        tot_rdy = m.sem("tot_rdy")
        all_rdy = m.sem("all_rdy")
        sc_rdy = m.sem("sc_rdy")
        neg_rdy = m.sem("neg_rdy")
        wq_rdy = m.sem("wq_rdy")

        src = [d[n].rearrange("(k p) n -> k p n", p=P)[k] for n in ("w_gate", "w_up") for k in range(4)]
        src += [d["w_down"].rearrange("(g k p) n -> g p k n", k=4, p=P)[k] for k in range(4)]

        with nc.Block() as block:
            @block.sync
            def _(sp):
                sp.dma_start(ones[:], d["ones"]).then_inc(ones_in, 16)
                for n in range(NP):
                    dst = W[:, n, :] if n < 8 else W[:, n, :].rearrange("p (k n) -> p k n", k=4)
                    sp.dma_start(dst, src[n]).then_inc(w_in[n], 16)

            @block.gpsimd
            def _(pool):
                for g in range(TT * TOPK):
                    i, k = g // TOPK, g % TOPK
                    if g >= NR:
                        pool.wait_ge(used, g - NR + 1)
                    nc.gpsimd.indirect_dma_start(
                        out=yr[:, g % NR, :], out_offset=None, in_=r["y_d"],
                        in_offset=bass.IndirectOffsetOnAxis(ap=r["pos"][:, i, k:k + 1], axis=0)).then_inc(got[g % NR], 16)

            @block.tensor
            def _(pe):
                pe.wait_ge(ones_in, 16)
                pe.wait_ge(tot_rdy, 1)
                nc.tensor.matmul(pa[:, 0:3], ones[:], wtot[:], start=True, stop=True).then_inc(all_rdy, 1)

            @block.vector
            def _(dve):
                V = nc.vector

                def magnitude(n):
                    dve.wait_ge(w_in[n], 16)
                    V.tensor_reduce(wsum[:, n // 4, n % 4:n % 4 + 1], W[:, n, :], AX.X, ALU.add,
                                    apply_absolute_value=True).then_inc(abs_rdy, 1)

                def total():
                    dve.wait_ge(abs_rdy, NP)
                    V.reduce_sum(wtot[:], wsum[:], AX.X).then_inc(tot_rdy, 1)

                def scales():
                    dve.wait_ge(all_rdy, 1)
                    V.tensor_scalar(wsc[:], pa[:, 0:3], 1.0 / (H * IF), EPS, ALU.mult, ALU.add).then_inc(sc_rdy, 1)
                    dve.wait_ge(sc_rdy, 1)
                    V.tensor_scalar(whi[:], wsc[:], 0.5, None, ALU.mult).then_inc(sc_rdy, 1)
                    V.tensor_scalar(wlo[:], wsc[:], -0.5, None, ALU.mult).then_inc(sc_rdy, 1)
                    dve.wait_ge(sc_rdy, 3)

                def below(n):
                    if n >= 2:
                        dve.wait_ge(wq_rdy, n - 1)
                    V.tensor_scalar(neg[:, n % 2, :], W[:, n, :], wlo[:, n // 4:n // 4 + 1], None,
                                    ALU.is_lt).then_inc(neg_rdy, 1)

                def quantise(n):
                    dve.wait_ge(neg_rdy, n + 1)
                    V.scalar_tensor_tensor(out=Wq[n // 4][:, n % 4, :], in0=W[:, n, :], scalar=whi[:, n // 4:n // 4 + 1],
                                           in1=neg[:, n % 2, :], op0=ALU.is_gt, op1=ALU.subtract).then_inc(wq_rdy, 1)

                for g in range(TT * TOPK):
                    i, k = g // TOPK, g % TOPK
                    dve.wait_ge(got[g % NR], 16 * (g // NR + 1))
                    if k:
                        dve.wait_ge(used, g)
                    V.scalar_tensor_tensor(out=X[:, i, :], in0=yr[:, g % NR, :], scalar=r["w8"][:, i, k:k + 1],
                                           in1=X[:, i, :], op0=ALU.mult, op1=ALU.add).then_inc(used, 1)
                    if 6 <= g < 6 + 2 * NP and g % 2:
                        magnitude((g - 6) // 2)
                    if g == 6 + 2 * NP:
                        total()
                    if g == 8 + 2 * NP:
                        scales()
                    if g >= 9 + 2 * NP and g < 9 + 4 * NP:
                        n = g - 9 - 2 * NP
                        (quantise if n % 2 else below)(n // 2)
        m.clear()


def quant_ffn(nc, d, X, Wq, wsc, out):
    with ExitStack() as ctx:
        m = Mem(nc, ctx, "ffn")
        ident = m.sb("ident", [P, P], BF16)
        eps = m.sb("eps", [P, 1])
        st = m.sb("st", [P, TT, 6])
        mv = m.sb("mv", [P, TT, 2])
        sd = m.sb("sd", [P, TT])
        rstd = m.sb("rstd", [P, TT])
        nmr = m.sb("nmr", [P, TT])
        xn = m.sb("xn", [P, 2, H])
        xq = m.sb("xq", [P, 2, H], BF16)
        xqT = m.sb("xqT", [P, 2, HK, P], BF16)
        sx = m.sb("sx", [P, TT, 5])
        hm = m.sb("hm", [P, 2, FC])
        rnd = m.sb("rnd", [P, 1])
        sh = m.sb("sh", [P, TT, 4])
        gg = m.sb("gg", [P, 2, IF])
        hq = m.sb("hq", [P, 2, IF], BF16)
        hqT = m.sb("hqT", [P, 2, FK, P], BF16)
        pg = [m.ps(f"pg{i}", [P, 512]) for i in range(2)]
        pu = [m.ps(f"pu{i}", [P, 512]) for i in range(2)]
        pt = [m.ps(f"pt{i}", [P, 8, P], BF16) for i in range(2)]
        pd = m.ps("pd", [P, H])

        loaded = m.sem("loaded")
        eps_rdy = m.sem("eps_rdy")
        mv_rdy = m.sem("mv_rdy")
        sd_rdy = m.sem("sd_rdy")
        ln_rdy = m.sem("ln_rdy")
        step = m.sem("step")
        xn_rdy = m.sem("xn_rdy")
        xq_rdy = m.sem("xq_rdy")
        tx_rdy = m.sem("tx_rdy")
        xqT_rdy = m.sem("xqT_rdy")
        gu_rdy = m.sem("gu_rdy")
        sg_rdy = m.sem("sg_rdy")
        gh_rdy = m.sem("gh_rdy")
        mx_rdy = m.sem("mx_rdy")
        s_rdy = m.sem("s_rdy")
        rnd_rdy = m.sem("rnd_rdy")
        hq_rdy = m.sem("hq_rdy")
        th_rdy = m.sem("th_rdy")
        hqT_rdy = m.sem("hqT_rdy")
        dn_rdy = m.sem("dn_rdy")
        x_rdy = m.sem("x_rdy")
        o_out = m.sem("o_out")

        with nc.Block() as block:

            @block.sync
            def _(sp):
                sp.dma_start(ident[:], d["ident_bf"]).then_inc(loaded, 16)
                for i in range(TT):
                    sp.wait_ge(x_rdy, i + 1)
                    sp.dma_start(out[i * P:(i + 1) * P, :], X[:, i, :]).then_inc(o_out, 16)
                sp.wait_ge(o_out, 16 * TT)

            @block.vector
            def _(dve):
                V = nc.vector
                n = [0]

                def own(ins):
                    ins.then_inc(step, 1)
                    n[0] += 1
                    dve.wait_ge(step, n[0])

                V.memset(rnd[:], ROUND)
                V.memset(eps[:], EPS).then_inc(eps_rdy, 1)
                for i in range(TT):
                    q = V.bn_stats(st[:, i, :], X[:, i, :])
                own(q)
                for i in range(TT):
                    q = V.bn_aggr(mv[:, i, :], st[:, i, :])
                q.then_inc(mv_rdy, 1)
                dve.wait_ge(sd_rdy, 1)
                own(V.reciprocal(rstd[:], sd[:]))
                V.scalar_tensor_tensor(out=nmr[:], in0=mv[:, :, 0], scalar=-1.0, in1=rstd[:], op0=ALU.mult,
                                       op1=ALU.mult).then_inc(ln_rdy, 1)

                def x_quant(i):
                    xi, s = xn[:, i % 2, :], sx[:, i, :]
                    dve.wait_ge(xn_rdy, i + 1)
                    own(V.tensor_reduce(s[:, 0:1], xi, AX.X, ALU.max, apply_absolute_value=True))
                    own(V.tensor_scalar(s[:, 1:2], s[:, 0:1], 1.0 / 127.0, EPS, ALU.mult, ALU.add))
                    own(V.reciprocal(s[:, 2:3], s[:, 1:2]))
                    own(V.tensor_scalar(xi, xi, s[:, 2:3], ROUND, ALU.mult, ALU.add))
                    if i >= 2:
                        dve.wait_ge(tx_rdy, i - 1)
                    V.tensor_scalar(xq[:, i % 2, :], xi, -ROUND, 127.0, ALU.add, ALU.min)
                    V.tensor_scalar(s[:, 3:4], s[:, 1:2], wsc[:, 0:1], None, ALU.mult)
                    V.tensor_scalar(s[:, 4:5], s[:, 1:2], wsc[:, 1:2], None, ALU.mult).then_inc(xq_rdy, 1)

                def add(i):
                    dve.wait_ge(dn_rdy, i + 1)
                    V.scalar_tensor_tensor(out=X[:, i, :], in0=pd[:], scalar=sh[:, i, 3:4], in1=X[:, i, :],
                                           op0=ALU.mult, op1=ALU.add).then_inc(x_rdy, 1)

                x_quant(0)
                for i in range(TT):
                    if i + 1 < TT:
                        x_quant(i + 1)
                    dve.wait_ge(xq_rdy, i + 1)
                    for f in range(FC):
                        g, own_f = i * FC + f, gg[:, i % 2, f * 512:(f + 1) * 512]
                        dve.wait_ge(sg_rdy, g + 1)
                        V.scalar_tensor_tensor(out=own_f, in0=pu[g % 2][:], scalar=sx[:, i, 4:5], in1=own_f,
                                               op0=ALU.mult, op1=ALU.mult).then_inc(gh_rdy, 1)
                        dve.wait_ge(gh_rdy, g + 1)
                        V.tensor_reduce(hm[:, i % 2, f:f + 1], own_f, AX.X, ALU.max,
                                        apply_absolute_value=True).then_inc(mx_rdy, 1)
                    s = sh[:, i, :]
                    dve.wait_ge(mx_rdy, (i + 1) * FC)
                    own(V.reduce_max(s[:, 0:1], hm[:, i % 2, :], AX.X))
                    own(V.tensor_scalar(s[:, 1:2], s[:, 0:1], 1.0 / 127.0, EPS, ALU.mult, ALU.add))
                    V.tensor_scalar(s[:, 3:4], s[:, 1:2], wsc[:, 2:3], None, ALU.mult)
                    V.reciprocal(s[:, 2:3], s[:, 1:2]).then_inc(s_rdy, 1)
                    if i >= 2:
                        dve.wait_ge(th_rdy, 2 * (i - 1))
                    dve.wait_ge(rnd_rdy, i + 1)
                    V.tensor_scalar(hq[:, i % 2, :], gg[:, i % 2, :], -ROUND, 127.0, ALU.add, ALU.min).then_inc(hq_rdy, 1)
                    if i:
                        add(i - 1)
                add(TT - 1)

            @block.scalar
            def _(act):
                act.wait_ge(eps_rdy, 1)
                act.wait_ge(mv_rdy, 1)
                nc.scalar.activation(sd[:], mv[:, :, 1], ACT.Sqrt, bias=eps[:]).then_inc(sd_rdy, 1)
                act.wait_ge(ln_rdy, 1)

                def layernorm(i):
                    if i >= 2:
                        act.wait_ge(xq_rdy, i - 1)
                    nc.scalar.activation(xn[:, i % 2, :], X[:, i, :], ACT.Identity, bias=nmr[:, i:i + 1],
                                         scale=rstd[:, i:i + 1]).then_inc(xn_rdy, 1)

                def x_evac(i):
                    act.wait_ge(tx_rdy, i + 1)
                    nc.scalar.copy(xqT[:, i % 2, :, :], pt[0][:, 0:HK, :]).then_inc(xqT_rdy, 1)

                def h_evac(i, a):
                    act.wait_ge(th_rdy, 2 * i + a + 1)
                    nc.scalar.copy(hqT[:, i % 2, 8 * a:8 * a + 8, :], pt[a][:]).then_inc(hqT_rdy, 1)

                layernorm(0)
                layernorm(1)
                x_evac(0)
                for i in range(TT):
                    act.wait_ge(xq_rdy, i + 1)
                    for f in range(FC):
                        g = i * FC + f
                        act.wait_ge(gu_rdy, g + 1)
                        if i >= 2:
                            act.wait_ge(hq_rdy, i - 1)
                        nc.scalar.activation(gg[:, i % 2, f * 512:(f + 1) * 512], pg[g % 2][:], ACT.Silu,
                                             scale=sx[:, i, 3:4]).then_inc(sg_rdy, 1)
                        if i and f in (1, 2):
                            h_evac(i - 1, f - 1)
                    if i + 1 < TT:
                        x_evac(i + 1)
                    act.wait_ge(s_rdy, i + 1)
                    nc.scalar.activation(gg[:, i % 2, :], gg[:, i % 2, :], ACT.Identity, bias=rnd[:],
                                         scale=sh[:, i, 2:3]).then_inc(rnd_rdy, 1)
                    if i + 2 < TT:
                        layernorm(i + 2)
                for a in range(2):
                    h_evac(TT - 1, a)

            @block.tensor
            def _(pe):
                pe.wait_ge(loaded, 16)

                def x_transpose(i):
                    pe.wait_ge(xq_rdy, i + 1)
                    if i >= 2:
                        pe.wait_ge(hqT_rdy, 2 * (i - 2) + 1)
                    for k in range(HK):
                        tr = nc.tensor.transpose(pt[0][:, k, :], xq[:, i % 2, k * P:(k + 1) * P], ident[:])
                    tr.then_inc(tx_rdy, 1)

                def h_transpose(i, a):
                    pe.wait_ge(hq_rdy, i + 1)
                    if a == 0:
                        pe.wait_ge(xqT_rdy, min(i + 2, TT))
                    elif i:
                        pe.wait_ge(hqT_rdy, 2 * i)
                    for k in range(8):
                        o = (8 * a + k) * P
                        tr = nc.tensor.transpose(pt[a][:, k, :], hq[:, i % 2, o:o + P], ident[:])
                    tr.then_inc(th_rdy, 1)

                def down(i):
                    if i:
                        pe.wait_ge(x_rdy, i)
                    for k in range(FK):
                        if k % 8 == 0:
                            pe.wait_ge(hqT_rdy, 2 * i + k // 8 + 1)
                        mm = nc.tensor.matmul(pd[:], hqT[:, i % 2, k, :], Wq[2][:, k // 4, (k % 4) * H:(k % 4 + 1) * H],
                                              start=(k == 0), stop=(k == FK - 1))
                    mm.then_inc(dn_rdy, 1)

                x_transpose(0)
                for i in range(TT):
                    pe.wait_ge(xqT_rdy, i + 1)
                    for f in range(FC):
                        g = i * FC + f
                        if g >= 2:
                            pe.wait_ge(gh_rdy, g - 1)
                        for ps, w in ((pg, 0), (pu, 1)):
                            for k in range(HK):
                                mm = nc.tensor.matmul(ps[g % 2][:], xqT[:, i % 2, k, :], Wq[w][:, k, f * 512:(f + 1) * 512],
                                                      start=(k == 0), stop=(k == HK - 1))
                        mm.then_inc(gu_rdy, 1)
                        if i and f in (1, 2):
                            h_transpose(i - 1, f - 1)
                    if i + 1 < TT:
                        x_transpose(i + 1)
                    if i:
                        down(i - 1)
                for a in range(2):
                    h_transpose(TT - 1, a)
                down(TT - 1)


def bass_program(nc, d, out):
    d = dict(d)
    for name in ("w_hi", "w_lo"):
        d[name] = nc.dram_tensor(name, (P, NEX * WE), F16).ap()
    y_ssm = nc.dram_tensor("y_ssm", (T, L), F32).ap()
    ssm_first(nc, d, y_ssm)
    with ExitStack() as ctx:
        m = Mem(nc, ctx, "all")
        X = m.sb("X", [P, TT, H])
        r = {
            "xn_d": nc.dram_tensor("xn_d", (T, H), F32).ap(),
            "y_d": nc.dram_tensor("y_d", (NSLOT, H), F32).ap(),
            "logit": m.sb("logit", [P, TT, E + 1]),
            "sig": m.sb("sig", [P, TT]),
            "w8": m.sb("w8", [P, TT, 8]),
            "pos": m.sb("pos", [P, TT, TOPK], U32),
            "idx": m.sb("idx", [P, NALL], U32),
            "tab": m.sb("tab", [1, 4, NALL], I32),
        }
        gate(nc, 0, d, X, y_ssm, r)
        routing(nc, d, r)
        experts_and_ssm(nc, d, r, X, y_ssm)
        Wq = [m.sb(f"Wq{i}", [P, 4, IF], BF16) for i in range(3)]
        wsc = m.sb("wsc", [P, 3])
        combine(nc, d, r, X, Wq, wsc)
        gate(nc, 1, d, X, y_ssm, r)
        quant_ffn(nc, d, X, Wq, wsc, out)


def layouts(inputs):
    import numpy as np
    a = {k: np.asarray(v) for k, v in inputs.items()}
    c = np.ascontiguousarray
    p = np.arange(P)
    d = {
        "x": c(a["x"].reshape(T, H)),
        "ctxT": c(a["ctx_1024"].reshape(T, DM).T),
        "ident": np.eye(P, dtype=np.float32),
        "sel": c((p[:96, None, None] % (2 * NS) == np.arange(2 * NS)[None, :, None])
                 * np.ones((1, 1, P))).astype(mybir.dt.np(BF16)),
    }
    d.update({
        "ident_bf": np.eye(P, dtype=np.float32).astype(mybir.dt.np(BF16)),
        "tri": np.triu(np.ones((P, P), np.float32), 1),
        "ones": np.ones((P, P), np.float32),
        "e_of": np.tile(np.arange(E, dtype=np.float32), (P, 1)),
        "thr": np.tile(np.arange(TT, dtype=np.float32) * P, (P, 1)),
        "col": np.tile(np.arange(P, dtype=np.float32), (P, 1)),
        "tok": c((np.arange(TT)[None, :] * P + p[:, None]).astype(np.float32)),
        "turn": np.array([[(e + 1) % WR - (e % WR if e else 0) for e in range(E)]], np.float32),
        "tab": np.array([[g // TT, 0, g // TT % WR, g % TT] if g < NA else [0] * 4
                         for g in range(NALL)], np.int32).T.copy()[None],
        "w_router": c(np.concatenate([a["L0_ffn_gate_w"], a["L0_ffn_sgate_w"]], 0).T),
        "w_all": w_all(a),
        "w_gate": c(a["L1_ffn_w_gate"].T),
        "w_up": c(a["L1_ffn_w_up"].T),
        "w_down": c(a["L1_ffn_w_down"].T),
    })
    for l in range(2):
        w = {k[len(f"L{l}_xattn_"):]: v for k, v in a.items() if k.startswith(f"L{l}_xattn_")}
        xp = w["x_proj_w"]
        d[f"w_in{l}"] = c(w["in_proj_w"].T)
        d[f"w_x{l}"] = c(np.concatenate([xp[DR:]] * 3 + [xp[:DR]], 0).T)
        d[f"w_up{l}"] = c(w["dt_proj_w"].T)
        d[f"cw{l}"] = c(w["conv_w"].reshape(DI, DC))
        d[f"cb{l}"] = c(w["conv_b"].reshape(KC, P).T)
        d[f"db{l}"] = c(w["dt_proj_b"].reshape(KC, P).T)
        d[f"D{l}"] = c(w["D"].reshape(KC, P).T)
        d[f"alog{l}"] = c(w["A_log"])
    return d


def w_all(a):
    import numpy as np
    w13 = [*a["L0_ffn_w13"], *a["L0_ffn_shared_gate_up_w"].reshape(2, NSH, IE, H).transpose(1, 0, 2, 3)]
    w2 = [*a["L0_ffn_w2"], *a["L0_ffn_shared_down_w"].reshape(H, NSH, IE).transpose(1, 0, 2)]
    w = np.zeros((P, NEX, 2 * IE * HK + 3 * H), np.float32)
    for e in range(NEX):
        up = w13[e].reshape(2 * IE, HK, P).transpose(2, 1, 0)
        w[:, e, :HK * 2 * IE] = up.reshape(P, HK * 2 * IE)
        down = np.zeros((3 * P, H), np.float32)
        down[:IE] = w2[e].T
        w[:, e, HK * 2 * IE:] = down.reshape(3, P, H).transpose(1, 0, 2).reshape(P, 3 * H)
    return w.reshape(P, NEX * WE)


def kernel(**inputs):
    import numpy as np
    import concourse.bacc as bacc
    from concourse.bass_utils import run_bass_kernel_spmd

    nc = bacc.Bacc("TRN2", target_bir_lowering=False, num_devices=1)
    arrays = {f"in_{k}": v for k, v in layouts(inputs).items()}
    aps = {k[3:]: nc.dram_tensor(k, v.shape, mybir.dt.from_np(v.dtype), kind="ExternalInput").ap()
           for k, v in arrays.items()}
    out = nc.dram_tensor("out_0_dram", (T, H), F32, kind="ExternalOutput").ap()
    bass_program(nc, aps, out)
    r = run_bass_kernel_spmd(nc, [arrays], core_ids=[0])
    return r.results[0]["out_0_dram"].reshape(B, L, H)
```

```python
import concourse.bass as bass
from concourse import mybir
from contextlib import ExitStack

F32 = mybir.dt.float32
F16 = mybir.dt.float16
BF16 = mybir.dt.bfloat16
I32 = mybir.dt.int32
U32 = mybir.dt.uint32
ALU = mybir.AluOpType
ACT = mybir.ActivationFunctionType
AX = mybir.AxisListType
ds = bass.ds

P = 128
B, L, H = 4, 512, 512
T = B * L
TT = T // P
DM = 256
DI, NS, DC, DR = 512, 16, 4, 16
KC = DI // P
HC = KC // 2
HK = H // P
E, TOPK, IE = 16, 4, 352
ISH = 1408
NSH = ISH // IE
NSTEP = T * TOPK // P + E
NSLOT = NSTEP * P
NEX = E + NSH
WE = 4 * 2 * IE + 3 * H
WS = 256.0
XS = 256.0
HS = 16.0
NA = NSH * TT
NALL = NA + NSTEP
R = 4
WR = 3
IF = 2048
FC = IF // 512
FK = IF // P
STEPS = 2 * NS
EPS = 1e-5
ROUND = 12582912.0
ICH = [(0, 128), (128, 128), (256, 96)]


class Mem:

    def __init__(self, nc, ctx, tag):
        self.nc, self.ctx, self.tag, self.sems = nc, ctx, tag, []

    def sb(self, name, shape, dt=F32):
        return self.ctx.enter_context(self.nc.sbuf_tensor(f"{self.tag}_{name}", shape, dt))

    def ps(self, name, shape, dt=F32):
        return self.ctx.enter_context(self.nc.psum_tensor(f"{self.tag}_{name}", shape, dt))

    def sem(self, name):
        self.sems.append(self.ctx.enter_context(self.nc.semaphore(f"{self.tag}_{name}")))
        return self.sems[-1]

    def clear(self):
        with self.nc.Block() as block:
            @block.sync
            def _(sp):
                for s in self.sems:
                    sp.sem_clear(s)


class Ssm:

    def __init__(self, nc, m, l, d, dbl, nb, ny, ring, alone):
        self.alone, self.ny = alone, ny
        self.nc, self.l, self.d, self.dbl, self.nb, self.ring = nc, l, d, dbl, nb, ring
        self.sel = m.sb("sel", [96, 2 * NS, P], BF16)
        self.cx = m.sb("cx", [P, 2, L])
        self.w_in = m.sb("w_in", [P, 2, DI])
        self.w_x = m.sb("w_x", [P, KC, 96 + DR])
        self.w_up = m.sb("w_up", [P, DI])
        self.cw = m.sb("cw", [P, KC, DC])
        self.cb = m.sb("cb", [P, KC])
        self.db = m.sb("db", [P, KC])
        self.alog = m.sb("alog", [P, KC, NS])
        self.A = m.sb("A", [P, KC, NS])
        self.Dv = m.sb("Dv", [P, KC])
        self.ident = m.sb("ident", [P, P])
        self.U = m.sb("U", [P, dbl, KC, L])
        self.dlt = m.sb("dlt", [P, dbl, KC, L])
        self.du = m.sb("du", [P, dbl, KC, L])
        self.bc3 = m.sb("bc3", [96, dbl, L], BF16)
        self.low = m.sb("low", [P, L])
        self.Bs = m.sb("Bs", [P, ring, L])
        self.Cs = m.sb("Cs", [P, R, L])
        self.dA = m.sb("dA", [P, ring, HC, L])
        self.hs = m.sb("hs", [P, R, HC, L])
        if alone:
            self.diagD = m.sb("diagD", [P, KC, P])
            self.pair = m.sb("pair", [P, 2, HC, L])
        if not alone:
            self.acc = self.hs[:, 0:2, :, :].rearrange("p a b t -> p (a b) t")
            self.tmp = self.hs[:, 2:4, :, :].rearrange("p a b t -> p (a b) t")
        else:
            self.acc = m.sb("acc", [P, KC, L])[:]
            self.tmp = m.sb("tmp", [P, KC, L])[:]
        self.pB = [m.ps(f"pB{i}", [P, L]) for i in range(nb)]
        self.pC = [m.ps(f"pC{i}", [P, L]) for i in range(nb)]
        self.pY = [[m.ps(f"pY{i}{k}", [P, L]) for k in range(HC)] for i in range(ny)]
        self.pw = [m.ps(f"pw{i}", [P, L]) for i in range(2)] if alone else [self.pB[0], self.pC[0]]

        self.loaded = m.sem("loaded")
        self.cx_in = m.sem("cx_in")
        self.a_exp = m.sem("a_exp")
        self.a_neg = m.sem("a_neg")
        self.diag_rdy = m.sem("diag_rdy")
        self.in_rdy = m.sem("in_rdy")
        self.conv_a = m.sem("conv_a")
        self.conv_v = m.sem("conv_v")
        self.u_rdy = m.sem("u_rdy")
        self.xp_rdy = m.sem("xp_rdy")
        self.dts_rdy = m.sem("dts_rdy")
        self.bc_split = m.sem("bc_split")
        self.dtz_rdy = m.sem("dtz_rdy")
        self.ar_rdy = m.sem("ar_rdy")
        self.e_rdy = m.sem("e_rdy")
        self.t_rdy = m.sem("t_rdy")
        self.q_rdy = m.sem("q_rdy")
        self.ln_rdy = m.sem("ln_rdy")
        self.d_step = m.sem("d_step")
        self.bc_rdy = m.sem("bc_rdy")
        self.bc_evac = m.sem("bc_evac")
        self.exp_rdy = m.sem("exp_rdy")
        self.bu_done = m.sem("bu_done")
        self.scan_done = m.sem("scan_done")
        self.prod_done = m.sem("prod_done")
        self.acc_done = m.sem("acc_done")
        self.pair_done = m.sem("pair_done")
        self.sum_done = m.sem("sum_done")
        self.y_init = m.sem("y_init")
        self.y_out = m.sem("y_out")
        self.y_dram = m.sem("y_dram")

    def load(self, sp):
        d, l = self.d, self.l
        for dst, src in [(self.ident[:], d["ident"]), (self.sel[:], d["sel"]),
                         (self.w_in[:], d[f"w_in{l}"].rearrange("(k p) n -> p k n", p=P)),
                         (self.w_x[:], d[f"w_x{l}"].rearrange("(k p) n -> p k n", p=P)),
                         (self.w_up[96:96 + DR, :], d[f"w_up{l}"]),
                         (self.cw[:], d[f"cw{l}"].rearrange("(k p) n -> p k n", p=P)),
                         (self.cb[:], d[f"cb{l}"]), (self.db[:], d[f"db{l}"]), (self.Dv[:], d[f"D{l}"]),
                         (self.alog[:], d[f"alog{l}"].rearrange("(k p) n -> p k n", p=P))]:
            sp.dma_start(dst, src).then_inc(self.loaded, 16)

    def load_ctx(self, sp, b):
        if b:
            sp.wait_ge(self.in_rdy, KC * b)
        sp.dma_start(self.cx[:], self.d["ctxT"].rearrange("(k p) n -> p k n", p=P)[:, :, b * L:(b + 1) * L])\
          .then_inc(self.cx_in, 16)

    def store_y(self, sp, y_ssm, b):
        if self.alone:
            sp.wait_ge(self.y_out, 2 * b + 2)
        else:
            sp.wait_ge(self.acc_done, (b + 1) * STEPS + R)
        sp.dma_start(y_ssm[b * L:(b + 1) * L, :].rearrange("(k p) n -> p k n", p=P),
                     self.U[:, b % self.dbl, :, :]).then_inc(self.y_dram, 16)

    def pe_start(self, pe):
        if self.alone:
            pe.sem_inc(self.sum_done, 1)
        pe.wait_ge(self.loaded, 160)

    def pe_in(self, pe, b, c):
        nc, g = self.nc, b * KC + c
        pe.wait_ge(self.cx_in, 16 * (b + 1))
        if c >= 2:
            pe.wait_ge(self.conv_v, 3 * (g - 1))
        elif b:
            pe.wait_ge(self.ar_rdy, b * KC)
            if not self.alone:
                pe.wait_ge(self.bc_evac, b * STEPS + self.nb)
        for k in range(2):
            mm = nc.tensor.matmul(self.pw[c % 2][:], self.w_in[:, k, c * P:(c + 1) * P], self.cx[:, k, :],
                                  start=(k == 0), stop=(k == 1))
        mm.then_inc(self.in_rdy, 1)

    def pe_x(self, pe, b):
        pe.wait_ge(self.u_rdy, b + 1)
        for c in range(KC):
            mm = self.nc.tensor.matmul(self.pw[0][0:96 + DR, :], self.w_x[:, c, :], self.U[:, b % self.dbl, c, :],
                                       start=(c == 0), stop=(c == KC - 1))
        mm.then_inc(self.xp_rdy, 1)

    def pe_dt(self, pe, b, c):
        pe.wait_ge(self.dts_rdy, b + 1)
        if c == 1:
            pe.wait_ge(self.bc_split, 5 * (b + 1))
        if c >= 2:
            pe.wait_ge(self.ar_rdy, b * KC + c - 1)
        self.nc.tensor.matmul(self.pw[(c + 1) % 2][:], self.w_up[96:96 + DR, c * P:(c + 1) * P],
                              self.low[96:96 + DR, :], start=True, stop=True).then_inc(self.dtz_rdy, 1)

    def pe_spread(self, pe, b, s, n, j):
        nc = self.nc
        pe.wait_ge(self.bc_evac, s + 1)
        nc.tensor.matmul(self.pB[j % self.nb][:], self.sel[:, ds(n, 1), :], self.bc3[:, b % self.dbl, :],
                         start=True, stop=True)
        nc.tensor.matmul(self.pC[j % self.nb][:], self.sel[:, ds(n + NS, 1), :], self.bc3[:, b % self.dbl, :],
                         start=True, stop=True).then_inc(self.bc_rdy, 1)

    def pe_y_init(self, pe, b, half):
        if 2 * b + half - self.ny >= 0:
            pe.wait_ge(self.y_out, 2 * b + half + 1 - self.ny)
        for k in range(HC):
            mm = self.nc.tensor.matmul(self.pY[half % self.ny][k][:], self.diagD[:, half * HC + k, :],
                                       self.U[:, b % self.dbl, half * HC + k, :],
                                       start=True, stop=False, skip_group_check=True)
        mm.then_inc(self.y_init, 1)

    def pe_sum(self, pe, half, p, par, last=False):
        pe.wait_ge(self.pair_done, p + 3)
        for k in range(HC):
            mm = self.nc.tensor.matmul(self.pY[half % self.ny][k][:], self.ident[:], self.pair[:, par, k, :],
                                       start=False, stop=last, skip_group_check=True)
        mm.then_inc(self.sum_done, 1)

    def act_start(self, act):
        nc = self.nc
        act.wait_ge(self.loaded, 160)
        nc.scalar.activation(self.alog[:], self.alog[:], ACT.Exp).then_inc(self.a_exp, 1)
        act.wait_ge(self.a_exp, 1)
        nc.scalar.activation(self.A[:], self.alog[:], ACT.Copy, scale=-1.0).then_inc(self.a_neg, 1)
        act.sem_inc(self.bc_evac, self.nb)
        act.wait_ge(self.a_neg, 1)
        act.wait_ge(self.diag_rdy, KC + 1 if self.alone else 1)

    def act_conv(self, act, b, c):
        act.wait_ge(self.in_rdy, b * KC + c + 1)
        if b:
            act.wait_ge(self.d_step, 3 * b)
            if not self.alone:
                act.wait_ge(self.acc_done, b * STEPS + R)
        self.nc.scalar.activation(self.acc[:, c, :], self.pw[c % 2][:], ACT.Identity,
                                  bias=self.cb[:, c:c + 1], scale=self.cw[:, c, DC - 1:DC]).then_inc(self.conv_a, 1)

    def act_u(self, act, b):
        act.wait_ge(self.conv_v, 3 * KC * (b + 1))
        if b >= self.dbl:
            act.wait_ge(self.y_dram, 16 * (b - self.dbl + 1))
        self.nc.scalar.activation(self.U[:, b % self.dbl, :, :], self.acc, ACT.Silu).then_inc(self.u_rdy, 1)

    def act_dt(self, act, b):
        act.wait_ge(self.xp_rdy, b + 1)
        self.nc.scalar.copy(self.low[96:96 + DR, :], self.pw[0][96:96 + DR, :]).then_inc(self.dts_rdy, 1)

    def act_z(self, act, b, c):
        nc = self.nc
        act.wait_ge(self.u_rdy, b + 1)
        act.wait_ge(self.dtz_rdy, b * KC + c + 1)
        nc.scalar.activation(self.acc[:, c, :], self.pw[(c + 1) % 2][:], ACT.Abs, bias=self.db[:, c:c + 1])
        nc.scalar.activation(self.dlt[:, b % self.dbl, c, :], self.pw[(c + 1) % 2][:], ACT.Relu,
                             bias=self.db[:, c:c + 1]).then_inc(self.ar_rdy, 1)

    def act_e(self, act, b):
        act.wait_ge(self.ar_rdy, (b + 1) * KC)
        self.nc.scalar.activation(self.acc, self.acc, ACT.Exp, scale=-1.0).then_inc(self.e_rdy, 1)

    def act_ln(self, act, b):
        act.wait_ge(self.q_rdy, b + 1)
        self.nc.scalar.activation(self.tmp, self.tmp, ACT.Ln, bias=1.0).then_inc(self.ln_rdy, 1)

    def act_step(self, act, b, half, s, n, j):
        nc, q = self.nc, j % self.ring
        act.wait_ge(self.bc_rdy, s + 1)
        act.wait_ge(self.bu_done, s + 1)
        nc.scalar.copy(self.Bs[:, q, :], self.pB[j % self.nb][:])
        act.wait_ge(self.prod_done, s + 1)
        nc.scalar.copy(self.Cs[:, j, :], self.pC[j % self.nb][:]).then_inc(self.bc_evac, 1)
        act.wait_ge(self.scan_done, s + 1)
        for k in range(HC):
            c = half * HC + k
            ex = nc.scalar.activation(self.dA[:, q, k, 1:L], self.dlt[:, b % self.dbl, c, 1:L], ACT.Exp,
                                      scale=self.A[:, c, ds(n, 1)])
        ex.then_inc(self.exp_rdy, 1)

    def act_y(self, act, b, half):
        act.wait_ge(self.sum_done, (2 * b + half + 1) * NS // 2 + 1)
        for k in range(HC):
            cp = self.nc.scalar.copy(self.U[:, b % self.dbl, half * HC + k, :], self.pY[half % self.ny][k][:])
        cp.then_inc(self.y_out, 1)

    def dve_start(self, dve):
        nc = self.nc
        dve.wait_ge(self.loaded, 160)
        for c in range(KC if self.alone else 0):
            nc.vector.tensor_scalar(self.diagD[:, c, :], self.ident[:], self.Dv[:, c:c + 1], None,
                                    ALU.mult).then_inc(self.diag_rdy, 1)
        nc.vector.memset(self.dA[:, :, :, 0:1], 0.0).then_inc(self.diag_rdy, 1)
        dve.sem_inc(self.bu_done, self.ring)
        dve.sem_inc(self.scan_done, self.ring)

    def dve_conv(self, dve, b, c):
        g, acc, cw = b * KC + c, self.acc, self.cw
        dve.wait_ge(self.conv_a, g + 1)
        for t in range(1, DC):
            if t > 1:
                dve.wait_ge(self.conv_v, 3 * g + t - 1)
            self.nc.vector.scalar_tensor_tensor(
                out=acc[:, c, t:L], in0=self.pw[c % 2][:, 0:L - t], scalar=cw[:, c, DC - 1 - t:DC - t],
                in1=acc[:, c, t:L], op0=ALU.mult, op1=ALU.add).then_inc(self.conv_v, 1)

    def dve_split(self, dve, b):
        V, q, part, rest, ps = self.nc.vector, 5 * b, self.bc3[:, b % self.dbl, :], self.low[64:96, :], self.pw[0]
        dve.wait_ge(self.xp_rdy, b + 1)
        V.tensor_copy(part, ps[0:96, :]).then_inc(self.bc_split, 1)
        dve.wait_ge(self.bc_split, q + 1)
        V.tensor_tensor(rest, ps[64:96, :], part[64:96, :], ALU.subtract).then_inc(self.bc_split, 1)
        V.tensor_tensor(part[32:64, :], ps[32:64, :], part[32:64, :], ALU.subtract).then_inc(self.bc_split, 1)
        dve.wait_ge(self.bc_split, q + 3)
        V.tensor_copy(part[64:96, :], rest).then_inc(self.bc_split, 1)
        dve.wait_ge(self.bc_split, q + 4)
        V.tensor_tensor(part[64:96, :], rest, part[64:96, :], ALU.subtract).then_inc(self.bc_split, 1)

    def dve_t(self, dve, b):
        V = self.nc.vector
        dve.wait_ge(self.e_rdy, b + 1)
        V.tensor_scalar(self.tmp, self.acc, 1.0, -1.0, ALU.add, ALU.add).then_inc(self.t_rdy, 1)
        dve.wait_ge(self.t_rdy, b + 1)
        V.tensor_tensor(self.acc, self.acc, self.tmp, ALU.subtract).then_inc(self.q_rdy, 1)

    def dve_delta(self, dve, b):
        V, D_ = self.nc.vector, self.dlt[:, b % self.dbl, :, :]
        dve.wait_ge(self.q_rdy, b + 1)
        V.tensor_tensor(D_, D_, self.acc, ALU.add).then_inc(self.d_step, 1)
        dve.wait_ge(self.d_step, 3 * b + 1)
        dve.wait_ge(self.ln_rdy, b + 1)
        V.tensor_tensor(D_, D_, self.tmp, ALU.add).then_inc(self.d_step, 1)
        dve.wait_ge(self.d_step, 3 * b + 2)
        V.tensor_tensor(self.du[:, b % self.dbl, :, :], D_, self.U[:, b % self.dbl, :, :], ALU.mult)\
         .then_inc(self.d_step, 1)

    def dve_step(self, dve, b, half, s, p, j):
        nc, q = self.nc, j % self.ring
        dve.wait_ge(self.bc_evac, s + 1 + self.nb)
        if self.alone:
            dve.wait_ge(self.pair_done, p + 1)
        else:
            dve.wait_ge(self.acc_done, s + 1)
        nc.vector.tensor_tensor(self.hs[:, j, :, :], self.du[:, b % self.dbl, half * HC:(half + 1) * HC, :],
                                self.Bs[:, q:q + 1, :].to_broadcast([P, HC, L]), ALU.mult).then_inc(self.bu_done, 1)
        dve.wait_ge(self.exp_rdy, s + 1)
        dve.wait_ge(self.bu_done, s + 1 + self.ring)
        flat = self.hs[:, j, :, :].rearrange("p k t -> p (k t)")
        nc.vector.tensor_tensor_scan(flat, self.dA[:, q, :, :].rearrange("p k t -> p (k t)"), flat,
                                     0.0, ALU.mult, ALU.add).then_inc(self.scan_done, 1)

    def pool_start(self, pool):
        pool.sem_inc(self.prod_done, R)
        if self.alone:
            pool.sem_inc(self.pair_done, 2)
        else:
            pool.sem_inc(self.acc_done, R)

    def pool_pair(self, pool, p, j):
        pool.wait_ge(self.prod_done, 2 * p + 2 + R)
        if not isinstance(p, int) or p:
            pool.wait_ge(self.sum_done, p)
        self.nc.gpsimd.tensor_tensor(self.pair[:, j // 2, :, :], self.hs[:, j, :, :], self.hs[:, j + 1, :, :],
                                     ALU.add).then_inc(self.pair_done, 1)

    def pool_y_init(self, pool, b):
        U = self.U[:, b % self.dbl, :, :]
        pool.wait_ge(self.d_step, 3 * (b + 1))
        self.nc.gpsimd.tensor_tensor(U, U, self.Dv[:].unsqueeze(2).to_broadcast([P, KC, L]), ALU.mult)\
            .then_inc(self.y_init, 1)
        pool.wait_ge(self.y_init, b + 1)

    def pool_add(self, pool, b, half, s, j):
        Y = self.U[:, b % self.dbl, half * HC:(half + 1) * HC, :]
        pool.wait_ge(self.prod_done, s + 1 + R)
        pool.wait_ge(self.acc_done, s + R)
        self.nc.gpsimd.tensor_tensor(Y, Y, self.hs[:, j, :, :], ALU.add).then_inc(self.acc_done, 1)

    def pool_step(self, pool, s, j):
        pool.wait_ge(self.scan_done, s + 1 + self.ring)
        pool.wait_ge(self.bc_evac, s + 1 + self.nb)
        self.nc.gpsimd.tensor_tensor(self.hs[:, j, :, :], self.hs[:, j, :, :],
                                     self.Cs[:, j:j + 1, :].to_broadcast([P, HC, L]), ALU.mult)\
            .then_inc(self.prod_done, 1)


def ssm_first(nc, d, X, y_ssm):
    with ExitStack() as ctx:
        m = Mem(nc, ctx, "ssm0")
        S = Ssm(nc, m, 0, d, dbl=2, nb=1, ny=2, ring=R, alone=True)
        NCH = 2 * B * STEPS // R
        CW = NEX * WE // NCH
        wst = m.sb("wst", [P, 2, CW])
        whi = m.sb("whi", [P, 2, CW], F16)
        wlo = m.sb("wlo", [P, 2, CW], F16)
        x_in = m.sem("x_in")
        w_in = [m.sem(f"w_in{i}") for i in range(2)]
        hi_rdy = m.sem("hi_rdy")
        lo_rdy = m.sem("lo_rdy")
        w_out = [m.sem(f"w_out{i}") for i in range(2)]

        AT = 16

        with nc.Block() as block:

            @block.sync
            def _(sp):
                S.load(sp)
                S.load_ctx(sp, 0)

                def w_load(k, i):
                    sp.dma_start(wst[:, k, :], d["w_all"][:, ds(i * (2 * CW) + k * CW, CW)]).then_inc(w_in[k], 16)

                def w_store(k, i, n):
                    sp.wait_ge(lo_rdy, n)
                    sp.dma_start(d["w_hi"][:, ds(i * (2 * CW) + k * CW, CW)], whi[:, k, :]).then_inc(w_out[k], 16)
                    sp.dma_start(d["w_lo"][:, ds(i * (2 * CW) + k * CW, CW)], wlo[:, k, :]).then_inc(w_out[k], 16)

                for k in range(2):
                    w_load(k, 0)
                sp.dma_start(X[:], d["x"].rearrange("(i p) n -> p i n", p=P)).then_inc(x_in, 16)
                with sp.Fori(0, NCH // 2 - 1) as i:
                    for k in range(2):
                        w_store(k, i, 2 * i + k + 1)
                        w_load(k, i + 1)
                for k in range(2):
                    w_store(k, NCH // 2 - 1, NCH - 1 + k)
                sp.wait_ge(x_in, 16)
                for k in range(2):
                    sp.wait_ge(w_out[k], 16 * NCH)
                sp.wait_ge(S.y_dram, 16 * B)

            @block.tensor
            def _(pe):
                S.pe_start(pe)

                def prologue(b, at):
                    if at == 0 or at == 3:
                        for c in range(2):
                            S.pe_in(pe, b, c + (2 if at else 0))
                    if at == 7:
                        S.pe_x(pe, b)
                    if at == 9 or at == 11:
                        for c in range(2):
                            S.pe_dt(pe, b, c + (2 if at == 11 else 0))

                def scan(b, half):
                    s0, p0 = b * STEPS + half * NS, (b * STEPS + half * NS) // 2
                    pe.wait_ge(S.bc_split, 5 * (b + 1))
                    S.pe_y_init(pe, b, half)
                    for n in range(R):
                        S.pe_spread(pe, b, s0 + n, n, n)
                        if (b or half) and n % 2:
                            S.pe_sum(pe, 1 - half, p0 + n // 2 - 2, n // 2, last=(n == 3))
                        if b + 1 < B:
                            prologue(b + 1, n + R * half)
                    if half:
                        for n in range(R, NS):
                            S.pe_spread(pe, b, s0 + n, n, n % R)
                            if n % 2:
                                S.pe_sum(pe, half, p0 + n // 2 - 2, n // 2 % 2)
                            if b + 1 < B:
                                prologue(b + 1, n + R)
                        return
                    with pe.Fori(1, NS // R) as i:
                        for j in range(R):
                            S.pe_spread(pe, b, R * i + (s0 + j), R * i + j, j)
                            if j % 2:
                                S.pe_sum(pe, half, (R // 2) * i + (p0 + j // 2 - 2), j // 2)

                for at in range(AT):
                    prologue(0, at)
                pe.wait_ge(S.diag_rdy, KC + 1)
                for b in range(B):
                    scan(b, 0)
                    scan(b, 1)
                for p in range(2):
                    S.pe_sum(pe, 1, B * STEPS // 2 - 2 + p, p, last=(p == 1))

            @block.scalar
            def _(act):
                S.act_start(act)

                def prologue(b, at):
                    for c in range(2):
                        if at == 1 or at == 4:
                            S.act_conv(act, b, c + (2 if at == 4 else 0))
                        if at == 4 and c == 1 and b + 1 < B:
                            S.load_ctx(act, b + 1)
                        if at == 10 or at == 12:
                            S.act_z(act, b, c + (2 if at == 12 else 0))
                    if at == 6:
                        S.act_u(act, b)
                    if at == 8:
                        S.act_dt(act, b)
                    if at == 12:
                        S.act_e(act, b)
                    if at == 14:
                        S.act_ln(act, b)

                def hi(k, i):
                    act.wait_ge(w_in[k], 16 * i + 16)
                    if not isinstance(i, int) or i:
                        act.wait_ge(w_out[k], 32 * i)
                    nc.scalar.activation(whi[:, k, :], wst[:, k, :], ACT.Copy, scale=WS).then_inc(hi_rdy, 1)

                def scan(b, half):
                    s0 = b * STEPS + half * NS
                    act.wait_ge(S.d_step, 3 * (b + 1))
                    for n in range(R):
                        S.act_step(act, b, half, s0 + n, n, n)
                        if n == R - 1 and (b or half):
                            S.act_y(act, b - 1 + half, 1 - half)
                            if not half:
                                S.store_y(act, y_ssm, b - 1)
                        if n % 2 == 0:
                            hi(n // 2, s0 // R)
                        if b + 1 < B:
                            prologue(b + 1, n + R * half)
                    if half:
                        for n in range(R, NS):
                            S.act_step(act, b, half, s0 + n, n, n % R)
                            if n % 2 == 0:
                                hi(n % R // 2, (s0 + n) // R)
                            if b + 1 < B:
                                prologue(b + 1, n + R)
                        return
                    with act.Fori(1, NS // R) as i:
                        for j in range(R):
                            S.act_step(act, b, half, R * i + (s0 + j), R * i + j, j)
                            if j % 2 == 0:
                                hi(j // 2, i + s0 // R)

                for at in range(AT):
                    prologue(0, at)
                for b in range(B):
                    scan(b, 0)
                    scan(b, 1)
                S.act_y(act, B - 1, 1)
                S.store_y(act, y_ssm, B - 1)

            @block.vector
            def _(dve):
                S.dve_start(dve)

                def prologue(b, at):
                    if at == 2 or at == 5:
                        for c in range(2):
                            S.dve_conv(dve, b, c + (2 if at == 5 else 0))
                    if at == 8:
                        S.dve_split(dve, b)
                    if at == 13:
                        S.dve_t(dve, b)
                    if at == 15:
                        S.dve_delta(dve, b)

                def lo(k, i):
                    dve.wait_ge(hi_rdy, 2 * i + (k + 1))
                    if not isinstance(i, int) or i:
                        dve.wait_ge(w_out[k], 32 * i)
                    nc.vector.scalar_tensor_tensor(out=wlo[:, k, :], in0=wst[:, k, :], scalar=WS, in1=whi[:, k, :],
                                                   op0=ALU.mult, op1=ALU.subtract).then_inc(lo_rdy, 1)

                def scan(b, half):
                    s0, p0 = b * STEPS + half * NS, (b * STEPS + half * NS) // 2
                    dve.wait_ge(S.d_step, 3 * (b + 1))
                    for n in range(R):
                        S.dve_step(dve, b, half, s0 + n, p0 + n // 2, n)
                        if n % 2:
                            lo(n // 2, s0 // R)
                        if b + 1 < B:
                            prologue(b + 1, n + R * half)
                    if half:
                        for n in range(R, NS):
                            S.dve_step(dve, b, half, s0 + n, p0 + n // 2, n % R)
                            if n % 2:
                                lo(n % R // 2, (s0 + n) // R)
                            if b + 1 < B:
                                prologue(b + 1, n + R)
                        return
                    with dve.Fori(1, NS // R) as i:
                        for j in range(R):
                            S.dve_step(dve, b, half, R * i + (s0 + j), (R // 2) * i + (p0 + j // 2), j)
                            if j % 2:
                                lo(j // 2, i + s0 // R)

                for at in range(AT):
                    prologue(0, at)
                for b in range(B):
                    scan(b, 0)
                    scan(b, 1)

            @block.gpsimd
            def _(pool):
                S.pool_start(pool)

                for n in range(R):
                    S.pool_step(pool, n, n)
                    if n % 2:
                        S.pool_pair(pool, n // 2, n - 1)
                with pool.Fori(1, B * STEPS // R) as i:
                    for j in range(R):
                        S.pool_step(pool, R * i + j, j)
                        if j % 2:
                            S.pool_pair(pool, (R // 2) * i + j // 2, j - 1)
        m.clear()


def gate(nc, l, d, X, y_ssm, r):
    with ExitStack() as ctx:
        m = Mem(nc, ctx, f"gate{l}")
        ident = m.sb("ident", [P, P])
        Y = m.sb("Y", [P, TT, L])
        xT = m.sb("xT", [P, 4, HK, P])
        st = m.sb("st", [P, 2, TT, 6])
        mv = m.sb("mv", [P, TT, 2])
        sd = m.sb("sd", [P, 2, TT])
        rstd = m.sb("rstd", [P, 2, TT])
        nmr = m.sb("nmr", [P, 2, TT])
        eps = m.sb("eps", [P, 1])
        G = m.sb("G", [P, TT, L])
        xn = m.sb("xn", [P, 4, H])
        wr = m.sb("wr", [P, HK, E + 1])
        pt = [m.ps(f"pt{i}", [P, KC, P]) for i in range(4)]
        pn = [m.ps(f"pn{i}", [P, HK, P]) for i in range(2)]
        plog = m.ps("plog", [P, TT, 32])

        loaded = m.sem("loaded")
        y_in = [m.sem(f"y_in{i}") for i in range(B)]
        eps_rdy = m.sem("eps_rdy")
        st_rdy = m.sem("st_rdy")
        mv_rdy = m.sem("mv_rdy")
        sd_rdy = m.sem("sd_rdy")
        rs_rdy = m.sem("rs_rdy")
        ln_rdy = m.sem("ln_rdy")
        g_rdy = m.sem("g_rdy")
        yg_rdy = m.sem("yg_rdy")
        tr_rdy = m.sem("tr_rdy")
        x_rdy = m.sem("x_rdy")
        xn_rdy = m.sem("xn_rdy")
        xn_out = [m.sem(f"xn_out{i}") for i in range(4)]
        tn_rdy = m.sem("tn_rdy")
        xT_rdy = m.sem("xT_rdy")
        lg_rdy = m.sem("lg_rdy")
        lg_out = m.sem("lg_out")

        with nc.Block() as block:

            @block.sync
            def _(sp):
                sp.dma_start(ident[:], d["ident"]).then_inc(loaded, 16)
                if l == 0:
                    sp.dma_start(wr[:], d["w_router"].rearrange("(k p) n -> p k n", p=P)).then_inc(loaded, 16)
                    for i in range(TT):
                        sp.wait_ge(xn_rdy, i + 1)
                        sp.dma_start(r["xn_d"][i * P:(i + 1) * P, :], xn[:, i % 4, :]).then_inc(xn_out[i % 4], 16)
                    for q in range(4):
                        sp.wait_ge(xn_out[q], 16 * TT // 4)

            NLOAD = 32 if l == 0 else 16

            @block.vector
            def _(dve):
                nc.vector.memset(eps[:], EPS).then_inc(eps_rdy, 1)
                for i in range(TT):
                    nc.vector.bn_stats(st[:, 0, i, :], X[:, i, :]).then_inc(st_rdy, 1)
                for i in range(TT):
                    dve.wait_ge(st_rdy, i + 1)
                    nc.vector.bn_aggr(mv[:, i, :], st[:, 0, i, :]).then_inc(mv_rdy, 1)
                dve.wait_ge(sd_rdy, 1)
                nc.vector.reciprocal(rstd[:, 0, :], sd[:, 0, :]).then_inc(rs_rdy, 1)
                dve.wait_ge(rs_rdy, 1)
                nc.vector.scalar_tensor_tensor(out=nmr[:, 0, :], in0=mv[:, :, 0], scalar=-1.0, in1=rstd[:, 0, :],
                                               op0=ALU.mult, op1=ALU.mult).then_inc(ln_rdy, 1)

                def add(b):
                    for c in range(KC):
                        i = b * KC + c
                        dve.wait_ge(tr_rdy, i + 1)
                        nc.vector.tensor_tensor(X[:, i, :], X[:, i, :], pt[i % 4][:].rearrange("p k t -> p (k t)"),
                                                ALU.add).then_inc(x_rdy, 1)
                    for c in range(KC):
                        i = b * KC + c
                        dve.wait_ge(x_rdy, i + 1)
                        nc.vector.bn_stats(st[:, 1, i, :], X[:, i, :]).then_inc(st_rdy, 1)
                    for c in range(KC):
                        i = b * KC + c
                        dve.wait_ge(st_rdy, TT + i + 1)
                        nc.vector.bn_aggr(r["mv"][:, i, :], st[:, 1, i, :]).then_inc(mv_rdy, 1)

                def layernorm(b):
                    own = slice(b * KC, (b + 1) * KC)
                    dve.wait_ge(sd_rdy, b + 2)
                    nc.vector.reciprocal(rstd[:, 1, own], sd[:, 1, own]).then_inc(rs_rdy, 1)
                    dve.wait_ge(rs_rdy, b + 2)
                    nc.vector.scalar_tensor_tensor(out=nmr[:, 1, own], in0=r["mv"][:, own, 0], scalar=-1.0,
                                                   in1=rstd[:, 1, own], op0=ALU.mult, op1=ALU.mult).then_inc(ln_rdy, 1)
                    dve.wait_ge(ln_rdy, b + 2)
                    for c in range(KC):
                        i = b * KC + c
                        if i >= 4:
                            dve.wait_ge(xn_out[i % 4], 16 * (i // 4))
                            dve.wait_ge(tn_rdy, i - 3)
                        nc.vector.tensor_scalar(xn[:, i % 4, :], X[:, i, :], rstd[:, 1, i:i + 1], nmr[:, 1, i:i + 1],
                                                ALU.mult, ALU.add).then_inc(xn_rdy, 1)

                add(0)
                add(1)
                for b in range(B):
                    if l == 0:
                        layernorm(b)
                    if b + 2 < B:
                        add(b + 2)

            @block.scalar
            def _(act):
                for b in range(B):
                    own = slice(b * KC, (b + 1) * KC)
                    act.dma_start(Y[:, own, :], y_ssm.rearrange("(i p) t -> p i t", p=P)[:, own, :]).then_inc(y_in[b], 16)
                act.wait_ge(eps_rdy, 1)
                act.wait_ge(mv_rdy, TT)
                nc.scalar.activation(sd[:, 0, :], mv[:, :, 1], ACT.Sqrt, bias=eps[:]).then_inc(sd_rdy, 1)
                act.wait_ge(ln_rdy, 1)

                for i in range(TT):
                    nc.scalar.activation(G[:, i, :], X[:, i, :], ACT.Silu, bias=nmr[:, 0, i:i + 1],
                                         scale=rstd[:, 0, i:i + 1]).then_inc(g_rdy, 1)

                def second(b):
                    own = slice(b * KC, (b + 1) * KC)
                    act.wait_ge(mv_rdy, TT + (b + 1) * KC)
                    nc.scalar.activation(sd[:, 1, own], r["mv"][:, own, 1], ACT.Sqrt, bias=eps[:]).then_inc(sd_rdy, 1)

                def evac(b):
                    for c in range(KC):
                        i = b * KC + c
                        act.wait_ge(tn_rdy, i + 1)
                        if i >= 4:
                            act.wait_ge(lg_rdy, i - 3)
                        nc.scalar.copy(xT[:, i % 4, :, :], pn[i % 2][:]).then_inc(xT_rdy, 1)

                if l == 0:
                    second(0)
                    second(1)
                    for b in range(B):
                        evac(b)
                        if b + 2 < B:
                            second(b + 2)
                    act.wait_ge(lg_rdy, TT)
                    nc.scalar.copy(r["logit"][:], plog[:, :, 0:E + 1]).then_inc(lg_out, 1)

            @block.gpsimd
            def _(pool):
                for i in range(TT):
                    pool.wait_ge(y_in[i // KC], 16)
                    pool.wait_ge(g_rdy, i + 1)
                    nc.gpsimd.tensor_tensor(Y[:, i, :], Y[:, i, :], G[:, i, :], ALU.mult).then_inc(yg_rdy, 1)

            @block.tensor
            def _(pe):
                pe.wait_ge(loaded, NLOAD)

                def y_transpose(b):
                    pe.wait_ge(yg_rdy, (b + 1) * KC)
                    for t in range(KC):
                        i = b * KC + t
                        if i >= 4:
                            pe.wait_ge(x_rdy, i - 3)
                        for c in range(KC):
                            tr = nc.tensor.transpose(pt[i % 4][:, c, :], Y[:, b * KC + c, t * P:(t + 1) * P], ident[:])
                        tr.then_inc(tr_rdy, 1)

                def router(b):
                    for t in range(KC):
                        i = b * KC + t
                        pe.wait_ge(xn_rdy, i + 1)
                        if i >= 2:
                            pe.wait_ge(xT_rdy, i - 1)
                        for k in range(HK):
                            tr = nc.tensor.transpose(pn[i % 2][:, k, :], xn[:, i % 4, k * P:(k + 1) * P], ident[:])
                        tr.then_inc(tn_rdy, 1)
                    for t in range(KC):
                        i = b * KC + t
                        pe.wait_ge(xT_rdy, i + 1)
                        for k in range(HK):
                            mm = nc.tensor.matmul(plog[:, i, 0:E + 1], xT[:, i % 4, k, :], wr[:, k, :],
                                                  start=(k == 0), stop=(k == HK - 1))
                        mm.then_inc(lg_rdy, 1)

                y_transpose(0)
                y_transpose(1)
                for b in range(B):
                    if b + 2 < B:
                        y_transpose(b + 2)
                    if l == 0:
                        router(b)
        m.clear()


def routing(nc, d, r):
    with ExitStack() as ctx:
        m = Mem(nc, ctx, "rt")
        tri = m.sb("tri", [P, P])
        ones = m.sb("ones", [P, P])
        e_of = m.sb("e_of", [P, E])
        thr = m.sb("thr", [P, TT])
        col = m.sb("col", [P, P])
        tok = m.sb("tok", [P, TT])
        ex = m.sb("ex", [P, TT, E])
        mx = m.sb("mx", [P, TT])
        sm = m.sb("sm", [P, TT])
        ri = m.sb("ri", [P, TT])
        i8 = m.sb("i8", [P, TT, 8], U32)
        idf = m.sb("idf", [P, TT, 8])
        oh = m.sb("oh", [P, TOPK, TT, E])
        M = m.sb("M", [P, TT, E])
        base = m.sb("base", [P, TT, E])
        cnt = m.sb("cnt", [P, TT, E])
        off = m.sb("off", [P, TT + 1, E])
        cmp = m.sb("cmp", [P, E, TT])
        nt = m.sb("nt", [P, E])
        incl = m.sb("incl", [P, E])
        start = m.sb("start", [P, E])
        one_e = m.sb("one_e", [P, E])
        pos = m.sb("pos", [P, TT, TOPK])
        posi = m.sb("posi", [P, TT, TOPK], I32)
        sti = m.sb("sti", [P, TT, TOPK], I32)
        stf = m.sb("stf", [P, TT, TOPK])
        pp = m.sb("pp", [P, TT, TOPK])
        ohp = m.sb("ohp", [P, 4, P])
        ohs = m.sb("ohs", [P, 4, NSTEP])
        turn = m.sb("turn", [1, E])
        scm = m.sb("scm", [1, NSTEP, E])
        se = m.sb("se", [1, NSTEP])
        ws = m.sb("ws", [1, NSTEP])
        pr_ = m.ps("pr", [P, TT * E])
        pc = m.ps("pc", [P, TT * E])
        pi = m.ps("pi", [P, NSTEP])

        loaded = m.sem("loaded")
        mx_rdy = m.sem("mx_rdy")
        e_rdy = m.sem("e_rdy")
        m_rdy = m.sem("m_rdy")
        rk_rdy = m.sem("rk_rdy")
        oh_rdy = m.sem("oh_rdy")
        oh_used = m.sem("oh_used")
        step = m.sem("step")
        fin = m.sem("fin")

        with nc.Block() as block:
            @block.sync
            def _(sp):
                for dst, n in [(tri, "tri"), (ones, "ones"), (e_of, "e_of"), (thr, "thr"), (col, "col"), (tok, "tok")]:
                    sp.dma_start(dst[:], d[n]).then_inc(loaded, 16)
                sp.dma_start(turn[:], d["turn"]).then_inc(loaded, 16)
                sp.dma_start(r["first"][:], d["first"]).then_inc(loaded, 16)
                sp.dma_start(r["tab"][:], d["tab"]).then_inc(loaded, 16)

            @block.scalar
            def _(act):
                act.wait_ge(mx_rdy, 1)
                nc.scalar.activation(ex[:], ex[:], ACT.Exp).then_inc(e_rdy, 1)
                nc.scalar.activation(r["sig"][:], r["logit"][:, :, E], ACT.Sigmoid).then_inc(fin, 1)

            @block.vector
            def _(dve):
                n = [0]

                def own(ins):
                    ins.then_inc(step, 1)
                    n[0] += 1
                    dve.wait_ge(step, n[0])

                V = nc.vector
                logit = r["logit"][:, :, 0:E]
                dve.wait_ge(loaded, 144)
                own(V.reduce_max(mx[:], logit, AX.X))
                V.tensor_tensor(ex[:], logit, mx[:].unsqueeze(2).to_broadcast([P, TT, E]), ALU.subtract).then_inc(mx_rdy, 1)
                dve.wait_ge(e_rdy, 1)
                own(V.reduce_sum(sm[:], ex[:], AX.X))
                own(V.reciprocal(ri[:], sm[:]))
                own(V.tensor_tensor(ex[:], ex[:], ri[:].unsqueeze(2).to_broadcast([P, TT, E]), ALU.mult))
                for i in range(TT):
                    mxi = V.max(r["w8"][:, i, :], ex[:, i, :])
                own(mxi)
                for i in range(TT):
                    mxi = V.max_index(i8[:, i, :], r["w8"][:, i, :], ex[:, i, :])
                own(mxi)
                own(V.tensor_copy(idf[:], i8[:]))
                for k in range(TOPK):
                    q = V.tensor_tensor(oh[:, k, :, :], e_of[:].unsqueeze(1).to_broadcast([P, TT, E]),
                                        idf[:, :, k:k + 1].to_broadcast([P, TT, E]), ALU.is_equal)
                own(q)
                own(V.tensor_tensor(M[:], oh[:, 0, :, :], oh[:, 1, :, :], ALU.add))
                own(V.tensor_tensor(M[:], M[:], oh[:, 2, :, :], ALU.add))
                own(V.tensor_tensor(M[:], M[:], oh[:, 3, :, :], ALU.add))
                V.memset(one_e[:], 1.0).then_inc(m_rdy, 1)
                own(V.memset(off[:, 0, :], 0.0))
                dve.wait_ge(rk_rdy, 2)
                own(V.tensor_copy(cnt[:].rearrange("p t e -> p (t e)"), pc[:]))
                for i in range(TT):
                    own(V.tensor_tensor(off[:, i + 1, :], off[:, i, :], cnt[:, i, :], ALU.add))
                own(V.tensor_tensor(cmp[:], off[:, TT, :].unsqueeze(2).to_broadcast([P, E, TT]),
                                    thr[:].unsqueeze(1).to_broadcast([P, E, TT]), ALU.is_gt))
                own(V.reduce_sum(nt[:], cmp[:], AX.X))
                own(V.tensor_scalar(nt[:], nt[:], 1.0, None, ALU.max))
                own(V.tensor_tensor_scan(incl[:], one_e[:], nt[:], 0.0, ALU.mult, ALU.add))
                own(V.tensor_tensor(start[:], incl[:], nt[:], ALU.subtract))
                own(V.scalar_tensor_tensor(out=base[:], in0=start[:].unsqueeze(1).to_broadcast([P, TT, E]), scalar=float(P),
                                           in1=off[:, 0:TT, :], op0=ALU.mult, op1=ALU.add))
                own(V.tensor_tensor(base[:], base[:], pr_[:].rearrange("p (t e) -> p t e", e=E), ALU.add))
                for k in range(TOPK):
                    q = V.tensor_tensor(oh[:, k, :, :], oh[:, k, :, :], base[:], ALU.mult)
                own(q)
                for k in range(TOPK):
                    q = V.reduce_sum(pos[:, :, k], oh[:, k, :, :], AX.X)
                own(q)
                V.tensor_copy(r["pos"][:], pos[:])
                own(V.tensor_copy(posi[:], pos[:]))
                own(V.tensor_scalar(sti[:], posi[:], 7, None, ALU.arith_shift_right))
                own(V.tensor_scalar(posi[:], posi[:], P - 1, None, ALU.bitwise_and))
                V.tensor_copy(stf[:], sti[:])
                own(V.tensor_copy(pp[:], posi[:]))
                for g in range(TT * TOPK):
                    i, k = g // TOPK, g % TOPK
                    if g >= 4:
                        dve.wait_ge(oh_used, g - 3)
                    V.tensor_scalar(ohp[:, g % 4, :], col[:], pp[:, i, k:k + 1], None, ALU.is_equal)
                    V.tensor_scalar(ohs[:, g % 4, :], col[:, 0:NSTEP], stf[:, i, k:k + 1], tok[:, i:i + 1],
                                    ALU.is_equal, ALU.mult).then_inc(oh_rdy, 1)
                own(V.tensor_tensor(scm[:], start[0:1, :].unsqueeze(1).to_broadcast([1, NSTEP, E]),
                                    col[0:1, 0:NSTEP].unsqueeze(2).to_broadcast([1, NSTEP, E]), ALU.is_le))
                own(V.reduce_sum(se[:], scm[:], AX.X))
                V.tensor_scalar(r["tab"][0:1, 0, NA:NALL], se[:], float(NSH), None, ALU.add)
                V.tensor_scalar(r["first"][0:1, NSH:NEX], start[0:1, :], float(NA), None, ALU.add)
                own(V.tensor_tensor(scm[:], scm[:], turn[:].unsqueeze(1).to_broadcast([1, NSTEP, E]), ALU.mult))
                own(V.reduce_sum(ws[:], scm[:], AX.X))
                own(V.tensor_copy(r["tab"][0:1, 1, NA:NALL], ws[:]))
                for q in range(NSH):
                    V.tensor_copy(r["idx"][:, q * TT:(q + 1) * TT], tok[:])
                dve.wait_ge(oh_used, TT * TOPK)
                own(V.tensor_copy(r["idx"][:, NA:NALL], pi[:]))

            @block.tensor
            def _(pe):
                pe.wait_ge(loaded, 144)
                pe.wait_ge(m_rdy, 1)
                Mf = M[:].rearrange("p t e -> p (t e)")
                nc.tensor.matmul(pr_[:], tri[:], Mf, start=True, stop=True).then_inc(rk_rdy, 1)
                nc.tensor.matmul(pc[:], ones[:], Mf, start=True, stop=True).then_inc(rk_rdy, 1)
                G = TT * TOPK
                for g in range(G):
                    pe.wait_ge(oh_rdy, g + 1)
                    nc.tensor.matmul(pi[:], ohp[:, g % 4, :], ohs[:, g % 4, :], start=(g == 0),
                                     stop=(g == G - 1)).then_inc(oh_used, 1)


def experts_and_ssm(nc, d, r, X, y_ssm):
    with ExitStack() as ctx:
        m = Mem(nc, ctx, "moe")
        S = Ssm(nc, m, 1, d, dbl=1, nb=1, ny=0, ring=2, alone=False)
        ident = S.ident
        Wh = m.sb("Wh", [P, WR, WE], F16)
        Wl = m.sb("Wl", [P, WR, WE], F16)
        xg = m.sb("xg", [P, 2, H])
        ist = m.sb("ist", [P, 2], U32)
        xth = m.sb("xth", [P, HK, P], F16)
        xtl = m.sb("xtl", [P, HK, P], F16)
        sg = m.sb("sg", [P, IE])
        hh = m.sb("hh", [P, IE])
        hth = m.sb("hth", [P, 3, P], F16)
        htl = m.sb("htl", [P, 3, P], F16)
        yo = m.sb("yo", [P, 2, H])
        sigs = m.sb("sigs", [P, TT])
        px = m.ps("px", [P, HK, P])
        ph = m.ps("ph", [P, 3, P])
        pg = m.ps("pg", [P, IE])
        pu = m.ps("pu", [P, IE])
        py = m.ps("py", [P, H])

        w_in = m.sem("w_in")
        w_free = m.sem("w_free")
        w_rdy = m.sem("w_rdy")
        xg_in = [m.sem(f"xg_in{i}") for i in range(2)]
        ix_rdy = m.sem("ix_rdy")
        ix_seen = m.sem("ix_seen")
        tx_rdy = m.sem("tx_rdy")
        xh_rdy = m.sem("xh_rdy")
        xl_rdy = m.sem("xl_rdy")
        gu_rdy = m.sem("gu_rdy")
        sg_rdy = m.sem("sg_rdy")
        gt_rdy = m.sem("gt_rdy")
        hh_rdy = m.sem("hh_rdy")
        th_rdy = m.sem("th_rdy")
        hth_rdy = m.sem("hth_rdy")
        htl_rdy = m.sem("htl_rdy")
        y_rdy = m.sem("y_rdy")
        py_read = m.sem("py_read")
        y_st = [m.sem(f"y_st{i}") for i in range(2)]
        sg_scl = m.sem("sg_scl")

        PRO = 4
        PER = PRO + STEPS
        assert B * PER == NALL

        def halves(eng, one, b, h):
            g0, s0 = b * PER + PRO + h * NS, b * STEPS + h * NS
            change = g0 + R - 2 < NA <= g0 + NS - 3
            for n in range(NS if change else R):
                one(h, g0 + n, (g0 + n) // 2, s0 + n, (s0 + n) // 2, n, n % R, g0 + n - 2 >= NA)
            if change:
                return
            with eng.Fori(1, NS // R) as i:
                for j in range(R):
                    one(h, R * i + (g0 + j), (R // 2) * i + (g0 + j) // 2, R * i + (s0 + j),
                        (R // 2) * i + (s0 + j) // 2, R * i + j, j, g0 + R - 2 >= NA)

        with nc.Block() as block:

            @block.sync
            def _(sp):
                S.load(sp)
                S.load_ctx(sp, 0)

                for n in range(NEX):
                    e = E + n if n < NSH else n - NSH
                    if n >= WR:
                        f = sp.value_load(r["first"][0:1, n - WR + 1:n - WR + 2], min_val=1, max_val=NALL)
                        sp.wait_ge(y_rdy, f)
                        sp.sem_inc(w_free, 1)
                    elif n:
                        sp.wait_ge(y_rdy, 1)
                    for W, src in ((Wh, d["w_hi"]), (Wl, d["w_lo"])):
                        sp.dma_start(W[:, n % WR, :], src[:, e * WE:(e + 1) * WE]).then_inc(w_in, 16)
                    sp.wait_ge(w_in, 32 * (n + 1))
                    sp.sem_inc(w_rdy, 1)
                sp.wait_ge(S.y_dram, 16 * B)

            @block.gpsimd
            def _(pool):
                S.pool_start(pool)

                def fetch(g, j):
                    nc.gpsimd.tensor_copy(ist[:, j:j + 1], r["idx"][:, ds(g, 1)]).then_inc(ix_rdy, 1)
                    pool.wait_ge(ix_rdy, g + 1)
                    pool.sem_inc(ix_seen, 1)
                    nc.gpsimd.indirect_dma_start(
                        out=xg[:, j, :], out_offset=None, in_=r["xn_d"],
                        in_offset=bass.IndirectOffsetOnAxis(ap=ist[:, j:j + 1], axis=0)).then_inc(xg_in[j], 16)

                def ahead(g, j):
                    pool.wait_ge(tx_rdy, g + 1)
                    fetch(g + 2, j)

                for g in range(2):
                    fetch(g, g)
                for b in range(B):
                    def one(half, g, g2, s, p, n, j, routed):
                        if not isinstance(g, int) or g + 2 < NALL:
                            ahead(g, j % 2)
                        if isinstance(n, int) and s == b * STEPS:
                            S.pool_y_init(pool, b)
                        if not (isinstance(n, int) and s == b * STEPS):
                            last = 0 if isinstance(n, int) and n == 0 else half
                            S.pool_add(pool, b, last, s - 1, (j - 1) % R)
                        S.pool_step(pool, s, j)

                    for g in range(b * PER, b * PER + PRO):
                        ahead(g, g % 2)
                    halves(pool, one, b, 0)
                    if b + 1 < B:
                        halves(pool, one, b, 1)
                    else:
                        for n in range(NS):
                            one(1, NALL - NS + n, None, B * STEPS - NS + n, None, n, n % R, True)
                    S.pool_add(pool, b, 1, (b + 1) * STEPS - 1, R - 1)

            @block.tensor
            def _(pe):
                def w_of(W, w, k, o, n):
                    return W[0:k, ds(w, 1), o:o + n].rearrange("p o n -> p (o n)")

                def slot_of(g):
                    return pe.value_load(r["tab"][0:1, 1, ds(g, 1)], min_val=0, max_val=WR - 1)

                def x_transpose(g, g2, j):
                    pe.wait_ge(xg_in[j], 16 * g2 + 16)
                    if not isinstance(g, int) or g:
                        pe.wait_ge(xl_rdy, g)
                    for k in range(HK):
                        tr = nc.tensor.transpose(px[:, k, :], xg[:, j, k * P:(k + 1) * P], ident[:])
                    tr.then_inc(tx_rdy, 1)

                def down(g):
                    w, o = slot_of(g), HK * 2 * IE
                    pe.wait_ge(htl_rdy, g + 1)
                    if not isinstance(g, int) or g:
                        pe.wait_ge(py_read, g)
                    for q, (_, n) in enumerate(ICH):
                        for z, (ht, W) in enumerate(((hth, Wh), (hth, Wl), (htl, Wh))):
                            mm = nc.tensor.matmul(py[:], ht[0:n, q, :], w_of(W, w, n, o + q * H, H),
                                                  start=(q == 0 and z == 0), stop=(q == 2 and z == 2))
                    mm.then_inc(y_rdy, 1)

                def h_transpose(g):
                    pe.wait_ge(hh_rdy, g + 1)
                    if not isinstance(g, int) or g:
                        pe.wait_ge(htl_rdy, g)
                    for q, (o, n) in enumerate(ICH):
                        tr = nc.tensor.transpose(ph[0:n, q, :], hh[:, o:o + n], ident[:])
                    tr.then_inc(th_rdy, 1)

                def up(g):
                    w = slot_of(g)
                    n = pe.value_load(r["tab"][0:1, 0, ds(g, 1)], min_val=1, max_val=NEX)
                    pe.wait_ge(xl_rdy, g + 1)
                    pe.wait_ge(w_rdy, n)
                    for k in range(HK):
                        for xt, W, z in ((xth, Wh, 0), (xth, Wl, 1), (xtl, Wh, 2)):
                            for ps, o in ((pg, 0), (pu, IE)):
                                mm = nc.tensor.matmul(ps[:], xt[:, k, :], w_of(W, w, P, k * 2 * IE + o, IE),
                                                      start=(k == 0 and z == 0), stop=(k == HK - 1 and z == 2))
                    mm.then_inc(gu_rdy, 1)

                def down_before(g):
                    if not isinstance(g, int) or g >= 2:
                        down(g - 2)

                def second(g):
                    if not isinstance(g, int) or g >= 1:
                        h_transpose(g - 1)
                    up(g)

                S.pe_start(pe)
                for b in range(B):
                    for at in range(PRO):
                        g = b * PER + at
                        x_transpose(g, g // 2, g % 2)
                        down_before(g)
                        if at == 0:
                            S.pe_in(pe, b, 0)
                            S.pe_in(pe, b, 1)
                        if at == 2:
                            S.pe_x(pe, b)
                        if at == 3:
                            S.pe_dt(pe, b, 0)
                            S.pe_dt(pe, b, 1)
                        second(g)
                        if at == 0:
                            S.pe_in(pe, b, 2)
                            S.pe_in(pe, b, 3)
                        if at == 3:
                            S.pe_dt(pe, b, 2)
                            S.pe_dt(pe, b, 3)

                    def one(h, g, g2, s, p, n, j, routed):
                        x_transpose(g, g2, j % 2)
                        if isinstance(n, int) and s == b * STEPS:
                            pe.wait_ge(S.ar_rdy, (b + 1) * KC)
                        S.pe_spread(pe, b, s, n, j)
                        down_before(g)
                        second(g)

                    for h in range(2):
                        halves(pe, one, b, h)
                down(NALL - 2)
                h_transpose(NALL - 1)
                down(NALL - 1)

            @block.scalar
            def _(act):
                def x_hi(g):
                    act.wait_ge(tx_rdy, g + 1)
                    nc.scalar.activation(xth[:], px[:], ACT.Copy, scale=XS).then_inc(xh_rdy, 1)

                def h_hi(g):
                    act.wait_ge(th_rdy, g + 1)
                    nc.scalar.copy(hth[:, 0:2, :], ph[:, 0:2, :])
                    nc.scalar.copy(hth[0:96, 2, :], ph[0:96, 2, :]).then_inc(hth_rdy, 1)

                def tanh(g):
                    act.wait_ge(gu_rdy, g + 1)
                    nc.scalar.activation(sg[:], pg[:], ACT.Tanh, scale=0.5 / (XS * WS)).then_inc(sg_rdy, 1)

                def y_store(g, j):
                    act.wait_ge(py_read, g + 1)
                    act.dma_start(r["y_d"][ds(g * P - NA * P, P), :], yo[:, j, :]).then_inc(y_st[j], 16)

                def late(g, j, routed):
                    if not isinstance(g, int) or g >= 1:
                        h_hi(g - 1)
                    tanh(g)
                    if routed:
                        y_store(g - 2, j)

                S.act_start(act)
                for b in range(B):
                    for at in range(PRO):
                        g = b * PER + at
                        x_hi(g)
                        if at == 0:
                            if b:
                                S.store_y(act, y_ssm, b - 1)
                            S.act_conv(act, b, 0)
                            S.act_conv(act, b, 1)
                        if at == 1:
                            S.act_conv(act, b, 2)
                            S.act_conv(act, b, 3)
                            if b + 1 < B:
                                S.load_ctx(act, b + 1)
                        if at == 3:
                            S.act_z(act, b, 0)
                            S.act_z(act, b, 1)
                        late(g, g % 2, g - 2 >= NA)
                        if at == 1:
                            S.act_u(act, b)
                        if at == 2:
                            S.act_dt(act, b)
                        if at == 3:
                            S.act_z(act, b, 2)
                            S.act_z(act, b, 3)
                            S.act_e(act, b)
                            S.act_ln(act, b)

                    def one(h, g, g2, s, p, n, j, routed):
                        x_hi(g)
                        if isinstance(n, int) and s == b * STEPS:
                            act.wait_ge(S.d_step, 3 * (b + 1))
                        S.act_step(act, b, h, s, n, j)
                        late(g, j % 2, routed)

                    halves(act, one, b, 0)
                    halves(act, one, b, 1)
                h_hi(NALL - 1)
                for j in range(2):
                    y_store(NALL - 2 + j, j)
                S.store_y(act, y_ssm, B - 1)
                for j in range(2):
                    act.wait_ge(y_st[j], 16 * NSTEP // 2)

            @block.vector
            def _(dve):
                def x_lo(g):
                    dve.wait_ge(xh_rdy, g + 1)
                    nc.vector.scalar_tensor_tensor(out=xtl[:], in0=px[:], scalar=XS, in1=xth[:],
                                                   op0=ALU.mult, op1=ALU.subtract).then_inc(xl_rdy, 1)

                def h_lo(g):
                    dve.wait_ge(hth_rdy, g + 1)
                    nc.vector.tensor_tensor(htl[:, 0:2, :], ph[:, 0:2, :], hth[:, 0:2, :], ALU.subtract)
                    nc.vector.tensor_tensor(htl[0:96, 2, :], ph[0:96, 2, :], hth[0:96, 2, :], ALU.subtract)\
                      .then_inc(htl_rdy, 1)

                def silu_up(g):
                    dve.wait_ge(sg_rdy, g + 1)
                    nc.vector.scalar_tensor_tensor(out=sg[:], in0=sg[:], scalar=1.0, in1=pg[:],
                                                   op0=ALU.add, op1=ALU.mult).then_inc(gt_rdy, 1)
                    dve.wait_ge(gt_rdy, g + 1)
                    nc.vector.scalar_tensor_tensor(out=hh[:], in0=pu[:], scalar=0.5 * HS / (XS * WS) ** 2, in1=sg[:],
                                                   op0=ALU.mult, op1=ALU.mult).then_inc(hh_rdy, 1)

                def y(g, g2, j, routed):
                    if not routed:
                        t = dve.value_load(r["tab"][0:1, 2, ds(g, 1)], min_val=0, max_val=TT - 1)
                    dve.wait_ge(y_rdy, g + 1)
                    if routed:
                        if not isinstance(g, int) or g >= NA + 2:
                            dve.wait_ge(y_st[j], 16 * g2 - 16 * (NA // 2))
                        nc.vector.tensor_scalar(yo[:, j, :], py[:], 1.0 / (HS * WS), None, ALU.mult).then_inc(py_read, 1)
                        return
                    if not isinstance(g, int) or g:
                        dve.wait_ge(py_read, g)
                    xs = X[:, ds(t, 1), :].rearrange("p o n -> p (o n)")
                    nc.vector.scalar_tensor_tensor(out=xs, in0=py[:], scalar=sigs[:, ds(t, 1)], in1=xs,
                                                   op0=ALU.mult, op1=ALU.add).then_inc(py_read, 1)

                def y_before(g, g2, j, routed):
                    if not isinstance(g, int) or g >= 2:
                        y(g - 2, g2 - 1, j, routed)

                nc.vector.tensor_scalar(sigs[:], r["sig"][:], 1.0 / (HS * WS), None, ALU.mult).then_inc(sg_scl, 1)
                S.dve_start(dve)
                dve.wait_ge(sg_scl, 1)
                for b in range(B):
                    for at in range(PRO):
                        g = b * PER + at
                        x_lo(g)
                        y_before(g, g // 2, g % 2, g - 2 >= NA)
                        if at == 0:
                            S.dve_conv(dve, b, 0)
                            S.dve_conv(dve, b, 1)
                        if at == 1:
                            S.dve_conv(dve, b, 2)
                            S.dve_conv(dve, b, 3)
                        if g:
                            h_lo(g - 1)
                        silu_up(g)
                        if at == 2:
                            S.dve_split(dve, b)
                        if at == 3:
                            S.dve_t(dve, b)
                            S.dve_delta(dve, b)

                    def one(half, g, g2, s, p, n, j, routed):
                        x_lo(g)
                        S.dve_step(dve, b, half, s, p, j)
                        y_before(g, g2, j % 2, routed)
                        h_lo(g - 1)
                        silu_up(g)

                    halves(dve, one, b, 0)
                    halves(dve, one, b, 1)
                for j in range(2):
                    g = NALL - 2 + j
                    if j:
                        h_lo(g)
                    y(g, g // 2, j, True)
        m.clear()


def combine(nc, d, r, X, Wq, wsc):
    with ExitStack() as ctx:
        m = Mem(nc, ctx, "comb")
        NR = 8
        NP = 3 * 4
        yr = m.sb("yr", [P, NR, H])
        W = m.sb("W", [P, NP, IF])
        ones = m.sb("ones", [P, P])
        wsum = m.sb("wsum", [P, 3, 4])
        wtot = m.sb("wtot", [P, 3])
        inv = m.sb("inv", [P, 3])
        rnd = m.sb("rnd", [P, 2])
        pa = m.ps("pa", [P, 4])

        got = [m.sem(f"got{i}") for i in range(NR)]
        used = m.sem("used")
        w_in = [m.sem(f"w_in{i}") for i in range(NP)]
        ones_in = m.sem("ones_in")
        abs_rdy = m.sem("abs_rdy")
        tot_rdy = m.sem("tot_rdy")
        all_rdy = m.sem("all_rdy")
        sc_rdy = m.sem("sc_rdy")
        rnd_rdy = m.sem("rnd_rdy")
        up_rdy = m.sem("up_rdy")
        clip_rdy = m.sem("clip_rdy")
        wq_rdy = m.sem("wq_rdy")

        src = [d[n].rearrange("(k p) n -> k p n", p=P)[k] for n in ("w_gate", "w_up") for k in range(4)]
        src += [d["w_down"].rearrange("(g k p) n -> g p k n", k=4, p=P)[k] for k in range(4)]

        with nc.Block() as block:
            @block.sync
            def _(sp):
                sp.dma_start(ones[:], d["ones"]).then_inc(ones_in, 16)
                for n in range(NP):
                    dst = W[:, n, :] if n < 8 else W[:, n, :].rearrange("p (k n) -> p k n", k=4)
                    sp.dma_start(dst, src[n]).then_inc(w_in[n], 16)

            @block.gpsimd
            def _(pool):
                for g in range(TT * TOPK):
                    i, k = g // TOPK, g % TOPK
                    if g >= NR:
                        pool.wait_ge(used, g - NR + 1)
                    nc.gpsimd.indirect_dma_start(
                        out=yr[:, g % NR, :], out_offset=None, in_=r["y_d"],
                        in_offset=bass.IndirectOffsetOnAxis(ap=r["pos"][:, i, k:k + 1], axis=0)).then_inc(got[g % NR], 16)

            @block.tensor
            def _(pe):
                pe.wait_ge(ones_in, 16)
                pe.wait_ge(tot_rdy, 1)
                nc.tensor.matmul(pa[:, 0:3], ones[:], wtot[:], start=True, stop=True).then_inc(all_rdy, 1)

            @block.scalar
            def _(act):
                def up(n):
                    nc.scalar.activation(W[:, n, :], W[:, n, :], ACT.Identity, bias=rnd[:, 0:1],
                                         scale=inv[:, n // 4:n // 4 + 1]).then_inc(up_rdy, 1)

                act.wait_ge(rnd_rdy, 2)
                act.wait_ge(sc_rdy, 2)
                up(0)
                for n in range(NP):
                    if n + 1 < NP:
                        up(n + 1)
                    act.wait_ge(clip_rdy, n + 1)
                    nc.scalar.activation(Wq[n // 4][:, n % 4, :], W[:, n, :], ACT.Identity,
                                         bias=rnd[:, 1:2]).then_inc(wq_rdy, 1)

            @block.vector
            def _(dve):
                V = nc.vector
                V.memset(rnd[:, 0:1], ROUND).then_inc(rnd_rdy, 1)
                V.memset(rnd[:, 1:2], -ROUND).then_inc(rnd_rdy, 1)

                def magnitude(n):
                    dve.wait_ge(w_in[n], 16)
                    V.tensor_reduce(wsum[:, n // 4, n % 4:n % 4 + 1], W[:, n, :], AX.X, ALU.add,
                                    apply_absolute_value=True).then_inc(abs_rdy, 1)

                def total():
                    dve.wait_ge(abs_rdy, NP)
                    V.reduce_sum(wtot[:], wsum[:], AX.X).then_inc(tot_rdy, 1)

                def scales():
                    dve.wait_ge(all_rdy, 1)
                    V.tensor_scalar(wsc[:], pa[:, 0:3], 1.0 / (H * IF), EPS, ALU.mult, ALU.add).then_inc(sc_rdy, 1)
                    dve.wait_ge(sc_rdy, 1)
                    V.reciprocal(inv[:], wsc[:]).then_inc(sc_rdy, 1)

                def clip(n):
                    dve.wait_ge(up_rdy, n + 1)
                    V.tensor_scalar(W[:, n, :], W[:, n, :], ROUND + 1.0, ROUND - 1.0, ALU.min, ALU.max).then_inc(clip_rdy, 1)

                for g in range(TT * TOPK):
                    i, k = g // TOPK, g % TOPK
                    dve.wait_ge(got[g % NR], 16 * (g // NR + 1))
                    if k:
                        dve.wait_ge(used, g)
                    V.scalar_tensor_tensor(out=X[:, i, :], in0=yr[:, g % NR, :], scalar=r["w8"][:, i, k:k + 1],
                                           in1=X[:, i, :], op0=ALU.mult, op1=ALU.add).then_inc(used, 1)
                    if 1 <= g <= NP:
                        magnitude(g - 1)
                    if g == NP:
                        total()
                    if g == NP + 2:
                        scales()
                    if NP + 4 <= g < 4 * NP + 4 and g % 3 == 1:
                        clip((g - NP - 4) // 3)
        m.clear()


def quant_ffn(nc, d, r, X, Wq, wsc, out):
    with ExitStack() as ctx:
        m = Mem(nc, ctx, "ffn")
        ident = m.sb("ident", [P, P], BF16)
        eps = m.sb("eps", [P, 1])
        mv = r["mv"]
        sd = m.sb("sd", [P, TT])
        rstd = m.sb("rstd", [P, TT])
        nmr = m.sb("nmr", [P, TT])
        xn = m.sb("xn", [P, 2, H])
        xq = m.sb("xq", [P, 2, H], BF16)
        xqT = m.sb("xqT", [P, 2, HK, P], BF16)
        sx = m.sb("sx", [P, TT, 5])
        hm = m.sb("hm", [P, 2, FC])
        rnd = m.sb("rnd", [P, 1])
        sh = m.sb("sh", [P, TT, 4])
        gg = m.sb("gg", [P, 2, IF])
        hq = m.sb("hq", [P, 2, IF], BF16)
        hqT = m.sb("hqT", [P, 2, FK, P], BF16)
        pg = [m.ps(f"pg{i}", [P, 512]) for i in range(2)]
        pu = [m.ps(f"pu{i}", [P, 512]) for i in range(2)]
        pt = [m.ps(f"pt{i}", [P, 8, P], BF16) for i in range(2)]
        pd = m.ps("pd", [P, H])

        loaded = m.sem("loaded")
        eps_rdy = m.sem("eps_rdy")
        sd_rdy = m.sem("sd_rdy")
        ln_rdy = m.sem("ln_rdy")
        step = m.sem("step")
        xn_rdy = m.sem("xn_rdy")
        rnd_set = m.sem("rnd_set")
        xs_rdy = m.sem("xs_rdy")
        xr_rdy = m.sem("xr_rdy")
        xq_rdy = m.sem("xq_rdy")
        tx_rdy = m.sem("tx_rdy")
        xqT_rdy = m.sem("xqT_rdy")
        gu_rdy = m.sem("gu_rdy")
        sg_rdy = m.sem("sg_rdy")
        gh_rdy = m.sem("gh_rdy")
        mx_rdy = m.sem("mx_rdy")
        s_rdy = m.sem("s_rdy")
        rnd_rdy = m.sem("rnd_rdy")
        hq_rdy = m.sem("hq_rdy")
        th_rdy = m.sem("th_rdy")
        hqT_rdy = m.sem("hqT_rdy")
        dn_rdy = m.sem("dn_rdy")
        x_rdy = m.sem("x_rdy")
        o_out = m.sem("o_out")

        with nc.Block() as block:

            @block.sync
            def _(sp):
                sp.dma_start(ident[:], d["ident_bf"]).then_inc(loaded, 16)
                for i in range(TT):
                    sp.wait_ge(x_rdy, i + 1)
                    sp.dma_start(out[i * P:(i + 1) * P, :], X[:, i, :]).then_inc(o_out, 16)
                sp.wait_ge(o_out, 16 * TT)

            @block.vector
            def _(dve):
                V = nc.vector
                n = [0]

                def own(ins):
                    ins.then_inc(step, 1)
                    n[0] += 1
                    dve.wait_ge(step, n[0])

                V.memset(rnd[:], ROUND).then_inc(rnd_set, 1)
                V.memset(eps[:], EPS).then_inc(eps_rdy, 1)
                dve.wait_ge(sd_rdy, 1)
                own(V.reciprocal(rstd[:], sd[:]))
                V.scalar_tensor_tensor(out=nmr[:], in0=mv[:, :, 0], scalar=-1.0, in1=rstd[:], op0=ALU.mult,
                                       op1=ALU.mult).then_inc(ln_rdy, 1)

                def x_scale(i):
                    s = sx[:, i, :]
                    dve.wait_ge(xn_rdy, i + 1)
                    own(V.tensor_reduce(s[:, 0:1], xn[:, i % 2, :], AX.X, ALU.max, apply_absolute_value=True))
                    own(V.tensor_scalar(s[:, 1:2], s[:, 0:1], 1.0 / 127.0, EPS, ALU.mult, ALU.add))
                    V.tensor_scalar(s[:, 3:4], s[:, 1:2], wsc[:, 0:1], None, ALU.mult)
                    V.tensor_scalar(s[:, 4:5], s[:, 1:2], wsc[:, 1:2], None, ALU.mult)
                    V.reciprocal(s[:, 2:3], s[:, 1:2]).then_inc(xs_rdy, 1)

                def add(i):
                    dve.wait_ge(dn_rdy, i + 1)
                    V.scalar_tensor_tensor(out=X[:, i, :], in0=pd[:], scalar=sh[:, i, 3:4], in1=X[:, i, :],
                                           op0=ALU.mult, op1=ALU.add).then_inc(x_rdy, 1)

                x_scale(0)
                x_scale(1)
                for i in range(TT):
                    dve.wait_ge(xs_rdy, i + 1)
                    for f in range(FC):
                        g, own_f = i * FC + f, gg[:, i % 2, f * 512:(f + 1) * 512]
                        dve.wait_ge(sg_rdy, g + 1)
                        V.scalar_tensor_tensor(out=own_f, in0=pu[g % 2][:], scalar=sx[:, i, 4:5], in1=own_f,
                                               op0=ALU.mult, op1=ALU.mult).then_inc(gh_rdy, 1)
                        dve.wait_ge(gh_rdy, g + 1)
                        V.tensor_reduce(hm[:, i % 2, f:f + 1], own_f, AX.X, ALU.max,
                                        apply_absolute_value=True).then_inc(mx_rdy, 1)
                    s = sh[:, i, :]
                    dve.wait_ge(mx_rdy, (i + 1) * FC)
                    own(V.reduce_max(s[:, 0:1], hm[:, i % 2, :], AX.X))
                    own(V.tensor_scalar(s[:, 1:2], s[:, 0:1], 1.0 / 127.0, EPS, ALU.mult, ALU.add))
                    V.tensor_scalar(s[:, 3:4], s[:, 1:2], wsc[:, 2:3], None, ALU.mult)
                    V.reciprocal(s[:, 2:3], s[:, 1:2]).then_inc(s_rdy, 1)
                    if i + 2 < TT:
                        x_scale(i + 2)
                    if i >= 2:
                        dve.wait_ge(th_rdy, 2 * (i - 1))
                    for a in range(2):
                        half = slice(a * IF // 2, (a + 1) * IF // 2)
                        dve.wait_ge(rnd_rdy, 2 * i + a + 1)
                        V.tensor_scalar(hq[:, i % 2, half], gg[:, i % 2, half], -ROUND, 127.0, ALU.add,
                                        ALU.min).then_inc(hq_rdy, 1)
                    if i:
                        add(i - 1)
                add(TT - 1)

            @block.scalar
            def _(act):
                act.wait_ge(eps_rdy, 1)
                nc.scalar.activation(sd[:], mv[:, :, 1], ACT.Sqrt, bias=eps[:]).then_inc(sd_rdy, 1)
                act.wait_ge(ln_rdy, 1)

                def layernorm(i):
                    if i >= 2:
                        act.wait_ge(xq_rdy, i - 1)
                    nc.scalar.activation(xn[:, i % 2, :], X[:, i, :], ACT.Identity, bias=nmr[:, i:i + 1],
                                         scale=rstd[:, i:i + 1]).then_inc(xn_rdy, 1)

                def x_round(i):
                    xi = xn[:, i % 2, :]
                    act.wait_ge(xn_rdy, i + 1)
                    act.wait_ge(xs_rdy, i + 1)
                    nc.scalar.activation(xi, xi, ACT.Identity, bias=rnd[:], scale=sx[:, i, 2:3]).then_inc(xr_rdy, 1)

                def x_evac(i):
                    act.wait_ge(tx_rdy, i + 1)
                    nc.scalar.copy(xqT[:, i % 2, :, :], pt[0][:, 0:HK, :]).then_inc(xqT_rdy, 1)

                def h_evac(i, a):
                    act.wait_ge(th_rdy, 2 * i + a + 1)
                    nc.scalar.copy(hqT[:, i % 2, 8 * a:8 * a + 8, :], pt[a][:]).then_inc(hqT_rdy, 1)

                act.wait_ge(rnd_set, 1)
                layernorm(0)
                layernorm(1)
                x_round(0)
                x_evac(0)
                for i in range(TT):
                    for f in range(FC):
                        g = i * FC + f
                        act.wait_ge(gu_rdy, g + 1)
                        if i >= 2:
                            act.wait_ge(hq_rdy, 2 * (i - 1))
                        nc.scalar.activation(gg[:, i % 2, f * 512:(f + 1) * 512], pg[g % 2][:], ACT.Silu,
                                             scale=sx[:, i, 3:4]).then_inc(sg_rdy, 1)
                        if f == 0 and i + 1 < TT:
                            x_round(i + 1)
                        if i and f in (1, 2):
                            h_evac(i - 1, f - 1)
                        if f == 2 and i + 2 < TT:
                            layernorm(i + 2)
                    if i + 1 < TT:
                        x_evac(i + 1)
                    act.wait_ge(s_rdy, i + 1)
                    for a in range(2):
                        half = gg[:, i % 2, a * IF // 2:(a + 1) * IF // 2]
                        nc.scalar.activation(half, half, ACT.Identity, bias=rnd[:], scale=sh[:, i, 2:3]).then_inc(rnd_rdy, 1)
                for a in range(2):
                    h_evac(TT - 1, a)

            @block.gpsimd
            def _(pool):
                for i in range(TT):
                    pool.wait_ge(xr_rdy, i + 1)
                    if i >= 2:
                        pool.wait_ge(tx_rdy, i - 1)
                    nc.gpsimd.tensor_scalar(xq[:, i % 2, :], xn[:, i % 2, :], -ROUND, 127.0, ALU.add,
                                            ALU.min).then_inc(xq_rdy, 1)

            @block.tensor
            def _(pe):
                pe.wait_ge(loaded, 16)

                def x_transpose(i):
                    pe.wait_ge(xq_rdy, i + 1)
                    if i >= 2:
                        pe.wait_ge(hqT_rdy, 2 * (i - 2) + 1)
                    for k in range(HK):
                        tr = nc.tensor.transpose(pt[0][:, k, :], xq[:, i % 2, k * P:(k + 1) * P], ident[:])
                    tr.then_inc(tx_rdy, 1)

                def h_transpose(i, a):
                    pe.wait_ge(hq_rdy, 2 * i + a + 1)
                    if a == 0:
                        pe.wait_ge(xqT_rdy, min(i + 2, TT))
                    elif i:
                        pe.wait_ge(hqT_rdy, 2 * i)
                    for k in range(8):
                        o = (8 * a + k) * P
                        tr = nc.tensor.transpose(pt[a][:, k, :], hq[:, i % 2, o:o + P], ident[:])
                    tr.then_inc(th_rdy, 1)

                def down(i):
                    if i:
                        pe.wait_ge(x_rdy, i)
                    for k in range(FK):
                        if k % 8 == 0:
                            pe.wait_ge(hqT_rdy, 2 * i + k // 8 + 1)
                        mm = nc.tensor.matmul(pd[:], hqT[:, i % 2, k, :], Wq[2][:, k // 4, (k % 4) * H:(k % 4 + 1) * H],
                                              start=(k == 0), stop=(k == FK - 1))
                    mm.then_inc(dn_rdy, 1)

                x_transpose(0)
                for i in range(TT):
                    pe.wait_ge(xqT_rdy, i + 1)
                    for f in range(FC):
                        g = i * FC + f
                        if g >= 2:
                            pe.wait_ge(gh_rdy, g - 1)
                        for ps, w in ((pg, 0), (pu, 1)):
                            for k in range(HK):
                                mm = nc.tensor.matmul(ps[g % 2][:], xqT[:, i % 2, k, :], Wq[w][:, k, f * 512:(f + 1) * 512],
                                                      start=(k == 0), stop=(k == HK - 1))
                        mm.then_inc(gu_rdy, 1)
                        if i and f in (1, 2):
                            h_transpose(i - 1, f - 1)
                    if i + 1 < TT:
                        x_transpose(i + 1)
                    if i:
                        down(i - 1)
                for a in range(2):
                    h_transpose(TT - 1, a)
                down(TT - 1)


def bass_program(nc, d, out):
    d = dict(d)
    for name in ("w_hi", "w_lo"):
        d[name] = nc.dram_tensor(name, (P, NEX * WE), F16).ap()
    y_ssm = nc.dram_tensor("y_ssm", (T, L), F32).ap()
    with ExitStack() as ctx:
        m = Mem(nc, ctx, "all")
        X = m.sb("X", [P, TT, H])
        ssm_first(nc, d, X, y_ssm)
        r = {
            "xn_d": nc.dram_tensor("xn_d", (T, H), F32).ap(),
            "y_d": nc.dram_tensor("y_d", (NSLOT, H), F32).ap(),
            "mv": m.sb("mv", [P, TT, 2]),
            "logit": m.sb("logit", [P, TT, E + 1]),
            "sig": m.sb("sig", [P, TT]),
            "w8": m.sb("w8", [P, TT, 8]),
            "pos": m.sb("pos", [P, TT, TOPK], U32),
            "idx": m.sb("idx", [P, NALL], U32),
            "tab": m.sb("tab", [1, 3, NALL], I32),
            "first": m.sb("first", [1, NEX], I32),
        }
        gate(nc, 0, d, X, y_ssm, r)
        routing(nc, d, r)
        experts_and_ssm(nc, d, r, X, y_ssm)
        Wq = [m.sb(f"Wq{i}", [P, 4, IF], BF16) for i in range(3)]
        wsc = m.sb("wsc", [P, 3])
        combine(nc, d, r, X, Wq, wsc)
        gate(nc, 1, d, X, y_ssm, r)
        quant_ffn(nc, d, r, X, Wq, wsc, out)


def layouts(inputs):
    import numpy as np
    a = {k: np.asarray(v) for k, v in inputs.items()}
    c = np.ascontiguousarray
    p = np.arange(P)
    d = {
        "x": c(a["x"].reshape(T, H)),
        "ctxT": c(a["ctx_1024"].reshape(T, DM).T),
        "ident": np.eye(P, dtype=np.float32),
        "sel": c((p[:96, None, None] % (2 * NS) == np.arange(2 * NS)[None, :, None])
                 * np.ones((1, 1, P))).astype(mybir.dt.np(BF16)),
    }
    d.update({
        "ident_bf": np.eye(P, dtype=np.float32).astype(mybir.dt.np(BF16)),
        "tri": np.triu(np.ones((P, P), np.float32), 1),
        "ones": np.ones((P, P), np.float32),
        "e_of": np.tile(np.arange(E, dtype=np.float32), (P, 1)),
        "thr": np.tile(np.arange(TT, dtype=np.float32) * P, (P, 1)),
        "col": np.tile(np.arange(P, dtype=np.float32), (P, 1)),
        "tok": c((np.arange(TT)[None, :] * P + p[:, None]).astype(np.float32)),
        "turn": np.array([[(e + 1) % WR - (e % WR if e else 0) for e in range(E)]], np.float32),
        "first": np.array([[n * TT if n < NSH else 0 for n in range(NEX)]], np.int32),
        "tab": np.array([[g // TT + 1, g // TT % WR, g % TT] if g < NA else [0] * 3
                         for g in range(NALL)], np.int32).T.copy()[None],
        "w_router": c(np.concatenate([a["L0_ffn_gate_w"], a["L0_ffn_sgate_w"]], 0).T),
        "w_all": w_all(a),
        "w_gate": c(a["L1_ffn_w_gate"].T),
        "w_up": c(a["L1_ffn_w_up"].T),
        "w_down": c(a["L1_ffn_w_down"].T),
    })
    for l in range(2):
        w = {k[len(f"L{l}_xattn_"):]: v for k, v in a.items() if k.startswith(f"L{l}_xattn_")}
        xp = w["x_proj_w"]
        d[f"w_in{l}"] = c(w["in_proj_w"].T)
        d[f"w_x{l}"] = c(np.concatenate([xp[DR:]] * 3 + [xp[:DR]], 0).T)
        d[f"w_up{l}"] = c(w["dt_proj_w"].T)
        d[f"cw{l}"] = c(w["conv_w"].reshape(DI, DC))
        d[f"cb{l}"] = c(w["conv_b"].reshape(KC, P).T)
        d[f"db{l}"] = c(w["dt_proj_b"].reshape(KC, P).T)
        d[f"D{l}"] = c(w["D"].reshape(KC, P).T)
        d[f"alog{l}"] = c(w["A_log"])
    return d


def w_all(a):
    import numpy as np
    w13 = [*a["L0_ffn_w13"], *a["L0_ffn_shared_gate_up_w"].reshape(2, NSH, IE, H).transpose(1, 0, 2, 3)]
    w2 = [*a["L0_ffn_w2"], *a["L0_ffn_shared_down_w"].reshape(H, NSH, IE).transpose(1, 0, 2)]
    w = np.zeros((P, NEX, 2 * IE * HK + 3 * H), np.float32)
    for e in range(NEX):
        up = w13[e].reshape(2 * IE, HK, P).transpose(2, 1, 0)
        w[:, e, :HK * 2 * IE] = up.reshape(P, HK * 2 * IE)
        down = np.zeros((3 * P, H), np.float32)
        down[:IE] = w2[e].T
        w[:, e, HK * 2 * IE:] = down.reshape(3, P, H).transpose(1, 0, 2).reshape(P, 3 * H)
    return w.reshape(P, NEX * WE)


def kernel(**inputs):
    import numpy as np
    import concourse.bacc as bacc
    from concourse.bass_utils import run_bass_kernel_spmd

    nc = bacc.Bacc("TRN2", target_bir_lowering=False, num_devices=1)
    arrays = {f"in_{k}": v for k, v in layouts(inputs).items()}
    aps = {k[3:]: nc.dram_tensor(k, v.shape, mybir.dt.from_np(v.dtype), kind="ExternalInput").ap()
           for k, v in arrays.items()}
    out = nc.dram_tensor("out_0_dram", (T, H), F32, kind="ExternalOutput").ap()
    bass_program(nc, aps, out)
    r = run_bass_kernel_spmd(nc, [arrays], core_ids=[0])
    return r.results[0]["out_0_dram"].reshape(B, L, H)
```
